# Optimizing a Trainium2 kernel written in Bass

```python
import numpy as np
import jax
import jax.numpy as jnp

def _softmax(x, axis=-1):
    return jax.nn.softmax(x, axis=axis)

def _gelu(x):
    return jax.nn.gelu(x, approximate=True)

def _silu(x):
    return jax.nn.silu(x)

def _sigmoid(x):
    return jax.nn.sigmoid(x)

def _layernorm(x, axis=-1, eps=1e-05):
    m = jnp.mean(x, axis=axis, keepdims=True)
    v = jnp.var(x, axis=axis, keepdims=True)
    return (x - m) / jnp.sqrt(v + eps)

def _scatter_add(tgt, idx, src, axis=0):
    return tgt.at[idx].add(src)

def _segment_sum(src, seg, n):
    return jax.ops.segment_sum(src, seg, n)
kernel_name = 'mk_adaln_d2_jaxref_r4_d76431'

def setup_inputs(seed: int=0):
    np.random.seed(seed)
    _w = jnp.asarray

    def _L0_attn_setup():
        import jax, jax.numpy as jnp
        import numpy as np
        B, T, C = (4, 256, 256)
        HEAD = 64
        H = C // HEAD
        LORA_MIX = 32
        LORA_DECAY = 64
        LN_EPS = 0.00064

        def _wkv6(r, k, v, w, u):
            rT = jnp.moveaxis(r, 1, 0)
            kT = jnp.moveaxis(k, 1, 0)
            vT = jnp.moveaxis(v, 1, 0)
            wT = jnp.moveaxis(w, 1, 0)

            def step(S, inputs):
                rt, kt, vt, wt = inputs
                kv = kt[..., :, None] * vt[..., None, :]
                y = jnp.einsum('bhi,bhij->bhj', rt, S + u[None, :, :, None] * kv)
                S = wt[..., :, None] * S + kv
                return (S, y)
            S0 = jnp.zeros((r.shape[0], H, HEAD, HEAD), r.dtype)
            _, yT = jax.lax.scan(step, S0, (rT, kT, vT, wT))
            return jnp.moveaxis(yT, 0, 1)

        def _tmix_forward(x, time_maa_x, time_maa_w, time_maa_k, time_maa_v, time_maa_r, time_maa_w1, time_maa_w2, time_decay, time_decay_w1, time_decay_w2, time_faaaa, W_r, W_k, W_v, W_o, ln_w, ln_b):
            b, t, c = x.shape
            xshift = jnp.pad(x, ((0, 0), (1, 0), (0, 0)))[:, :t]
            xx = xshift - x
            xxx = x + xx * time_maa_x
            m = jnp.tanh(xxx @ time_maa_w1).reshape(b, t, 4, LORA_MIX)
            m = jnp.einsum('btfl,flc->fbtc', m, time_maa_w2)
            mw, mk, mv, mr = (m[0], m[1], m[2], m[3])
            xw = x + xx * (time_maa_w + mw)
            xk = x + xx * (time_maa_k + mk)
            xv = x + xx * (time_maa_v + mv)
            xr = x + xx * (time_maa_r + mr)
            r = (xr @ W_r).reshape(b, t, H, HEAD)
            k = (xk @ W_k).reshape(b, t, H, HEAD)
            v = (xv @ W_v).reshape(b, t, H, HEAD)
            ww = time_decay + jnp.tanh(xw @ time_decay_w1) @ time_decay_w2
            w = jnp.exp(-jnp.exp(ww)).reshape(b, t, H, HEAD)
            y = _wkv6(r, k, v, w, time_faaaa)
            mean = y.mean(-1, keepdims=True)
            var = y.var(-1, keepdims=True)
            yn = ((y - mean) * jax.lax.rsqrt(var + LN_EPS)).reshape(b, t, c)
            yn = yn * ln_w + ln_b
            return yn @ W_o
        key0 = jax.random.key(seed)
        ks = jax.random.split(key0, 24)
        rn = lambda k, shape, s: jax.random.normal(k, shape, jnp.float32) * s
        inp = {'query': jax.random.normal(ks[0], (B, T, C), jnp.float32), 'key': jax.random.normal(ks[1], (B, T, C), jnp.float32), 'value': jax.random.normal(ks[2], (B, T, C), jnp.float32), 'time_maa_x': rn(ks[3], (C,), 0.1) + 0.5, 'time_maa_w': rn(ks[4], (C,), 0.1) + 0.5, 'time_maa_k': rn(ks[5], (C,), 0.1) + 0.5, 'time_maa_v': rn(ks[6], (C,), 0.1) + 0.5, 'time_maa_r': rn(ks[7], (C,), 0.1) + 0.5, 'time_maa_w1': rn(ks[8], (C, 4 * LORA_MIX), 0.02), 'time_maa_w2': rn(ks[9], (4, LORA_MIX, C), 0.02), 'time_decay': rn(ks[10], (C,), 0.5) - 5.0, 'time_decay_w1': rn(ks[11], (C, LORA_DECAY), 0.02), 'time_decay_w2': rn(ks[12], (LORA_DECAY, C), 0.02), 'time_faaaa': rn(ks[13], (H, HEAD), 0.5), 'W_r': rn(ks[14], (C, C), 0.02), 'W_k': rn(ks[15], (C, C), 0.02), 'W_v': rn(ks[16], (C, C), 0.02), 'W_o': rn(ks[17], (C, C), 0.02), 'ln_w': jnp.ones((C,), jnp.float32), 'ln_b': jnp.zeros((C,), jnp.float32)}
        return inp
    _L0_attn_in = _L0_attn_setup()

    def _L0_ffn_setup():
        import jax, jax.numpy as jnp
        import numpy as np
        ALPHA = 1.0
        key = jax.random.key(seed)
        ks = jax.random.split(key, 7)
        B, S, IN, OUT = (8, 2048, 256, 256)
        RANK, DDIM, UDIM = (4, 100, 50)
        return {'hidden_states': jax.random.normal(ks[0], (B, S, IN), dtype=jnp.float32), 'W': jax.random.normal(ks[1], (OUT, IN), dtype=jnp.float32) * 0.02, 'b': jax.random.normal(ks[2], (OUT,), dtype=jnp.float32) * 0.02, 'lora_down': jax.random.normal(ks[3], (RANK, DDIM), dtype=jnp.float32) * 0.1, 'lora_up': jax.random.normal(ks[4], (UDIM, RANK), dtype=jnp.float32) * 0.1, 'down_aux': jax.random.normal(ks[5], (DDIM, IN), dtype=jnp.float32) * 0.03, 'up_aux': jax.random.normal(ks[6], (OUT, UDIM), dtype=jnp.float32) * 0.03}
    _L0_ffn_in = _L0_ffn_setup()
    _L0_c = _w((lambda *s: np.random.randn(*s).astype(np.float32) * 0.05)(2, 256))
    _L0_wmod = _w((lambda *s: np.random.randn(*s).astype(np.float32) * 0.05)(256, 6 * 256) * 256 ** (-0.5))

    def _L1_attn_setup():
        import jax, jax.numpy as jnp
        import numpy as np
        B, S, D = (8, 512, 256)
        key = jax.random.key(seed)
        k1, k2, k3, k4 = jax.random.split(key, 4)
        x = jax.random.normal(k1, (B, S, D), dtype=jnp.float32)
        W0 = jax.random.normal(k2, (D, D), dtype=jnp.float32) / jnp.sqrt(jnp.float32(D))
        Wkv = jax.random.normal(k3, (2 * D, D), dtype=jnp.float32) / jnp.sqrt(jnp.float32(D))
        bkv = jax.random.normal(k4, (2 * D,), dtype=jnp.float32) * 0.01
        eta = jnp.float32(0.1)
        return {'x': x, 'W0': W0, 'Wkv': Wkv, 'bkv': bkv, 'eta': eta}
    _L1_attn_in = _L1_attn_setup()

    def _L1_ffn_setup():
        import jax, jax.numpy as jnp
        import numpy as np
        E = 8
        K = 2
        CF = 1.2
        D = 256
        F = 1024
        B, S = (4, 256)
        key = jax.random.key(seed)
        ks = jax.random.split(key, 4)

        def init(k, shape, fan_in):
            return jax.random.normal(k, shape, jnp.float32) * (1.0 / np.sqrt(fan_in))
        return {'x': jax.random.normal(ks[0], (B, S, D), jnp.float32), 'Wg': init(ks[1], (D, E), D), 'bg': jnp.zeros((E,), jnp.float32), 'W1': init(ks[2], (E, D, F), D), 'b1': jnp.zeros((E, F), jnp.float32), 'W2': init(ks[3], (E, F, D), F), 'b2': jnp.zeros((E, D), jnp.float32)}
    _L1_ffn_in = _L1_ffn_setup()
    _L1_c = _w((lambda *s: np.random.randn(*s).astype(np.float32) * 0.05)(2, 256))
    _L1_wmod = _w((lambda *s: np.random.randn(*s).astype(np.float32) * 0.05)(256, 6 * 256) * 256 ** (-0.5))
    _d = {'L0_attn_query': _L0_attn_in['query'], 'L0_attn_key': _L0_attn_in['key'], 'L0_attn_value': _L0_attn_in['value'], 'L0_attn_time_maa_x': _L0_attn_in['time_maa_x'], 'L0_attn_time_maa_w': _L0_attn_in['time_maa_w'], 'L0_attn_time_maa_k': _L0_attn_in['time_maa_k'], 'L0_attn_time_maa_v': _L0_attn_in['time_maa_v'], 'L0_attn_time_maa_r': _L0_attn_in['time_maa_r'], 'L0_attn_time_maa_w1': _L0_attn_in['time_maa_w1'], 'L0_attn_time_maa_w2': _L0_attn_in['time_maa_w2'], 'L0_attn_time_decay': _L0_attn_in['time_decay'], 'L0_attn_time_decay_w1': _L0_attn_in['time_decay_w1'], 'L0_attn_time_decay_w2': _L0_attn_in['time_decay_w2'], 'L0_attn_time_faaaa': _L0_attn_in['time_faaaa'], 'L0_attn_W_r': _L0_attn_in['W_r'], 'L0_attn_W_k': _L0_attn_in['W_k'], 'L0_attn_W_v': _L0_attn_in['W_v'], 'L0_attn_W_o': _L0_attn_in['W_o'], 'L0_attn_ln_w': _L0_attn_in['ln_w'], 'L0_attn_ln_b': _L0_attn_in['ln_b'], 'L0_ffn_W': _L0_ffn_in['W'], 'L0_ffn_b': _L0_ffn_in['b'], 'L0_ffn_lora_down': _L0_ffn_in['lora_down'], 'L0_ffn_lora_up': _L0_ffn_in['lora_up'], 'L0_ffn_down_aux': _L0_ffn_in['down_aux'], 'L0_ffn_up_aux': _L0_ffn_in['up_aux'], 'L0_c': _L0_c, 'L0_wmod': _L0_wmod, 'L1_attn_W0': _L1_attn_in['W0'], 'L1_attn_Wkv': _L1_attn_in['Wkv'], 'L1_attn_bkv': _L1_attn_in['bkv'], 'L1_attn_eta': _L1_attn_in['eta'], 'L1_ffn_Wg': _L1_ffn_in['Wg'], 'L1_ffn_bg': _L1_ffn_in['bg'], 'L1_ffn_W1': _L1_ffn_in['W1'], 'L1_ffn_b1': _L1_ffn_in['b1'], 'L1_ffn_W2': _L1_ffn_in['W2'], 'L1_ffn_b2': _L1_ffn_in['b2'], 'L1_c': _L1_c, 'L1_wmod': _L1_wmod}
    _x0 = _d['L0_attn_query']
    _d['L0_attn_query'] = jax.random.normal(jax.random.fold_in(jax.random.key(seed), 1), (2, 2048, 256), dtype=_x0.dtype)
    del _x0
    return _d

def reference(L0_attn_query, L0_attn_key, L0_attn_value, L0_attn_time_maa_x, L0_attn_time_maa_w, L0_attn_time_maa_k, L0_attn_time_maa_v, L0_attn_time_maa_r, L0_attn_time_maa_w1, L0_attn_time_maa_w2, L0_attn_time_decay, L0_attn_time_decay_w1, L0_attn_time_decay_w2, L0_attn_time_faaaa, L0_attn_W_r, L0_attn_W_k, L0_attn_W_v, L0_attn_W_o, L0_attn_ln_w, L0_attn_ln_b, L0_ffn_W, L0_ffn_b, L0_ffn_lora_down, L0_ffn_lora_up, L0_ffn_down_aux, L0_ffn_up_aux, L0_c, L0_wmod, L1_attn_W0, L1_attn_Wkv, L1_attn_bkv, L1_attn_eta, L1_ffn_Wg, L1_ffn_bg, L1_ffn_W1, L1_ffn_b1, L1_ffn_W2, L1_ffn_b2, L1_c, L1_wmod):

    def _L0_attn_ref(query, key, value, time_maa_x, time_maa_w, time_maa_k, time_maa_v, time_maa_r, time_maa_w1, time_maa_w2, time_decay, time_decay_w1, time_decay_w2, time_faaaa, W_r, W_k, W_v, W_o, ln_w, ln_b):
        import jax, jax.numpy as jnp
        import numpy as np
        B, T, C = (4, 256, 256)
        HEAD = 64
        H = C // HEAD
        LORA_MIX = 32
        LORA_DECAY = 64
        LN_EPS = 0.00064

        def _wkv6(r, k, v, w, u):
            rT = jnp.moveaxis(r, 1, 0)
            kT = jnp.moveaxis(k, 1, 0)
            vT = jnp.moveaxis(v, 1, 0)
            wT = jnp.moveaxis(w, 1, 0)

            def step(S, inputs):
                rt, kt, vt, wt = inputs
                kv = kt[..., :, None] * vt[..., None, :]
                y = jnp.einsum('bhi,bhij->bhj', rt, S + u[None, :, :, None] * kv)
                S = wt[..., :, None] * S + kv
                return (S, y)
            S0 = jnp.zeros((r.shape[0], H, HEAD, HEAD), r.dtype)
            _, yT = jax.lax.scan(step, S0, (rT, kT, vT, wT))
            return jnp.moveaxis(yT, 0, 1)

        def _tmix_forward(x, time_maa_x, time_maa_w, time_maa_k, time_maa_v, time_maa_r, time_maa_w1, time_maa_w2, time_decay, time_decay_w1, time_decay_w2, time_faaaa, W_r, W_k, W_v, W_o, ln_w, ln_b):
            b, t, c = x.shape
            xshift = jnp.pad(x, ((0, 0), (1, 0), (0, 0)))[:, :t]
            xx = xshift - x
            xxx = x + xx * time_maa_x
            m = jnp.tanh(xxx @ time_maa_w1).reshape(b, t, 4, LORA_MIX)
            m = jnp.einsum('btfl,flc->fbtc', m, time_maa_w2)
            mw, mk, mv, mr = (m[0], m[1], m[2], m[3])
            xw = x + xx * (time_maa_w + mw)
            xk = x + xx * (time_maa_k + mk)
            xv = x + xx * (time_maa_v + mv)
            xr = x + xx * (time_maa_r + mr)
            r = (xr @ W_r).reshape(b, t, H, HEAD)
            k = (xk @ W_k).reshape(b, t, H, HEAD)
            v = (xv @ W_v).reshape(b, t, H, HEAD)
            ww = time_decay + jnp.tanh(xw @ time_decay_w1) @ time_decay_w2
            w = jnp.exp(-jnp.exp(ww)).reshape(b, t, H, HEAD)
            y = _wkv6(r, k, v, w, time_faaaa)
            mean = y.mean(-1, keepdims=True)
            var = y.var(-1, keepdims=True)
            yn = ((y - mean) * jax.lax.rsqrt(var + LN_EPS)).reshape(b, t, c)
            yn = yn * ln_w + ln_b
            return yn @ W_o
        return _tmix_forward(query, time_maa_x, time_maa_w, time_maa_k, time_maa_v, time_maa_r, time_maa_w1, time_maa_w2, time_decay, time_decay_w1, time_decay_w2, time_faaaa, W_r, W_k, W_v, W_o, ln_w, ln_b)

    def _L0_ffn_ref(hidden_states, W, b, lora_down, lora_up, down_aux, up_aux):
        import jax, jax.numpy as jnp
        import numpy as np
        ALPHA = 1.0
        lilora_weight = up_aux @ (lora_up @ (lora_down @ down_aux))
        base = jnp.einsum('bsi,oi->bso', hidden_states, W) + b
        delta = jnp.einsum('bsi,oi->bso', hidden_states, lilora_weight)
        return base + ALPHA * delta

    def _L1_attn_ref(x, W0, Wkv, bkv, eta):
        import jax, jax.numpy as jnp
        import numpy as np
        B, S, D = (8, 512, 256)
        b, s, d = x.shape
        v = jnp.einsum('bsd,ed->bse', x, Wkv[d:, :]) + bkv[d:]
        scale = 2.0 / (b * d)

        def step(W, inp):
            xt, vt = inp
            y = xt @ W.T
            err = y - vt
            gW = scale * (err.T @ xt)
            return (W - eta * gW, y)
        xs = jnp.swapaxes(x, 0, 1)
        vs = jnp.swapaxes(v, 0, 1)
        _, ys = jax.lax.scan(step, W0, (xs, vs))
        return jnp.swapaxes(ys, 0, 1)

    def _L1_ffn_ref(x, Wg, bg, W1, b1, W2, b2):
        import jax, jax.numpy as jnp
        import numpy as np
        E = 8
        K = 2
        CF = 1.2
        D = 256
        F = 1024
        B, S = (4, 256)
        Bx, Sx, Dx = x.shape
        T = Bx * Sx
        xt = x.reshape(T, Dx)
        logits = xt @ Wg + bg
        probs = jax.nn.softmax(logits, axis=-1)
        gate_vals, exp_idx = jax.lax.top_k(probs, K)
        gate_vals = gate_vals / jnp.sum(gate_vals, axis=-1, keepdims=True)
        capacity = int(np.ceil(CF * T * K / E))
        eidx = exp_idx.T.reshape(-1)
        gv = gate_vals.T.reshape(-1)
        oh = jax.nn.one_hot(eidx, E, dtype=jnp.int32)
        pos = jnp.sum((jnp.cumsum(oh, axis=0) - oh) * oh, axis=-1)
        keep = pos < capacity
        pos_c = jnp.where(keep, pos, capacity)
        xk = jnp.tile(xt, (K, 1))
        buf = jnp.zeros((E, capacity + 1, Dx), x.dtype)
        buf = buf.at[eidx, pos_c].add(jnp.where(keep[:, None], xk, 0.0))
        buf = buf[:, :capacity]
        h = jax.nn.gelu(jnp.einsum('ecd,edf->ecf', buf, W1) + b1[:, None, :], approximate=True)
        ye = jnp.einsum('ecf,efd->ecd', h, W2) + b2[:, None, :]
        ye = jnp.concatenate([ye, jnp.zeros((E, 1, Dx), ye.dtype)], axis=1)
        gathered = ye[eidx, pos_c] * (gv * keep.astype(gv.dtype))[:, None]
        out = jnp.sum(gathered.reshape(K, T, Dx), axis=0)
        return out.reshape(Bx, Sx, Dx)
    x = L0_attn_query
    mod = (_silu(L0_c) @ L0_wmod).reshape(L0_c.shape[0], 6, 1, -1)
    sa, ca, ga, sb, cb, gb = (mod[:, 0], mod[:, 1], mod[:, 2], mod[:, 3], mod[:, 4], mod[:, 5])
    ga = (2 * (ga >= 0) - 1) * jnp.maximum(jnp.abs(ga), 0.25)
    gb = (2 * (gb >= 0) - 1) * jnp.maximum(jnp.abs(gb), 0.25)
    h = _layernorm(x, axis=-1) * (1 + ca) + sa
    x = x + ga * _L0_attn_ref(h, L0_attn_key, L0_attn_value, L0_attn_time_maa_x, L0_attn_time_maa_w, L0_attn_time_maa_k, L0_attn_time_maa_v, L0_attn_time_maa_r, L0_attn_time_maa_w1, L0_attn_time_maa_w2, L0_attn_time_decay, L0_attn_time_decay_w1, L0_attn_time_decay_w2, L0_attn_time_faaaa, L0_attn_W_r, L0_attn_W_k, L0_attn_W_v, L0_attn_W_o, L0_attn_ln_w, L0_attn_ln_b)
    h = _layernorm(x, axis=-1) * (1 + cb) + sb
    x = x + gb * _L0_ffn_ref(h, L0_ffn_W, L0_ffn_b, L0_ffn_lora_down, L0_ffn_lora_up, L0_ffn_down_aux, L0_ffn_up_aux)
    mod = (_silu(L1_c) @ L1_wmod).reshape(L1_c.shape[0], 6, 1, -1)
    sa, ca, ga, sb, cb, gb = (mod[:, 0], mod[:, 1], mod[:, 2], mod[:, 3], mod[:, 4], mod[:, 5])
    ga = (2 * (ga >= 0) - 1) * jnp.maximum(jnp.abs(ga), 0.25)
    gb = (2 * (gb >= 0) - 1) * jnp.maximum(jnp.abs(gb), 0.25)
    h = _layernorm(x, axis=-1) * (1 + ca) + sa
    x = x + ga * _L1_attn_ref(h, L1_attn_W0, L1_attn_Wkv, L1_attn_bkv, L1_attn_eta)
    h = _layernorm(x, axis=-1) * (1 + cb) + sb
    x = x + gb * _L1_ffn_ref(h, L1_ffn_Wg, L1_ffn_bg, L1_ffn_W1, L1_ffn_b1, L1_ffn_W2, L1_ffn_b2)
    return x

_drawn_inputs = setup_inputs


def setup_inputs(seed=0):
    import zlib

    import numpy as np

    out = dict(_drawn_inputs(seed))
    spreads = {'L0_attn_ln_w': (1.0, 0.6),
     'L0_attn_ln_b': (0.0, 0.623),
     'L1_ffn_bg': (0.0, 0.8),
     'L1_ffn_b1': (0.0, 2.0),
     'L1_ffn_b2': (0.0, 2.0)}
    factors = {'L0_attn_time_maa_x': 8.0,
     'L0_attn_time_maa_w': 64.0,
     'L0_attn_time_maa_k': 5.256,
     'L0_attn_time_maa_v': 5.09,
     'L0_attn_time_maa_r': 2.771,
     'L0_attn_time_maa_w1': 7.483,
     'L0_attn_time_maa_w2': 7.332,
     'L0_attn_time_decay_w1': 37.374,
     'L0_attn_time_decay_w2': 29.092,
     'L0_attn_time_faaaa': 8.0,
     'L0_ffn_b': 59.392,
     'L0_ffn_lora_down': 7.165,
     'L0_ffn_lora_up': 7.522,
     'L0_ffn_down_aux': 7.605,
     'L0_ffn_up_aux': 7.462,
     'L1_attn_bkv': 64.0,
     'L0_ffn_W': 8.0,
     'L1_attn_W0': 8.0,
     'L1_attn_Wkv': 3.298,
     'L1_ffn_Wg': 5.87,
     'L1_ffn_W1': 7.182,
     'L1_ffn_W2': 5.57,
     'L1_c': 2.728,
     'L1_wmod': 2.892}
    for name, (base, spread) in spreads.items():
        noise = np.random.default_rng([zlib.crc32(name.encode()), seed]).standard_normal(out[name].shape)
        drawn = base * np.exp(spread * noise) if base else spread * noise
        out[name] = jnp.asarray(drawn.astype(out[name].dtype))
    for name, factor in factors.items():
        out[name] = (out[name] * factor).astype(out[name].dtype)
    return out
```

```python
import numpy as np
from contextlib import ExitStack

import concourse.bass as bass
from concourse import mybir

FP32 = mybir.dt.float32
I32 = mybir.dt.int32
ALU = mybir.AluOpType
ACT = mybir.ActivationFunctionType
AX = mybir.AxisListType

BATCH, TIME, CH = 2, 2048, 256
P = 128
KH = CH // P
STEPS = P // BATCH
TILES = TIME // STEPS
HEAD = 64
HEADS = CH // HEAD
MIX, MIXES = 32, 4
DECAY_RANK = 64
LEVELS = [1, 2, 4, 8, 16, 32]
RANK, DDIM, UDIM = 4, 100, 50
EXPERTS, TOPK, HIDDEN = 8, 2, 1024
TOKENS = BATCH * TIME
CAPACITY = int(np.ceil(1.2 * TOKENS * TOPK / EXPERTS))
ROWS = 123
GROUP = 2 * ROWS
GROUPS = -(-CAPACITY // GROUP)
SLOTS = GROUPS * GROUP
NSLOT = EXPERTS * SLOTS
DROPPED = NSLOT
FT = HIDDEN // P
LN_EPS, HEAD_EPS = 1e-5, 0.00064


class Steps:

    def __init__(self, sem, names):
        self.sem, self.names, self.at = sem, names.split(), 0

    def __getitem__(self, name):
        assert self.names[self.at] == name, (self.names[self.at], name)
        self.at = (self.at + 1) % len(self.names)
        return self.sem

    def __call__(self, name, t):
        return self.sem, t * len(self.names) + (self.names.index(name) + 1)


def run_pipeline(eng, chains, tiles, slots=2):
    lag = max(l for _, l in chains)
    head = lag + slots
    turns = (tiles - head) // slots

    def once(parts):
        gens = [f(*at) for f, *at in parts]
        while gens:
            gens = [g for g in gens if next(g, "end") != "end"]

    def peeled(i):
        once([(f, i - l, (i - l) % slots, (i - l) // slots) for f, l in chains if 0 <= i - l < tiles])

    for i in range(head):
        peeled(i)
    with eng.Fori(0, turns, 1) as turn:
        for s in range(slots):
            once([(f, turn * slots + (head + s - l), (head + s - l) % slots, turn + (head + s - l) // slots)
                  for f, l in chains])
    for i in range(head + turns * slots, tiles + lag):
        peeled(i)


def begun(t, distance):
    return not isinstance(t, int) or t >= distance


class Memory:
    pass


def alloc(nc, ctx):
    m = Memory()

    def sb(name, shape, dt=FP32):
        return ctx.enter_context(nc.sbuf_tensor(name, shape, dt))

    m.sb = sb
    m.ident = sb("ident", [P, P])
    m.x = sb("x_stream", [P, TILES, CH])
    m.y = sb("y_stream", [P, TILES, CH])
    m.mod = [sb(f"mod{l}", [P, 6, CH]) for l in range(2)]
    m.half = sb("minus_half", [P, 4])
    m.bank = [ctx.enter_context(nc.psum_tensor(f"bank{i}", [P, 512], FP32)) for i in range(8)]
    m.side = sb("side", [P, 2])
    m.maa = sb("maa", [P, 5, KH])
    m.w1 = sb("w1", [P, KH, P])
    m.w2 = sb("w2", [P, MIXES, CH])
    m.dw1 = sb("dw1", [P, KH, DECAY_RANK])
    m.dw2 = sb("dw2", [DECAY_RANK, CH])
    m.decay = sb("decay", [P, KH])
    m.bonus = sb("bonus", [P, KH])
    m.wr = sb("wr", [P, KH, CH])
    m.wk = sb("wk", [P, KH, CH])
    m.wv = sb("wv", [P, KH, CH])
    m.lmask = sb("lmask", [P, len(LEVELS), 2, STEPS], I32)
    m.dmask = sb("dmask", [P, 2, STEPS])
    m.wo = sb("wo", [P, KH, CH])
    m.wob = sb("wob", [P, CH])
    m.wf = sb("wf", [P, KH, CH])
    m.bf = sb("bf", [P, CH])
    m.wvt = sb("wvt", [P, KH, CH])
    m.bv = sb("bv", [P, CH])
    m.w0t = sb("w0t", [P, KH, CH])
    m.nbeta = sb("nbeta", [P, 1])
    m.later = sb("later", [P, P])
    m.earlier = sb("earlier", [P, P])
    m.wg = sb("wg", [P, KH, EXPERTS])
    m.bg = sb("bg", [P, EXPERTS])
    m.logits = sb("logits", [P, TILES, EXPERTS])
    return m


def prologue(nc, m, a):
    ctx = ExitStack()
    with ctx:
        def sb(name, shape, dt=FP32):
            return ctx.enter_context(nc.sbuf_tensor(name, shape, dt))

        def sem(name):
            return ctx.enter_context(nc.semaphore(name))

        wmod = [sb(f"wmod{l}", [P, KH, 6 * CH]) for l in range(2)]
        cT = sb("cT", [P, 2, KH, BATCH])
        ec = sb("ec", [P, 2, KH, BATCH])
        dc = sb("dc", [P, 2, KH, BATCH])
        rc = sb("rc", [P, 2, KH, BATCH])
        sc = sb("sc", [P, 2, KH, BATCH])
        cb = sb("cb", [P, 2, KH, P])
        big = sb("big", [P, 2, CH])
        sign = sb("sign", [P, 2, CH])
        wfr = sb("wfr", [P, KH, CH])
        wvr = sb("wvr", [P, KH, CH])
        w0r = sb("w0r", [P, KH, CH])
        down = sb("down", [DDIM, RANK])
        aux = sb("aux", [DDIM, CH])
        upT = sb("upT", [RANK, UDIM])
        uaT = sb("uaT", [UDIM, CH])
        d1 = sb("d1", [RANK, CH])
        r1 = sb("r1", [UDIM, CH])
        lnw = sb("lnw", [P, KH])
        lnb = sb("lnb", [P, KH])
        lnbb = sb("lnbb", [P, KH, P])
        wor = sb("wor", [P, KH, CH])
        eta = sb("eta", [P, 1])
        row = sb("row", [P, 1], I32)
        rows = sb("rows", [P, 1], I32)
        col = sb("col", [P, STEPS], I32)
        xor = sb("xor", [P, STEPS], I32)
        xorf = sb("xorf", [P, STEPS])
        colf = sb("colf", [P, STEPS])
        rowf = sb("rowf", [P, 1])
        prowf = sb("prowf", [P, 1])
        causal = sb("causal", [P, STEPS])
        lm = sb("lm", [P, len(LEVELS), STEPS])
        ones = sb("ones", [P, P])

        loaded = sem("loaded")
        loaded_mod = sem("loaded_mod")
        made = sem("made")
        v = sem("pro_dve")
        s_act = sem("pro_act")
        s_pe = sem("pro_pe")
        block = ctx.enter_context(nc.Block())
        count = {"w": 0}

        def halves(ap):
            return ap.rearrange("(k p) n -> p k n", p=P)

        def per_channel(ap):
            return ap.rearrange("(k p) -> p k", p=P)

        @block.sync
        def _(sp):
            def load(dst, src, s=loaded):
                sp.dma_start(dst, src).then_inc(s, 16)
                if s is loaded:
                    count["w"] += 16

            with nc.allow_non_contiguous_dma(reason="a few vectors and small weights, once"):
                for l, name in enumerate(("L0_c", "L1_c")):
                    for b in range(BATCH):
                        load(cT[:, l, :, b], per_channel(a[name][b, :]), loaded_mod)
                for l, name in enumerate(("L0_wmod", "L1_wmod")):
                    load(wmod[l][:, :, :], halves(a[name]), loaded_mod)
                for i, x in enumerate("xwkvr"):
                    load(m.maa[:, i, :], per_channel(a["L0_attn_time_maa_" + x]))
                load(m.decay[:, :], per_channel(a["L0_attn_time_decay"]))
                load(m.bonus[:, :], per_channel(a["L0_attn_time_faaaa"].rearrange("h i -> (h i)")))
                load(lnw[:, :], per_channel(a["L0_attn_ln_w"]))
                load(lnb[:, :], per_channel(a["L0_attn_ln_b"]))
                load(down[:, :], a["L0_ffn_lora_down"].rearrange("r d -> d r"))
                load(upT[:, :], a["L0_ffn_lora_up"].rearrange("u r -> r u"))
                load(uaT[:, :], a["L0_ffn_up_aux"].rearrange("o u -> u o"))
                load(aux[:, :], a["L0_ffn_down_aux"])
                load(m.w1[:, :, :], halves(a["L0_attn_time_maa_w1"]))
                load(m.dw1[:, :, :], halves(a["L0_attn_time_decay_w1"]))
                load(m.dw2[:, :], a["L0_attn_time_decay_w2"])
                for dst, name in ((m.wr, "W_r"), (m.wk, "W_k"), (m.wv, "W_v"), (wor, "W_o")):
                    load(dst[:, :, :], halves(a["L0_attn_" + name]))
                load(wfr[:, :, :], halves(a["L0_ffn_W"]))
                load(w0r[:, :, :], halves(a["L1_attn_W0"]))
                load(wvr[:, :, :], halves(a["L1_attn_Wkv"][CH:2 * CH, :]))
                load(m.wg[:, :, :], halves(a["L1_ffn_Wg"]))
                load(m.bf[:, :], a["L0_ffn_b"].partition_broadcast(P))
                load(m.bv[:, :], a["L1_attn_bkv"][CH:2 * CH].partition_broadcast(P))
                load(m.bg[:, :], a["L1_ffn_bg"].partition_broadcast(P))
                load(eta[:, :], a["L1_attn_eta"].partition_broadcast(P))
                sp.wait_ge(made, 1)
                for f in range(MIXES):
                    load(m.w2[f * MIX:(f + 1) * MIX, f, :], a["L0_attn_time_maa_w2"][f, :, :])

        all_loaded = count["w"]

        @block.gpsimd
        def _(pool):
            pool.memset(m.w2[:, :, :], 0.0).then_inc(made, 1)
            pool.memset(m.ident[:, :], 0.0)
            pool.memset(ones[:, :], 1.0)
            pool.memset(m.half[:, :], -0.5)
            pool.iota(row[:, :], pattern=[[0, 1]], base=0, channel_multiplier=1)
            pool.iota(col[:, :], pattern=[[1, STEPS]], base=0, channel_multiplier=0).then_inc(made, 1)
            pool.wait_ge(made, 2)
            pool.affine_select(out=m.ident[:, :], in_=m.ident[:, :], compare_op=ALU.not_equal, fill=1.0, base=0,
                               pattern=[[-1, P]], channel_multiplier=1).then_inc(made, 1)

        @block.scalar
        def _(act):
            act.wait_ge(loaded_mod, 16 * (2 * BATCH + 2))
            act.activation(ec[:, :, :, :], cT[:, :, :, :], ACT.Exp, scale=-1.0).then_inc(s_act, 1)

        def step_list(eng, s):
            state = [0]

            def then(ins):
                ins.then_inc(s, 1)
                state[0] += 1
                eng.wait_ge(s, state[0])
                return state[0]
            return then

        marks = {}

        @block.vector
        def _(dve):
            then = step_list(dve, v)
            dve.wait_ge(s_act, 1)
            then(dve.tensor_scalar_add(dc[:, :, :, :], ec[:, :, :, :], 1.0))
            then(dve.reciprocal(rc[:, :, :, :], dc[:, :, :, :]))
            then(dve.tensor_tensor(sc[:, :, :, :], cT[:, :, :, :], rc[:, :, :, :], ALU.mult))
            dve.wait_ge(made, 3)
            for l in range(2):
                for k in range(KH):
                    for b in range(BATCH):
                        n = then(dve.tensor_scalar(cb[:, l, k, b * STEPS:(b + 1) * STEPS], ones[:, 0:STEPS],
                                                   sc[:, l, k, b:b + 1], None, ALU.mult))
            marks["cb"] = n
            then(dve.tensor_single_scalar(rows[:, :], row[:, :], STEPS - 1, ALU.bitwise_and))
            then(dve.tensor_tensor(xor[:, :], col[:, :], rows[:, 0:1].to_broadcast([P, STEPS]), ALU.bitwise_xor))
            then(dve.tensor_copy(xorf[:, :], xor[:, :]))
            then(dve.tensor_copy(colf[:, :], col[:, :]))
            then(dve.tensor_copy(rowf[:, :], rows[:, :]))
            then(dve.tensor_copy(prowf[:, :], row[:, :]))
            then(dve.tensor_scalar(m.side[:, 0:1], prowf[:, :], float(STEPS), None, ALU.is_lt))
            then(dve.tensor_scalar(m.side[:, 1:2], prowf[:, :], float(STEPS), None, ALU.is_ge))
            then(dve.tensor_scalar(causal[:, :], colf[:, :], rowf[:, 0:1], None, ALU.is_gt))
            for n_, half in enumerate(LEVELS):
                then(dve.tensor_scalar(lm[:, n_, :], xorf[:, :], float(half), None, ALU.is_ge))
                then(dve.scalar_tensor_tensor(lm[:, n_, :], xorf[:, :], float(2 * half), lm[:, n_, :],
                                              ALU.is_lt, ALU.mult))
                then(dve.tensor_tensor(lm[:, n_, :], lm[:, n_, :], causal[:, :], ALU.mult))
                for q in range(2):
                    then(dve.tensor_copy(m.lmask[:, n_, q, :], lm[:, n_, :]))
            for q in range(2):
                then(dve.tensor_scalar(m.dmask[:, q, :], xorf[:, :], 0.0, None, ALU.is_equal))
            for b in range(BATCH):
                then(dve.tensor_scalar(m.later[:, b * STEPS:(b + 1) * STEPS], colf[:, :], rowf[:, 0:1], None,
                                       ALU.is_gt))
                then(dve.tensor_scalar(m.earlier[:, b * STEPS:(b + 1) * STEPS], colf[:, :], rowf[:, 0:1], None,
                                       ALU.is_lt))
            dve.wait_ge(loaded, all_loaded)
            then(dve.tensor_scalar(m.nbeta[:, :], eta[:, :], -2.0 / (BATCH * CH), None, ALU.mult))
            for k in range(KH):
                then(dve.tensor_scalar(m.wo[:, k, :], wor[:, k, :], lnw[:, k:k + 1], None, ALU.mult))
                n = then(dve.tensor_scalar(lnbb[:, k, :], ones[:, :], lnb[:, k:k + 1], None, ALU.mult))
            marks["lnbb"] = n
            for l in range(2):
                dve.wait_ge(s_pe, 3 * l + 3)
                for i in range(3):
                    n = then(dve.tensor_copy(m.mod[l][:, 2 * i:2 * i + 2, :].rearrange("p a c -> p (a c)"),
                                             m.bank[i][:, :]))
                marks[f"mod{l}"] = n
                for i in (1, 4):
                    then(dve.tensor_scalar_add(m.mod[l][:, i, :], m.mod[l][:, i, :], 1.0))
                g = m.mod[l][:, 2:6:3, :]
                then(dve.tensor_scalar(big[:, :, :], g, -1.0, None, ALU.mult))
                then(dve.tensor_tensor(big[:, :, :], big[:, :, :], g, ALU.max))
                then(dve.tensor_scalar(big[:, :, :], big[:, :, :], 0.25, None, ALU.max))
                then(dve.tensor_scalar(sign[:, :, :], g, 0.0, 2.0, ALU.is_ge, ALU.mult))
                then(dve.scalar_tensor_tensor(g, sign[:, :, :], -1.0, big[:, :, :], ALU.add, ALU.mult))
            then(dve.tensor_tensor(m.bf[:, :], m.bf[:, :], m.mod[0][:, 5, :], ALU.mult))
            dve.wait_ge(s_pe, 7)
            marks["d1"] = then(dve.tensor_copy(d1[:, :], m.bank[3][0:RANK, 0:CH]))
            dve.wait_ge(s_pe, 8)
            marks["r1"] = then(dve.tensor_copy(r1[:, :], m.bank[4][0:UDIM, 0:CH]))
            dve.wait_ge(s_pe, 9)
            then(dve.tensor_tensor(m.wob[:, :], m.bank[5][:, 0:CH], m.mod[0][:, 2, :], ALU.mult))
            for i, dst in enumerate((m.wf, m.wvt, m.w0t)):
                dve.wait_ge(s_pe, 10 + i)
                then(dve.tensor_copy(dst[:, :, :].rearrange("p k c -> p (k c)"), m.bank[(6, 7, 3)[i]][:, :]))

        @block.tensor
        def _(pe):
            pe.wait_ge(made, 3)
            pe.wait_ge(loaded_mod, 16 * (2 * BATCH + 2))
            pe.wait_ge(v, marks["cb"])
            for l in range(2):
                if l:
                    pe.wait_ge(v, marks["mod0"])
                for i in range(3):
                    for k in range(KH):
                        mm = pe.matmul(m.bank[i][:, :], cb[:, l, k, :], wmod[l][:, k, 512 * i:512 * i + 512],
                                       start=(k == 0), stop=(k == KH - 1))
                    mm.then_inc(s_pe, 1)
            pe.wait_ge(loaded, all_loaded)
            pe.matmul(m.bank[3][0:RANK, 0:CH], down[:, :], aux[:, :], start=True, stop=True).then_inc(s_pe, 1)
            pe.wait_ge(v, marks["d1"])
            pe.matmul(m.bank[4][0:UDIM, 0:CH], upT[:, :], d1[:, :], start=True, stop=True).then_inc(s_pe, 1)
            pe.wait_ge(v, marks["lnbb"])
            for k in range(KH):
                mm = pe.matmul(m.bank[5][:, 0:CH], lnbb[:, k, :], wor[:, k, :], start=(k == 0), stop=(k == KH - 1))
            mm.then_inc(s_pe, 1)
            pe.wait_ge(v, marks["r1"])
            for i, src in enumerate((wfr, wvr, w0r)):
                bank = m.bank[(6, 7, 3)[i]]
                for k in range(KH):
                    for o in range(KH):
                        out = bank[:, k * CH + o * P:k * CH + (o + 1) * P]
                        mm = pe.matmul(out, src[:, o, k * P:(k + 1) * P], m.ident[:, :], start=True, stop=(i > 0))
                        if i == 0:
                            mm = pe.matmul(out, r1[:, k * P:(k + 1) * P], uaT[:, o * P:(o + 1) * P],
                                           start=False, stop=True)
                mm.then_inc(s_pe, 1)


def time_mix(nc, m, a):
    ctx = ExitStack()
    with ctx:
        def sb(name, shape, dt=FP32):
            return ctx.enter_context(nc.sbuf_tensor(name, shape, dt))

        def sem(name):
            return ctx.enter_context(nc.semaphore(name))

        stats = sb("a_stats", [P, 6])
        mv = sb("a_mv", [P, 2])
        ve = sb("a_ve", [P, 1])
        rstd = sb("a_rstd", [P, 1])
        xn = sb("a_xn", [P, CH])
        xm = sb("a_xm", [P, CH])
        h = sb("a_h", [P, CH])
        hT = [sb(f"a_hT{s}", [P, KH, BATCH, STEPS + 1]) for s in range(2)]
        xx = sb("a_xx", [P, KH, BATCH, STEPS])
        xxx = sb("a_xxx", [P, KH, P])
        mt = sb("a_mt", [P, P])
        xf = sb("a_xf", [P, MIXES, KH, P])
        dt_ = sb("a_dt", [DECAY_RANK, P])
        ew = sb("a_ew", [P, KH, P])
        rp = [sb(f"a_rp{s}", [P, KH, P]) for s in range(2)]
        kq = [sb(f"a_kq{s}", [P, KH, P]) for s in range(2)]
        ru = [sb(f"a_ru{s}", [P, KH, P]) for s in range(2)]
        tot = [sb(f"a_tot{s}", [P, KH * P]) for s in range(2)]
        vt = [sb(f"a_vt{s}", [P, CH]) for s in range(2)]
        tots = {half: sb(f"a_tots{half}", [P, KH * P // (2 * half)]) for half in LEVELS}
        att = sb("a_att", [P, KH, 2, STEPS])
        blk = sb("a_blk", [P, HEADS, P])
        kt = sb("a_kt", [P, BATCH, CH])
        state = sb("a_state", [P, BATCH * KH, HEAD])
        sdec = sb("a_sdec", [P, BATCH * KH, HEAD])
        sblk = sb("a_sblk", [P, BATCH * KH, P])

        x_loaded = [sem(f"a_x_loaded{s}") for s in range(2)]
        ready = sem("a_ready")
        passed = {e: sem(f"a_passed_{e}") for e in ("dve", "pool", "pe")}
        FD = Steps(sem("front_dve"), "stats mv ve xn xx xxx xf0 xf1 xf2 xf3")
        FP = Steps(sem("front_pool"), "rstd xm h add0 add1 add2 add3")
        FA = Steps(sem("front_act"), "carry hT mt dt ew0 ew1 w r k ru0 ru1 v")
        FE = Steps(sem("front_pe"), "hT m x0 x1 x2 x3 d w r k v")
        BD = Steps(sem("back_dve"), "diag0 diag1 " + " ".join(
            f"cp{i}a cp{i}b rp{i} tot{i}" for i in range(6)) + " sdec state")
        BP = Steps(sem("back_pool"), "sblk0 sblk1 " + " ".join(f"kq{i}" for i in range(6)) + " blk0 blk1")
        BA = Steps(sem("back_act"), "kt0 kt1 y")
        BE = Steps(sem("back_pe"), "diag " + " ".join(f"l{i}" for i in range(6)) + " kT y kv")
        block = ctx.enter_context(nc.Block())

        hbank, xbank, rkbank = m.bank[0], m.bank[1], m.bank[2]
        lbank = [(m.bank[3], m.bank[4]), (m.bank[5], m.bank[6])]
        ybank = m.bank[7]
        MAA = dict(x=0, w=1, k=2, v=3, r=4)

        @block.sync
        def _(sp):
            def load(t, slot):
                for b in range(BATCH):
                    sp.dma_start(m.x[b * STEPS:(b + 1) * STEPS, bass.ds(t, 1), :].rearrange("p a c -> p (a c)"),
                                 a["L0_attn_query"][b, bass.ds(t * STEPS, STEPS), :]).then_inc(x_loaded[slot], 16)

            for slot in range(2):
                load(slot, slot)
            with sp.Fori(1, TILES // 2, 1) as turn:
                for slot in range(2):
                    sp.wait_ge(x_loaded[slot], turn * 32)
                    load(turn * 2 + slot, slot)

        @block.gpsimd
        def _(pool):
            pool.memset(hT[1][:, :, :, :], 0.0)
            pool.memset(kt[:, :, :], 0.0)
            pool.memset(state[:, :, :], 0.0).then_inc(ready, 1)
            pool.wait_ge(ready, 1)

            def front(t, slot, turn):
                pool.wait_ge(*FD("ve", t))
                pool.tensor_tensor(rstd[:, :], ve[:, :], m.half[:, 0:1], ALU.pow).then_inc(FP["rstd"], 1)
                yield
                pool.wait_ge(*FD("xn", t))
                pool.tensor_tensor(xm[:, :], xn[:, :], m.mod[0][:, 1, :], ALU.mult).then_inc(FP["xm"], 1)
                pool.wait_ge(*FP("xm", t))
                pool.tensor_tensor(h[:, :], xm[:, :], m.mod[0][:, 0, :], ALU.add).then_inc(FP["h"], 1)
                yield
                yield
                yield
                for f in range(MIXES):
                    pool.wait_ge(*FD(f"xf{f}", t))
                    pool.tensor_tensor(xf[:, f, :, :].rearrange("p k (b s) -> p k b s", b=BATCH),
                                       xf[:, f, :, :].rearrange("p k (b s) -> p k b s", b=BATCH),
                                       hT[slot][:, :, :, 1:STEPS + 1], ALU.add).then_inc(FP[f"add{f}"], 1)
                    yield

            def back(t, slot, turn):
                if begun(t, 1):
                    pool.wait_ge(*BD("state", t - 1))
                    pool.wait_ge(*BE("y", t - 1))
                    pool.sem_inc(passed["pool"], 1)
                for q in range(2):
                    pool.tensor_scalar(sblk[:, :, q * HEAD:(q + 1) * HEAD], state[:, :, :], m.side[:, q:q + 1], None,
                                       ALU.mult).then_inc(BP[f"sblk{q}"], 1)
                yield
                for i, half in enumerate(LEVELS):
                    pool.wait_ge(*BE(f"l{i}", t))
                    if i:
                        pool.wait_ge(*BD(f"tot{i - 1}", t))
                    view = kq[slot][:, :, :].rearrange("p k (n two s) -> p (k n) two s", two=2, s=half)[:, :, 0, :]
                    n = KH * P // (2 * half)
                    dec = (tot[slot] if i == 0 else tots[LEVELS[i - 1]])[:, :].rearrange("p (n two) -> p n two",
                                                                                         two=2)[:, :, 1:2]
                    pool.tensor_tensor(view, view, dec.to_broadcast([P, n, half]), ALU.mult).then_inc(BP[f"kq{i}"], 1)
                    yield
                pool.wait_ge(*BD("cp5b", t))
                pool.sem_inc(passed["pool"], 1)
                for b in range(BATCH):
                    pool.tensor_scalar(blk[:, :, b * STEPS:(b + 1) * STEPS],
                                       att[:, :, :, :].rearrange("p k q s -> p (k q) s"), m.side[:, b:b + 1], None,
                                       ALU.mult).then_inc(BP[f"blk{b}"], 1)
                yield

            run_pipeline(pool, [(front, 0), (back, 1)], TILES)

        @block.vector
        def _(dve):
            def front(t, slot, turn):
                x = m.x[:, bass.ds(t, 1), :].rearrange("p a c -> p (a c)")
                dve.wait_ge(x_loaded[slot], turn * 32 + 32)
                dve.bn_stats(stats[:, :], x).then_inc(FD["stats"], 1)
                dve.wait_ge(*FD("stats", t))
                dve.sem_inc(passed["dve"], 1)
                dve.bn_aggr(mv[:, :], stats[:, :]).then_inc(FD["mv"], 1)
                dve.wait_ge(*FD("mv", t))
                dve.tensor_scalar_add(ve[:, :], mv[:, 1:2], LN_EPS).then_inc(FD["ve"], 1)
                yield
                dve.wait_ge(*FP("rstd", t))
                dve.tensor_scalar(xn[:, :], x, mv[:, 0:1], rstd[:, 0:1], ALU.subtract, ALU.mult)\
                   .then_inc(FD["xn"], 1)
                yield
                dve.wait_ge(*FA("hT", t))
                dve.tensor_tensor(xx[:, :, :, :], hT[slot][:, :, :, 0:STEPS], hT[slot][:, :, :, 1:STEPS + 1],
                                  ALU.subtract).then_inc(FD["xx"], 1)
                dve.wait_ge(*FD("xx", t))
                for k in range(KH):
                    last = dve.scalar_tensor_tensor(
                        xxx[:, k, :].rearrange("p (b s) -> p b s", b=BATCH), xx[:, k, :, :], m.maa[:, 0, k:k + 1],
                        hT[slot][:, k, :, 1:STEPS + 1], ALU.mult, ALU.add)
                last.then_inc(FD["xxx"], 1)
                yield
                yield
                for f in range(MIXES):
                    if f % 2 == 0:
                        dve.wait_ge(*FE(f"x{f + 1}", t))
                    for k in range(KH):
                        last = dve.scalar_tensor_tensor(
                            xf[:, f, k, :], xbank[:, (f % 2) * CH + k * P:(f % 2) * CH + (k + 1) * P],
                            m.maa[:, 1 + f, k:k + 1], xx[:, k, :, :].rearrange("p b s -> p (b s)"),
                            ALU.add, ALU.mult)
                    last.then_inc(FD[f"xf{f}"], 1)
                    yield

            def back(t, slot, turn):
                dve.wait_ge(*BE("diag", t))
                for q in range(2):
                    dve.tensor_tensor(att[:, :, q, :], lbank[0][q][:, 0:P].rearrange("p (k s) -> p k s", k=KH),
                                      m.dmask[:, :, :], ALU.mult).then_inc(BD[f"diag{q}"], 1)
                yield
                for i, half in enumerate(LEVELS):
                    dve.wait_ge(*BE(f"l{i}", t))
                    if i == 0:
                        dve.wait_ge(*BD("diag1", t))
                    dve.sem_inc(passed["dve"], 1)
                    for q in range(2):
                        dve.copy_predicated(att[:, :, q, :], m.lmask[:, i, :, :],
                                            lbank[(i + 1) % 2][q][:, 0:P].rearrange("p (k s) -> p k s", k=KH))\
                           .then_inc(BD[f"cp{i}{'ab'[q]}"], 1)
                    n = KH * P // (2 * half)
                    src = (tot[slot] if i == 0 else tots[LEVELS[i - 1]])[:, :].rearrange("p (n two) -> p n two", two=2)
                    if i:
                        dve.wait_ge(*BD(f"tot{i - 1}", t))
                    view = rp[slot][:, :, :].rearrange("p k (n two s) -> p (k n) two s", two=2, s=half)[:, :, 1, :]
                    dve.tensor_tensor(view, view, src[:, :, 0:1].to_broadcast([P, n, half]), ALU.mult)\
                       .then_inc(BD[f"rp{i}"], 1)
                    dve.tensor_tensor(tots[half][:, :].rearrange("p (n one) -> p n one", one=1), src[:, :, 0:1],
                                      src[:, :, 1:2], ALU.mult).then_inc(BD[f"tot{i}"], 1)
                    yield
                yield
                dve.wait_ge(*BD("tot5", t))
                dve.tensor_tensor(sdec[:, :, :], state[:, :, :],
                                  tots[32][:, :].rearrange("p (k b one) -> p k b one", b=BATCH, one=1)
                                  .rearrange("p k b one -> p (k b) one").to_broadcast([P, KH * BATCH, HEAD]),
                                  ALU.mult).then_inc(BD["sdec"], 1)
                dve.wait_ge(*BE("kv", t))
                dve.wait_ge(*BD("sdec", t))
                dve.tensor_tensor(state[:, :, :], sdec[:, :, :],
                                  ybank[:, CH:2 * CH].rearrange("p (n j) -> p n j", j=HEAD), ALU.add)\
                   .then_inc(BD["state"], 1)
                yield

            dve.wait_ge(ready, 1)
            run_pipeline(dve, [(front, 0), (back, 1)], TILES)

        @block.scalar
        def _(act):
            def front(t, slot, turn):
                yield
                yield
                act.activation(hT[slot][:, :, :, 0:1], hT[1 - slot][:, :, :, STEPS:STEPS + 1], ACT.Copy)\
                   .then_inc(FA["carry"], 1)
                act.wait_ge(*FE("hT", t))
                act.activation(hT[slot][:, :, :, 1:STEPS + 1],
                               hbank[:, 0:CH].rearrange("p (k b s) -> p k b s", k=KH, b=BATCH), ACT.Copy)\
                   .then_inc(FA["hT"], 1)
                yield
                act.wait_ge(*FE("m", t))
                act.activation(mt[:, :], hbank[:, CH:CH + P], ACT.Tanh).then_inc(FA["mt"], 1)
                yield
                yield
                yield
                act.wait_ge(*FE("d", t))
                act.activation(dt_[:, :], hbank[0:DECAY_RANK, CH + P:CH + 2 * P], ACT.Tanh).then_inc(FA["dt"], 1)
                act.wait_ge(*FE("w", t))
                for k in range(KH):
                    act.activation(ew[:, k, :], hbank[:, k * P:(k + 1) * P], ACT.Exp, bias=m.decay[:, k:k + 1])\
                       .then_inc(FA[f"ew{k}"], 1)
                act.wait_ge(*FA("ew1", t))
                act.activation(tot[slot][:, :], ew[:, :, :].rearrange("p k s -> p (k s)"), ACT.Exp, scale=-1.0)\
                   .then_inc(FA["w"], 1)
                yield
                act.wait_ge(*FE("r", t))
                act.activation(rp[slot][:, :, :], rkbank[:, 0:CH].rearrange("p (k s) -> p k s", k=KH), ACT.Copy)\
                   .then_inc(FA["r"], 1)
                yield
                act.wait_ge(*FE("k", t))
                act.activation(kq[slot][:, :, :], rkbank[:, CH:2 * CH].rearrange("p (k s) -> p k s", k=KH), ACT.Copy)\
                   .then_inc(FA["k"], 1)
                act.wait_ge(*FA("r", t))
                for k in range(KH):
                    act.activation(ru[slot][:, k, :], rp[slot][:, k, :], ACT.Copy, scale=m.bonus[:, k:k + 1])\
                       .then_inc(FA[f"ru{k}"], 1)
                act.wait_ge(*FE("v", t))
                act.activation(vt[slot][:, :], xbank[:, 0:CH], ACT.Copy).then_inc(FA["v"], 1)
                yield

            def back(t, slot, turn):
                for _ in range(7):
                    yield
                act.wait_ge(*BE("kT", t))
                for b in range(BATCH):
                    rows = slice(b * STEPS, (b + 1) * STEPS)
                    act.activation(kt[rows, b, :], ybank[rows, 0:CH], ACT.Copy).then_inc(BA[f"kt{b}"], 1)
                yield
                act.wait_ge(*BE("y", t))
                act.activation(m.y[:, bass.ds(t, 1), :].rearrange("p a c -> p (a c)"), lbank[0][0][:, 0:CH], ACT.Copy)\
                   .then_inc(BA["y"], 1)
                yield

            act.wait_ge(ready, 1)
            run_pipeline(act, [(front, 0), (back, 1)], TILES)

        @block.tensor
        def _(pe):
            def front(t, slot, turn):
                yield
                yield
                pe.wait_ge(*FP("h", t))
                for k in range(KH):
                    last = pe.transpose(hbank[:, k * P:(k + 1) * P], h[:, k * P:(k + 1) * P], m.ident[:, :])
                last.then_inc(FE["hT"], 1)
                yield
                pe.wait_ge(*FD("xxx", t))
                for k in range(KH):
                    last = pe.matmul(hbank[:, CH:CH + P], m.w1[:, k, :], xxx[:, k, :], start=(k == 0),
                                     stop=(k == KH - 1))
                last.then_inc(FE["m"], 1)
                yield
                pe.wait_ge(*FA("mt", t))
                for f in range(MIXES):
                    if f == 2:
                        pe.wait_ge(*FD("xf1", t))
                    for k in range(KH):
                        last = pe.matmul(xbank[:, (f % 2) * CH + k * P:(f % 2) * CH + (k + 1) * P],
                                         m.w2[:, f, k * P:(k + 1) * P], mt[:, :], start=True, stop=True)
                    last.then_inc(FE[f"x{f}"], 1)
                    if f == 1:
                        yield
                        yield
                pe.wait_ge(*FP("add0", t))
                for k in range(KH):
                    last = pe.matmul(hbank[0:DECAY_RANK, CH + P:CH + 2 * P], m.dw1[:, k, :], xf[:, 0, k, :],
                                     start=(k == 0), stop=(k == KH - 1))
                last.then_inc(FE["d"], 1)
                pe.wait_ge(*FA("dt", t))
                for k in range(KH):
                    last = pe.matmul(hbank[:, k * P:(k + 1) * P], m.dw2[:, k * P:(k + 1) * P], dt_[:, :],
                                     start=True, stop=True)
                last.then_inc(FE["w"], 1)
                yield
                for name, f, w, base in (("r", 3, m.wr, 0), ("k", 1, m.wk, CH)):
                    pe.wait_ge(*FP(f"add{f}", t))
                    if name == "k":
                        pe.wait_ge(*FA("r", t))
                    for o in range(KH):
                        for k in range(KH):
                            last = pe.matmul(rkbank[:, base + o * P:base + (o + 1) * P],
                                             w[:, k, o * P:(o + 1) * P], xf[:, f, k, :], start=(k == 0),
                                             stop=(k == KH - 1))
                    last.then_inc(FE[name], 1)
                pe.wait_ge(*FD("xf3", t))
                for k in range(KH):
                    last = pe.matmul(xbank[:, 0:CH], xf[:, 2, k, :], m.wv[:, k, :], start=(k == 0),
                                     stop=(k == KH - 1))
                last.then_inc(FE["v"], 1)
                yield

            def products(out, keys, queries):
                for k in range(KH):
                    for b in range(BATCH):
                        tok = slice(b * STEPS, (b + 1) * STEPS)
                        for q in range(2):
                            ch = slice(q * HEAD, (q + 1) * HEAD)
                            last = pe.matmul(out[q][tok, k * STEPS:(k + 1) * STEPS], keys[ch, k, tok],
                                             queries[ch, k, tok], start=True, stop=True)
                return last

            def back(t, slot, turn):
                pe.wait_ge(*FA("v", t))
                if begun(t, 1):
                    pe.wait_ge(*BA("y", t - 1))
                pe.sem_inc(passed["pe"], 1)
                products(lbank[0], kq[slot], ru[slot]).then_inc(BE["diag"], 1)
                yield
                for i in range(len(LEVELS)):
                    if i:
                        pe.wait_ge(*BD(f"rp{i - 1}", t))
                        pe.wait_ge(*BP(f"kq{i - 1}", t))
                        pe.sem_inc(passed["pe"], 1)
                    products(lbank[(i + 1) % 2], kq[slot], rp[slot]).then_inc(BE[f"l{i}"], 1)
                    yield
                pe.wait_ge(*BP("kq5", t))
                if begun(t, 1):
                    pe.wait_ge(*BD("state", t - 1))
                for k in range(KH):
                    last = pe.transpose(ybank[:, k * P:(k + 1) * P], kq[slot][:, k, :], m.ident[:, :])
                last.then_inc(BE["kT"], 1)
                yield
                pe.wait_ge(*BP("blk1", t))
                pe.wait_ge(*BD("rp5", t))
                out = lbank[0][0]
                for hd in range(HEADS):
                    pe.matmul(out[:, hd * HEAD:(hd + 1) * HEAD], blk[:, hd, :],
                              vt[slot][:, hd * HEAD:(hd + 1) * HEAD], start=(hd == 0), stop=False,
                              skip_group_check=True)
                for k in range(KH):
                    for b in range(BATCH):
                        tok = slice(b * STEPS, (b + 1) * STEPS)
                        last = pe.matmul(out[tok, k * P:(k + 1) * P], rp[slot][:, k, tok], sblk[:, k * BATCH + b, :],
                                         start=False, stop=True, skip_group_check=True)
                last.then_inc(BE["y"], 1)
                pe.wait_ge(*BA("kt1", t))
                for k in range(KH):
                    for b in range(BATCH):
                        for q in range(2):
                            ch = slice(k * P + q * HEAD, k * P + (q + 1) * HEAD)
                            n = k * BATCH + b
                            last = pe.matmul(ybank[q * HEAD:(q + 1) * HEAD, CH + n * HEAD:CH + (n + 1) * HEAD],
                                             kt[:, b, ch], vt[slot][:, ch], start=True, stop=True)
                last.then_inc(BE["kv"], 1)
                yield

            run_pipeline(pe, [(front, 0), (back, 1)], TILES)



def ffn_and_training(nc, m, a):
    ctx = ExitStack()
    with ctx:
        def sb(name, shape, dt=FP32):
            return ctx.enter_context(nc.sbuf_tensor(name, shape, dt))

        def sem(name):
            return ctx.enter_context(nc.semaphore(name))

        S = 4
        s1 = sb("b_s1", [P, HEADS])
        yc = sb("b_yc", [P, CH])
        sq = sb("b_sq", [P, CH])
        s2 = sb("b_s2", [P, HEADS])
        vh = sb("b_vh", [P, HEADS])
        rh = sb("b_rh", [P, HEADS])
        yn = sb("b_yn", [P, CH])
        ynT = sb("b_ynT", [P, KH, P])
        xb = sb("b_xb", [P, CH])
        t1 = sb("b_t1", [P, CH])
        x1 = sb("b_x1", [P, CH])
        x1b = sb("b_x1b", [P, CH])
        h2T = sb("b_h2T", [P, KH, P])
        t2 = sb("b_t2", [P, CH])
        x2 = sb("b_x2", [P, CH])
        stats = [sb(f"b_stats{i}", [P, 6]) for i in range(3)]
        mv = [sb(f"b_mv{i}", [P, 2]) for i in range(3)]
        ve = [sb(f"b_ve{i}", [P, 1]) for i in range(3)]
        rstd = [sb(f"b_rstd{i}", [P, 1]) for i in range(3)]
        xn = [sb(f"b_xn{i}", [P, CH]) for i in range(3)]
        xm = [sb(f"b_xm{i}", [P, CH]) for i in range(3)]
        h2 = sb("b_h2", [P, CH])
        h3 = [sb(f"b_h3_{s}", [P, CH]) for s in range(S)]
        h3T = [sb(f"b_h3T{s}", [P, KH, P]) for s in range(S)]
        v3 = [sb(f"b_v3_{s}", [P, CH]) for s in range(S)]
        h4 = sb("b_h4", [P, CH])
        h4T = sb("b_h4T", [P, KH, P])
        p0 = sb("b_p0", [P, 2, P])
        pw = [sb(f"b_pw{s}", [P, 2, P]) for s in range(2)]
        inv = [sb(f"b_inv{s}", [P, P]) for s in range(S)]
        diff = sb("b_diff", [P, CH])
        es = sb("b_es", [P, CH])
        yl = sb("b_yl", [P, CH])
        t3 = sb("b_t3", [P, CH])
        wt = m.w0t

        ready = sem("b_ready")
        passed = {e: sem(f"b_passed_{e}") for e in ("dve", "pool", "pe", "act")}
        FD = Steps(sem("ffn_dve"), "s1 yc s2 vh yn t1 x1 stats0 mv0 ve0 xn0 t2 x2 xst stats1 mv1 ve1 xn1 v3")
        FP = Steps(sem("ffn_pool"), "xb sq rh x1b rstd0 xm0 h2 rstd1 xm1 h3")
        FA = Steps(sem("ffn_act"), "ynT h2T h3T")
        FE = Steps(sem("ffn_pe"), "yT z h2T f h3T v")
        MD = Steps(sem("inverse_dve"), "p pT t0 " + " ".join(f"t{j}" for j in range(1, 6)))
        MA = Steps(sem("inverse_act"), " ".join(f"pw{j}" for j in range(1, 6)))
        ME = Steps(sem("inverse_pe"), "g sq1 " + " ".join(f"sq{j + 1} up{j}" for j in range(1, 5)) + " up5")
        BD = Steps(sem("train_dve"), "diff es yl")
        BP = Steps(sem("train_pool"), "t3 x3")
        BA = Steps(sem("train_act"), "w")
        BE = Steps(sem("train_pe"), "xw err dw")
        RD = Steps(sem("route_dve"), "stats mv ve xn logits")
        RP = Steps(sem("route_pool"), "rstd xm h4")
        RA = Steps(sem("route_act"), "h4T keep")
        RE = Steps(sem("route_pe"), "h4T logits")
        block = ctx.enter_context(nc.Block())
        tbank, obank, sqbank, upbank, ebank, wbank, rbank = (
            m.bank[0], m.bank[1], (m.bank[2], m.bank[3]), m.bank[4], m.bank[5], m.bank[6], m.bank[7])

        def at(stream, t):
            return stream[:, bass.ds(t, 1), :].rearrange("p a c -> p (a c)")

        def heads(ap):
            return ap.rearrange("p (h i) -> p h i", h=HEADS)

        def spread(ap, n):
            return ap.rearrange("p (h one) -> p h one", one=1).to_broadcast([P, ap.shape[1], n])

        @block.gpsimd
        def _(pool):
            def front(t, slot, turn):
                pool.tensor_tensor(xb[:, :], at(m.x, t), m.wob[:, :], ALU.add).then_inc(FP["xb"], 1)
                yield
                pool.wait_ge(*FD("yc", t))
                pool.tensor_tensor(sq[:, :], yc[:, :], yc[:, :], ALU.mult).then_inc(FP["sq"], 1)
                pool.wait_ge(*FD("vh", t))
                pool.tensor_tensor(rh[:, :], vh[:, :], m.half[:, :], ALU.pow).then_inc(FP["rh"], 1)
                yield
                yield
                yield
                pool.wait_ge(*FD("x1", t))
                pool.tensor_tensor(x1b[:, :], x1[:, :], m.bf[:, :], ALU.add).then_inc(FP["x1b"], 1)
                pool.wait_ge(*FD("ve0", t))
                pool.tensor_tensor(rstd[0][:, :], ve[0][:, :], m.half[:, 0:1], ALU.pow).then_inc(FP["rstd0"], 1)
                yield
                pool.wait_ge(*FD("xn0", t))
                pool.tensor_tensor(xm[0][:, :], xn[0][:, :], m.mod[0][:, 4, :], ALU.mult).then_inc(FP["xm0"], 1)
                pool.wait_ge(*FP("xm0", t))
                pool.tensor_tensor(h2[:, :], xm[0][:, :], m.mod[0][:, 3, :], ALU.add).then_inc(FP["h2"], 1)
                yield
                yield
                pool.wait_ge(*FD("ve1", t))
                pool.tensor_tensor(rstd[1][:, :], ve[1][:, :], m.half[:, 0:1], ALU.pow).then_inc(FP["rstd1"], 1)
                yield
                pool.wait_ge(*FD("xn1", t))
                pool.tensor_tensor(xm[1][:, :], xn[1][:, :], m.mod[1][:, 1, :], ALU.mult).then_inc(FP["xm1"], 1)
                pool.wait_ge(*FP("xm1", t))
                pool.tensor_tensor(h3[slot][:, :], xm[1][:, :], m.mod[1][:, 0, :], ALU.add).then_inc(FP["h3"], 1)
                yield

            def train(t, slot, turn):
                for _ in range(5):
                    yield
                pool.wait_ge(*BD("yl", t))
                pool.tensor_tensor(t3[:, :], yl[:, :], m.mod[1][:, 2, :], ALU.mult).then_inc(BP["t3"], 1)
                pool.wait_ge(*BP("t3", t))
                pool.sem_inc(passed["pool"], 1)
                pool.tensor_tensor(at(m.x, t), t3[:, :], at(m.x, t), ALU.add).then_inc(BP["x3"], 1)
                yield

            def route(t, slot, turn):
                pool.wait_ge(*RD("ve", t))
                pool.tensor_tensor(rstd[2][:, :], ve[2][:, :], m.half[:, 0:1], ALU.pow).then_inc(RP["rstd"], 1)
                yield
                yield
                pool.wait_ge(*RD("xn", t))
                pool.tensor_tensor(xm[2][:, :], xn[2][:, :], m.mod[1][:, 4, :], ALU.mult).then_inc(RP["xm"], 1)
                pool.wait_ge(*RP("xm", t))
                pool.tensor_tensor(h4[:, :], xm[2][:, :], m.mod[1][:, 3, :], ALU.add).then_inc(RP["h4"], 1)
                yield

            run_pipeline(pool, [(front, 0), (train, 2), (route, 3)], TILES, S)

        @block.vector
        def _(dve):
            def front(t, slot, turn):
                y = at(m.y, t)
                dve.tensor_reduce(s1[:, :], heads(y), AX.X, ALU.add).then_inc(FD["s1"], 1)
                dve.wait_ge(*FD("s1", t))
                dve.sem_inc(passed["dve"], 1)
                dve.scalar_tensor_tensor(heads(yc[:, :]), spread(s1[:, :], HEAD), -1.0 / HEAD, heads(y), ALU.mult,
                                         ALU.add).then_inc(FD["yc"], 1)
                yield
                dve.wait_ge(*FP("sq", t))
                dve.tensor_reduce(s2[:, :], heads(sq[:, :]), AX.X, ALU.add).then_inc(FD["s2"], 1)
                dve.wait_ge(*FD("s2", t))
                dve.tensor_scalar(vh[:, :], s2[:, :], 1.0 / HEAD, HEAD_EPS, ALU.mult, ALU.add).then_inc(FD["vh"], 1)
                yield
                dve.wait_ge(*FP("rh", t))
                dve.tensor_tensor(heads(yn[:, :]), heads(yc[:, :]), spread(rh[:, :], HEAD), ALU.mult)\
                   .then_inc(FD["yn"], 1)
                yield
                dve.wait_ge(*FE("z", t))
                dve.tensor_tensor(t1[:, :], obank[:, 0:CH], m.mod[0][:, 2, :], ALU.mult).then_inc(FD["t1"], 1)
                dve.wait_ge(*FD("t1", t))
                dve.wait_ge(*FP("xb", t))
                dve.tensor_tensor(x1[:, :], t1[:, :], xb[:, :], ALU.add).then_inc(FD["x1"], 1)
                yield
                dve.wait_ge(*FD("x1", t))
                dve.bn_stats(stats[0][:, :], x1[:, :]).then_inc(FD["stats0"], 1)
                dve.wait_ge(*FD("stats0", t))
                dve.sem_inc(passed["dve"], 1)
                dve.bn_aggr(mv[0][:, :], stats[0][:, :]).then_inc(FD["mv0"], 1)
                dve.wait_ge(*FD("mv0", t))
                dve.tensor_scalar_add(ve[0][:, :], mv[0][:, 1:2], LN_EPS).then_inc(FD["ve0"], 1)
                yield
                dve.wait_ge(*FP("rstd0", t))
                dve.tensor_scalar(xn[0][:, :], x1[:, :], mv[0][:, 0:1], rstd[0][:, 0:1], ALU.subtract, ALU.mult)\
                   .then_inc(FD["xn0"], 1)
                yield
                yield
                dve.wait_ge(*FE("f", t))
                dve.tensor_tensor(t2[:, :], obank[:, 0:CH], m.mod[0][:, 5, :], ALU.mult).then_inc(FD["t2"], 1)
                dve.wait_ge(*FD("t2", t))
                dve.wait_ge(*FP("x1b", t))
                dve.tensor_tensor(x2[:, :], t2[:, :], x1b[:, :], ALU.add).then_inc(FD["x2"], 1)
                dve.wait_ge(*FD("x2", t))
                dve.sem_inc(passed["dve"], 1)
                dve.tensor_copy(at(m.x, t), x2[:, :]).then_inc(FD["xst"], 1)
                dve.bn_stats(stats[1][:, :], x2[:, :]).then_inc(FD["stats1"], 1)
                dve.wait_ge(*FD("stats1", t))
                dve.sem_inc(passed["dve"], 1)
                dve.bn_aggr(mv[1][:, :], stats[1][:, :]).then_inc(FD["mv1"], 1)
                dve.wait_ge(*FD("mv1", t))
                dve.tensor_scalar_add(ve[1][:, :], mv[1][:, 1:2], LN_EPS).then_inc(FD["ve1"], 1)
                yield
                dve.wait_ge(*FP("rstd1", t))
                dve.tensor_scalar(xn[1][:, :], x2[:, :], mv[1][:, 0:1], rstd[1][:, 0:1], ALU.subtract, ALU.mult)\
                   .then_inc(FD["xn1"], 1)
                yield
                dve.wait_ge(*FE("v", t))
                dve.tensor_tensor(v3[slot][:, :], obank[:, 0:CH], m.bv[:, :], ALU.add).then_inc(FD["v3"], 1)
                yield

            def inverse(t, slot, turn):
                dve.wait_ge(*ME("g", t))
                dve.scalar_tensor_tensor(p0[:, 0, :], sqbank[0][:, 0:P], m.nbeta[:, 0:1], m.earlier[:, :], ALU.mult,
                                         ALU.mult).then_inc(MD["p"], 1)
                dve.scalar_tensor_tensor(p0[:, 1, :], sqbank[0][:, 0:P], m.nbeta[:, 0:1], m.later[:, :], ALU.mult,
                                         ALU.mult).then_inc(MD["pT"], 1)
                dve.wait_ge(*MD("pT", t))
                dve.tensor_tensor(inv[slot][:, :], p0[:, 1, :], m.ident[:, :], ALU.add).then_inc(MD["t0"], 1)
                yield
                yield
                for j in range(1, 6):
                    dve.wait_ge(*ME(f"up{j}", t))
                    dve.tensor_tensor(inv[slot][:, :], upbank[:, 0:P], inv[slot][:, :], ALU.add)\
                       .then_inc(MD[f"t{j}"], 1)
                    yield

            def train(t, slot, turn):
                yield
                dve.wait_ge(*BE("xw", t))
                dve.tensor_tensor(diff[:, :], ebank[:, 0:CH], v3[slot][:, :], ALU.subtract).then_inc(BD["diff"], 1)
                yield
                yield
                dve.wait_ge(*BE("err", t))
                dve.tensor_scalar(es[:, :], ebank[:, CH:2 * CH], m.nbeta[:, 0:1], None, ALU.mult)\
                   .then_inc(BD["es"], 1)
                dve.tensor_tensor(yl[:, :], ebank[:, CH:2 * CH], v3[slot][:, :], ALU.add).then_inc(BD["yl"], 1)
                yield

            def route(t, slot, turn):
                dve.wait_ge(*BP("x3", t))
                dve.sem_inc(passed["dve"], 1)
                dve.bn_stats(stats[2][:, :], at(m.x, t)).then_inc(RD["stats"], 1)
                dve.wait_ge(*RD("stats", t))
                dve.sem_inc(passed["dve"], 1)
                dve.bn_aggr(mv[2][:, :], stats[2][:, :]).then_inc(RD["mv"], 1)
                dve.wait_ge(*RD("mv", t))
                dve.tensor_scalar_add(ve[2][:, :], mv[2][:, 1:2], LN_EPS).then_inc(RD["ve"], 1)
                yield
                yield
                dve.wait_ge(*RP("rstd", t))
                dve.tensor_scalar(xn[2][:, :], at(m.x, t), mv[2][:, 0:1], rstd[2][:, 0:1], ALU.subtract, ALU.mult)\
                   .then_inc(RD["xn"], 1)
                yield
                yield
                yield
                yield
                dve.wait_ge(*RE("logits", t))
                dve.sem_inc(passed["dve"], 1)
                dve.tensor_tensor(at(m.logits, t), rbank[:, CH:CH + EXPERTS], m.bg[:, :], ALU.add)\
                   .then_inc(RD["logits"], 1)
                yield

            run_pipeline(dve, [(front, 0), (inverse, 1), (train, 2), (route, 3)], TILES, S)

        @block.scalar
        def _(act):
            def front(t, slot, turn):
                for name, dst, n in (("ynT", ynT, 3), ("h2T", h2T, 3), ("h3T", h3T[slot], 3)):
                    for _ in range(n):
                        yield
                    act.wait_ge(*FE({"ynT": "yT"}.get(name, name), t))
                    act.activation(dst[:, :, :], tbank[:, 0:CH].rearrange("p (k s) -> p k s", k=KH), ACT.Copy)\
                       .then_inc(FA[name], 1)
                yield

            def inverse(t, slot, turn):
                yield
                for j in range(1, 6):
                    act.wait_ge(*ME(f"sq{j}", t))
                    n = 2 if j < 5 else 1
                    act.activation(pw[j % 2][:, 0:n, :], sqbank[j % 2][:, 0:n * P].rearrange("p (n s) -> p n s", n=n),
                                   ACT.Copy).then_inc(MA[f"pw{j}"], 1)
                    yield

            def train(t, slot, turn):
                for _ in range(5):
                    yield
                act.wait_ge(*BE("dw", t))
                act.activation(wt[:, :, :], wbank[:, :].rearrange("p (k c) -> p k c", k=KH), ACT.Copy)\
                   .then_inc(BA["w"], 1)
                yield

            def route(t, slot, turn):
                for _ in range(4):
                    yield
                act.wait_ge(*RE("h4T", t))
                act.activation(h4T[:, :, :], rbank[:, 0:CH].rearrange("p (k s) -> p k s", k=KH), ACT.Copy)\
                   .then_inc(RA["h4T"], 1)
                act.activation(at(m.y, t), h4[:, :], ACT.Copy).then_inc(RA["keep"], 1)
                yield

            run_pipeline(act, [(front, 0), (inverse, 1), (train, 2), (route, 3)], TILES, S)

        @block.tensor
        def _(pe):
            for k in range(KH):
                pe.matmul(wbank[:, k * CH:(k + 1) * CH], m.ident[:, :], m.w0t[:, k, :], start=(k == 0), stop=False,
                          skip_group_check=True)

            def turned(out, src):
                for k in range(KH):
                    last = pe.transpose(out[:, k * P:(k + 1) * P], src[:, k * P:(k + 1) * P], m.ident[:, :])
                return last

            def project(out, lhs, w):
                for k in range(KH):
                    last = pe.matmul(out, lhs[:, k, :], w[:, k, :], start=(k == 0), stop=(k == KH - 1))
                return last

            def front(t, slot, turn):
                yield
                yield
                pe.wait_ge(*FD("yn", t))
                turned(tbank, yn).then_inc(FE["yT"], 1)
                yield
                pe.wait_ge(*FA("ynT", t))
                project(obank[:, 0:CH], ynT, m.wo).then_inc(FE["z"], 1)
                yield
                yield
                yield
                pe.wait_ge(*FP("h2", t))
                turned(tbank, h2).then_inc(FE["h2T"], 1)
                pe.wait_ge(*FA("h2T", t))
                project(obank[:, 0:CH], h2T, m.wf).then_inc(FE["f"], 1)
                yield
                yield
                yield
                pe.wait_ge(*FP("h3", t))
                turned(tbank, h3[slot]).then_inc(FE["h3T"], 1)
                pe.wait_ge(*FA("h3T", t))
                project(obank[:, 0:CH], h3T[slot], m.wvt).then_inc(FE["v"], 1)
                yield

            def inverse(t, slot, turn):
                pe.wait_ge(*FA("h3T", t))
                for k in range(KH):
                    last = pe.matmul(sqbank[0][:, 0:P], h3T[slot][:, k, :], h3T[slot][:, k, :], start=(k == 0),
                                     stop=(k == KH - 1))
                last.then_inc(ME["g"], 1)
                yield
                for j in range(1, 6):
                    src = p0 if j == 1 else pw[(j - 1) % 2]
                    if j == 1:
                        pe.wait_ge(*MD("t0", t))
                    else:
                        pe.wait_ge(*MA(f"pw{j - 1}", t))
                    last = pe.matmul(sqbank[j % 2][:, 0:P], src[:, 1, :], src[:, 0, :], start=True, stop=True)
                    if j < 5:
                        last = pe.matmul(sqbank[j % 2][:, P:2 * P], src[:, 0, :], src[:, 1, :], start=True, stop=True)
                    last.then_inc(ME[f"sq{j}"], 1)
                    if j > 1:
                        pe.wait_ge(*MD(f"t{j - 2}", t))
                        pe.matmul(upbank[:, 0:P], src[:, 0, :], inv[slot][:, :], start=True, stop=True)\
                          .then_inc(ME[f"up{j - 1}"], 1)
                    yield
                pe.wait_ge(*MA("pw5", t))
                pe.wait_ge(*MD("t4", t))
                pe.matmul(upbank[:, 0:P], pw[1][:, 0, :], inv[slot][:, :], start=True, stop=True)\
                  .then_inc(ME["up5"], 1)
                yield

            def train(t, slot, turn):
                if begun(t, 1):
                    pe.wait_ge(*BA("w", t - 1))
                pe.wait_ge(*FD("v3", t))
                project(ebank[:, 0:CH], h3T[slot], wt).then_inc(BE["xw"], 1)
                yield
                yield
                pe.wait_ge(*BD("diff", t))
                pe.wait_ge(*MD("t5", t))
                pe.matmul(ebank[:, CH:2 * CH], inv[slot][:, :], diff[:, :], start=True, stop=True)\
                  .then_inc(BE["err"], 1)
                yield
                yield
                pe.wait_ge(*BD("yl", t))
                for k in range(KH):
                    last = pe.matmul(wbank[:, k * CH:(k + 1) * CH], h3[slot][:, k * P:(k + 1) * P], es[:, :],
                                     start=False, stop=False, skip_group_check=True)
                last.then_inc(BE["dw"], 1)
                yield

            def route(t, slot, turn):
                for _ in range(4):
                    yield
                pe.wait_ge(*RP("h4", t))
                turned(rbank, h4).then_inc(RE["h4T"], 1)
                yield
                pe.wait_ge(*RA("keep", t))
                for k in range(KH):
                    last = pe.matmul(rbank[:, CH:CH + EXPERTS], h4T[:, k, :], m.wg[:, k, :], start=(k == 0),
                                     stop=(k == KH - 1))
                last.then_inc(RE["logits"], 1)
                yield

            run_pipeline(pe, [(front, 0), (inverse, 1), (train, 2), (route, 3)], TILES, S)


def routing(nc, m, r):
    ctx = ExitStack()
    with ctx:
        def sb(name, shape, dt=FP32):
            return ctx.enter_context(nc.sbuf_tensor(name, shape, dt))

        E, T = EXPERTS, TILES
        KET = TOPK * E * T
        number = sb("c_number", [P, E], I32)
        eight = sb("c_eight", [P, T, E])
        base = sb("c_base", [P, E])
        own = sb("c_own", [P, TOPK, T])
        owni = sb("c_owni", [P, TOPK, T], I32)
        numf = sb("c_numf", [P, E])
        best = [sb(f"c_best{k}", [P, T]) for k in range(TOPK)]
        eq = sb("c_eq", [P, T, E])
        first = sb("c_first", [P, T])
        oh = [sb(f"c_oh{k}", [P, T, E]) for k in range(TOPK)]
        rest = sb("c_rest", [P, T, E])
        gap = sb("c_gap", [P, T])
        expg = sb("c_expg", [P, T])
        den = sb("c_den", [P, T])
        ohs = sb("c_ohs", [P, TOPK, E, T])
        same = sb("c_same", [P, P])
        before = sb("c_before", [P, P])
        prior = sb("c_prior", [P, P])
        every = sb("c_every", [P, P])
        keepon = sb("c_keepon", [P, TOPK, E, T])
        tiles_ = sb("c_tiles", [P, KET])
        upto = sb("c_upto", [P, KET])
        pos = sb("c_pos", [P, TOPK, E, T])
        batch0 = sb("c_batch0", [P, TOPK * E])
        choice0 = sb("c_choice0", [P, E])
        picked = sb("c_picked", [P, TOPK, E, T])
        spot = sb("c_spot", [P, TOPK, T])
        keep = sb("c_keep", [P, TOPK, T])
        row = sb("c_row", [P, TOPK, T])
        dest = sb("c_dest", [P, TOPK, T])

        done = ctx.enter_context(nc.semaphore("c_dve"))
        made = ctx.enter_context(nc.semaphore("c_pool"))
        counted = ctx.enter_context(nc.semaphore("c_pe"))
        expd = ctx.enter_context(nc.semaphore("c_act"))
        block = ctx.enter_context(nc.Block())
        marks = {}

        @block.gpsimd
        def _(pool):
            pool.iota(number[:, :], pattern=[[1, E]], base=0, channel_multiplier=0)
            pool.iota(owni[:, :, :], pattern=[[T * P, TOPK], [P, T]], base=DROPPED, channel_multiplier=1)
            pool.memset(every[:, :], 1.0)
            pool.memset(keepon[:, :, :, :], 1.0)
            pool.memset(prior[:, :], 0.0).then_inc(made, 1)

        @block.vector
        def _(dve):
            state = [0]

            def then(ins):
                ins.then_inc(done, 1)
                state[0] += 1
                dve.wait_ge(done, state[0])
                return state[0]

            def over_e(ap):
                return ap.rearrange("p (t one) -> p t one", one=1).to_broadcast([P, T, E])

            def by_expert(ap):
                return ap.rearrange("p t e -> p e t")

            dve.wait_ge(made, 1)
            then(dve.tensor_copy(numf[:, :], number[:, :]))
            then(dve.tensor_copy(own[:, :, :], owni[:, :, :]))
            then(dve.tensor_scalar(base[:, :], numf[:, :], float(SLOTS), None, ALU.mult))
            for t in range(T):
                last = dve.tensor_scalar(eight[:, t, :], numf[:, :], -1.0, float(E), ALU.mult, ALU.add)
            then(last)
            scores = m.logits
            for k in range(TOPK):
                then(dve.tensor_reduce(best[k][:, :], scores[:, :, :], AX.X, ALU.max))
                then(dve.tensor_tensor(eq[:, :, :], scores[:, :, :], over_e(best[k][:, :]), ALU.is_equal))
                then(dve.tensor_tensor(eq[:, :, :], eq[:, :, :], eight[:, :, :], ALU.mult))
                then(dve.tensor_reduce(first[:, :], eq[:, :, :], AX.X, ALU.max))
                then(dve.tensor_tensor(oh[k][:, :, :], eight[:, :, :], over_e(first[:, :]), ALU.is_equal))
                then(dve.tensor_copy(ohs[:, k, :, :], by_expert(oh[k][:, :, :])))
                if k == 0:
                    then(dve.scalar_tensor_tensor(rest[:, :, :], oh[0][:, :, :], -3e38, m.logits[:, :, :], ALU.mult,
                                                  ALU.add))
                    scores = rest
            for b in range(BATCH):
                cols = slice(b * STEPS, (b + 1) * STEPS)
                then(dve.tensor_scalar(same[:, cols], every[:, cols], m.side[:, b:b + 1], None, ALU.mult))
            then(dve.tensor_tensor(before[:, :], same[:, :], m.later[:, :], ALU.mult))
            then(dve.tensor_scalar(prior[:, STEPS:P], every[:, STEPS:P], m.side[:, 0:1], None, ALU.mult))
            then(dve.memset(keepon[:, :, :, 0:1], 0.0))
            marks["pe"] = state[0]
            marks["gap"] = then(dve.tensor_tensor(gap[:, :], best[1][:, :], best[0][:, :], ALU.subtract))
            dve.wait_ge(expd, 1)
            then(dve.tensor_scalar_add(den[:, :], expg[:, :], 1.0))
            then(dve.reciprocal(r.gate[:, 0, :], den[:, :]))
            then(dve.tensor_tensor(r.gate[:, 1, :], r.gate[:, 0, :], expg[:, :], ALU.mult))
            dve.wait_ge(counted, 4)
            then(dve.tensor_copy(tiles_[:, :], m.bank[1][:, :]))
            then(dve.tensor_tensor_scan(upto[:, :], keepon[:, :, :, :].rearrange("p k e t -> p (k e t)"), tiles_[:, :],
                                        0.0, ALU.mult, ALU.add))
            flat = pos[:, :, :, :].rearrange("p k e t -> p (k e t)")
            then(dve.tensor_tensor(flat, upto[:, :], tiles_[:, :], ALU.subtract))
            then(dve.tensor_tensor(flat, m.bank[0][:, :], flat, ALU.add))
            then(dve.tensor_reduce(batch0[:, :], m.bank[2][:, :].rearrange("p (n t) -> p n t", t=T), AX.X, ALU.add))
            then(dve.tensor_reduce(choice0[:, :], m.bank[3][:, 0:E * T].rearrange("p (n t) -> p n t", t=T), AX.X,
                                   ALU.add))
            pket = pos[:, :, :, :].rearrange("p k e t -> p (k e) t")
            then(dve.tensor_tensor(pket, pket, batch0[:, :].rearrange("p (n one) -> p n one", one=1)
                                   .to_broadcast([P, TOPK * E, T]), ALU.add))
            then(dve.tensor_tensor(pos[:, 1, :, :], pos[:, 1, :, :], choice0[:, :].rearrange("p (n one) -> p n one", one=1)
                                   .to_broadcast([P, E, T]), ALU.add))
            for k in range(TOPK):
                then(dve.tensor_tensor(picked[:, k, :, :], pos[:, k, :, :], ohs[:, k, :, :], ALU.mult))
                then(dve.tensor_reduce(spot[:, k, :], picked[:, k, :, :].rearrange("p e t -> p t e"), AX.X, ALU.add))
                then(dve.tensor_tensor(picked[:, k, :, :], ohs[:, k, :, :],
                                       base[:, :].rearrange("p (n one) -> p n one", one=1).to_broadcast([P, E, T]),
                                       ALU.mult))
                then(dve.tensor_reduce(row[:, k, :], picked[:, k, :, :].rearrange("p e t -> p t e"), AX.X, ALU.add))
            then(dve.tensor_tensor(row[:, :, :], row[:, :, :], spot[:, :, :], ALU.add))
            then(dve.tensor_scalar(keep[:, :, :], spot[:, :, :], float(CAPACITY), None, ALU.is_lt))
            then(dve.tensor_tensor(r.gate[:, :, :], r.gate[:, :, :], keep[:, :, :], ALU.mult))
            then(dve.tensor_tensor(dest[:, :, :], row[:, :, :], own[:, :, :], ALU.subtract))
            then(dve.tensor_tensor(dest[:, :, :], dest[:, :, :], keep[:, :, :], ALU.mult))
            then(dve.tensor_tensor(dest[:, :, :], dest[:, :, :], own[:, :, :], ALU.add))
            then(dve.tensor_copy(r.put[:, :, :], dest[:, :, :]))
            then(dve.tensor_tensor(row[:, :, :], row[:, :, :], keep[:, :, :], ALU.mult))
            then(dve.tensor_copy(r.get[:, :, :], row[:, :, :]))

        @block.scalar
        def _(act):
            act.wait_ge(done, marks["gap"])
            act.activation(expg[:, :], gap[:, :], ACT.Exp).then_inc(expd, 1)

        @block.tensor
        def _(pe):
            pe.wait_ge(made, 1)
            pe.wait_ge(done, marks["pe"])
            chosen = ohs[:, :, :, :].rearrange("p k e t -> p (k e t)")
            for i, mask in enumerate((before, same, prior, every)):
                pe.matmul(m.bank[i][:, :], mask[:, :], chosen, start=True, stop=True).then_inc(counted, 1)


def experts(nc, m, r, a, out):
    ctx = ExitStack()
    with ctx:
        def sb(name, shape, dt=FP32):
            return ctx.enter_context(nc.sbuf_tensor(name, shape, dt))

        def sem(name):
            return ctx.enter_context(nc.semaphore(name))

        SPLIT = ((0, ROWS // 16 * 16), (ROWS // 16 * 16, ROWS))
        E2 = 2
        w1 = [sb(f"d_w1_{s}", [P, KH, HIDDEN]) for s in range(E2)]
        w2 = [sb(f"d_w2_{s}", [P, FT, CH]) for s in range(E2)]
        b1 = [sb(f"d_b1_{s}", [P, FT]) for s in range(E2)]
        b2 = [sb(f"d_b2_{s}", [P, CH]) for s in range(E2)]
        rows = [sb(f"d_rows{s}", [ROWS, 2, CH]) for s in range(2)]
        xg = [sb(f"d_xg{s}", [P, KH, GROUP]) for s in range(2)]
        hid = [sb(f"d_hid{s}", [P, FT, GROUP]) for s in range(2)]
        res = [sb(f"d_res{s}", [ROWS, 2, CH]) for s in range(2)]

        put_done = sem("d_put")
        w_in = [sem(f"d_w_in{s}") for s in range(E2)]
        rows_in = [sem(f"d_rows_in{s}") for s in range(2)]
        res_out = [sem(f"d_res_out{s}") for s in range(2)]
        passed = {e: sem(f"d_passed_{e}") for e in ("dve", "pe", "act")}
        TD = Steps(sem("turn_dve"), "xg")
        TE = Steps(sem("turn_pe"), "turned")
        ED = Steps(sem("expert_dve"), "res")
        EA = Steps(sem("expert_act"), " ".join(f"gelu{f}" for f in range(FT)))
        EE = Steps(sem("expert_pe"), " ".join(f"up{f}" for f in range(0, FT, 2)) + " down")
        block = ctx.enter_context(nc.Block())
        N = EXPERTS * GROUPS
        U = E2 * GROUPS

        @block.gpsimd
        def _(pool):
            for t in range(TILES):
                for k in range(TOPK):
                    pool.indirect_dma_start(
                        out=r.sent[:, :], out_offset=bass.IndirectOffsetOnAxis(ap=r.put[:, k, t:t + 1], axis=0),
                        in_=m.y[:, t, :], in_offset=None).then_inc(put_done, 16)

        @block.sync
        def _(sp):
            def weights(e, s):
                sp.dma_start(w1[s][:, :, :], a["L1_ffn_W1"][bass.ds(e, 1), :, :]
                             .rearrange("a (k p) f -> p (a k) f", p=P)).then_inc(w_in[s], 16)
                sp.dma_start(w2[s][:, :, :], a["L1_ffn_W2"][bass.ds(e, 1), :, :]
                             .rearrange("a (k p) f -> p (a k) f", p=P)).then_inc(w_in[s], 16)
                with nc.allow_non_contiguous_dma(reason="an expert's bias, by hidden unit"):
                    sp.dma_start(b1[s][:, :], a["L1_ffn_b1"][bass.ds(e, 1), :]
                                 .rearrange("a (k p) -> p (a k)", p=P)).then_inc(w_in[s], 16)
                sp.dma_start(b2[s][:, :], a["L1_ffn_b2"][bass.ds(e, 1), :].to_broadcast([P, CH]))\
                  .then_inc(w_in[s], 16)

            for s in range(E2):
                weights(s, s)
            sp.wait_ge(put_done, 16 * TILES * TOPK)

            def fetch(n, slot, turn):
                if slot % GROUPS == 0 and begun(n, U):
                    sp.wait_ge(*EE("down", n - GROUPS - 1))
                    sp.wait_ge(*ED("res", n - GROUPS - 1))
                    weights(turn * E2 + slot // GROUPS, slot // GROUPS)
                if begun(n, 2):
                    sp.wait_ge(*TE("turned", n - 2))
                for lo, hi in SPLIT:
                    sp.dma_start(rows[slot % 2][lo:hi, :, :], r.sent[bass.ds(n * GROUP, GROUP), :]
                                 .rearrange("(a p) c -> p a c", p=ROWS)[lo:hi, :, :]).then_inc(rows_in[slot % 2], 16)
                yield

            def store(n, slot, turn):
                sp.wait_ge(*ED("res", n))
                for lo, hi in SPLIT:
                    sp.dma_start(r.back[bass.ds(n * GROUP, GROUP), :].rearrange("(a p) c -> p a c", p=ROWS)[lo:hi, :, :],
                                 res[slot % 2][lo:hi, :, :]).then_inc(res_out[slot % 2], 16)
                yield

            run_pipeline(sp, [(fetch, 0), (store, 2)], N, U)
            for s in range(2):
                sp.wait_ge(res_out[s], 32 * (N // 2))

        @block.vector
        def _(dve):
            def turn_in(n, slot, turn):
                dve.wait_ge(*TE("turned", n))
                dve.sem_inc(passed["dve"], 1)
                dve.tensor_copy(xg[slot % 2][:, :, :].rearrange("p k s -> p (k s)"),
                                m.bank[0][:, 0:KH * GROUP]).then_inc(TD["xg"], 1)
                yield

            def result(n, slot, turn):
                s = slot // GROUPS
                dve.wait_ge(w_in[s], turn * 64 + 64)
                dve.wait_ge(*EE("down", n))
                if begun(n, 2):
                    dve.wait_ge(res_out[slot % 2], (turn * (U // 2) + slot // 2) * 32)
                for i in range(2):
                    last = dve.tensor_tensor(res[slot % 2][:, i, :], m.bank[5 + slot % 2][0:ROWS, i * CH:(i + 1) * CH],
                                             b2[s][0:ROWS, :], ALU.add)
                last.then_inc(ED["res"], 1)
                yield

            run_pipeline(dve, [(turn_in, 0), (result, 1)], N, U)

        @block.scalar
        def _(act):
            def gelu(n, slot, turn):
                s = slot // GROUPS
                act.wait_ge(w_in[s], turn * 64 + 64)
                for f in range(FT):
                    if f % 2 == 0:
                        act.wait_ge(*EE(f"up{f}", n))
                    act.activation(hid[slot % 2][:, f, :], m.bank[1 + f // 2][:, (f % 2) * GROUP:(f % 2 + 1) * GROUP],
                                   ACT.Gelu_apprx_tanh, bias=b1[s][:, f:f + 1]).then_inc(EA[f"gelu{f}"], 1)
                yield

            run_pipeline(act, [(gelu, 1)], N, U)

        @block.tensor
        def _(pe):
            def turn_in(n, slot, turn):
                pe.wait_ge(rows_in[slot % 2], (turn * (U // 2) + (slot // 2 + 1)) * 32)
                if begun(n, 1):
                    pe.wait_ge(*TD("xg", n - 1))
                for k in range(KH):
                    for i in range(2):
                        last = pe.transpose(m.bank[0][:, k * GROUP + i * ROWS:k * GROUP + (i + 1) * ROWS],
                                            rows[slot % 2][:, i, k * P:(k + 1) * P], m.ident[0:ROWS, 0:ROWS])
                last.then_inc(TE["turned"], 1)
                yield

            def up(n, slot, turn):
                s = slot // GROUPS
                pe.wait_ge(w_in[s], turn * 64 + 64)
                pe.wait_ge(*TD("xg", n))
                for f in range(FT):
                    if f % 2 == 0 and begun(n, 1):
                        pe.wait_ge(*EA(f"gelu{f + 1}", n - 1))
                    for k in range(KH):
                        last = pe.matmul(m.bank[1 + f // 2][:, (f % 2) * GROUP:(f % 2 + 1) * GROUP],
                                         w1[s][:, k, f * P:(f + 1) * P], xg[slot % 2][:, k, :], start=(k == 0),
                                         stop=(k == KH - 1))
                    if f % 2:
                        last.then_inc(EE[f"up{f - 1}"], 1)
                yield

            def down(n, slot, turn):
                s = slot // GROUPS
                if begun(n, 2):
                    pe.wait_ge(*ED("res", n - 2))
                pe.wait_ge(*EA("gelu7", n))
                for i in range(2):
                    for f in range(FT):
                        last = pe.matmul(m.bank[5 + slot % 2][0:ROWS, i * CH:(i + 1) * CH],
                                         hid[slot % 2][:, f, i * ROWS:(i + 1) * ROWS], w2[s][:, f, :],
                                         start=(f == 0), stop=(f == FT - 1))
                last.then_inc(EE["down"], 1)
                yield

            run_pipeline(pe, [(up, 1), (turn_in, 0), (down, 1)], N, U)


def combine(nc, m, r, out):
    ctx = ExitStack()
    with ctx:
        def sb(name, shape, dt=FP32):
            return ctx.enter_context(nc.sbuf_tensor(name, shape, dt))

        def sem(name):
            return ctx.enter_context(nc.semaphore(name))

        S = 4
        got = [sb(f"e_got{s}", [P, TOPK, CH]) for s in range(S)]
        one = [sb(f"e_one{s}", [P, CH]) for s in range(2)]
        two = [sb(f"e_two{s}", [P, CH]) for s in range(2)]
        gated = [sb(f"e_gated{s}", [P, CH]) for s in range(2)]
        final = [sb(f"e_final{s}", [P, CH]) for s in range(S)]
        got_in = [sem(f"e_got_in{s}") for s in range(S)]
        stored = [sem(f"e_stored{s}") for s in range(S)]
        CD = Steps(sem("combine_dve"), "one two gated final")
        block = ctx.enter_context(nc.Block())

        @block.gpsimd
        def _(pool):
            for t in range(TILES):
                if t >= S:
                    pool.wait_ge(*CD("two", t - S))
                for k in range(TOPK):
                    pool.indirect_dma_start(
                        out=got[t % S][:, k, :], out_offset=None, in_=r.back[:, :],
                        in_offset=bass.IndirectOffsetOnAxis(ap=r.get[:, k, t:t + 1], axis=0)).then_inc(got_in[t % S], 16)

        @block.vector
        def _(dve):
            def add(t, slot, turn):
                x = m.x[:, bass.ds(t, 1), :].rearrange("p a c -> p (a c)")
                dve.wait_ge(got_in[slot], turn * 32 + 32)
                dve.tensor_scalar(one[slot % 2][:, :], got[slot][:, 0, :], r.gate[:, 0, bass.ds(t, 1)], None, ALU.mult)\
                   .then_inc(CD["one"], 1)
                dve.wait_ge(*CD("one", t))
                dve.scalar_tensor_tensor(two[slot % 2][:, :], got[slot][:, 1, :], r.gate[:, 1, bass.ds(t, 1)],
                                         one[slot % 2][:, :], ALU.mult, ALU.add).then_inc(CD["two"], 1)
                dve.wait_ge(*CD("two", t))
                dve.tensor_tensor(gated[slot % 2][:, :], two[slot % 2][:, :], m.mod[1][:, 5, :], ALU.mult)\
                   .then_inc(CD["gated"], 1)
                dve.wait_ge(*CD("gated", t))
                if begun(t, S):
                    dve.wait_ge(stored[slot], turn * 32)
                dve.tensor_tensor(final[slot][:, :], gated[slot % 2][:, :], x, ALU.add).then_inc(CD["final"], 1)
                yield

            run_pipeline(dve, [(add, 0)], TILES, S)

        @block.sync
        def _(sp):
            def store(t, slot, turn):
                sp.wait_ge(*CD("final", t))
                for b in range(BATCH):
                    sp.dma_start(out[b, bass.ds(t * STEPS, STEPS), :], final[slot][b * STEPS:(b + 1) * STEPS, :])\
                      .then_inc(stored[slot], 16)
                yield

            run_pipeline(sp, [(store, 0)], TILES, S)
            for s in range(S):
                sp.wait_ge(stored[s], 32 * (TILES // S))


def clear(nc, r):
    ctx = ExitStack()
    with ctx:
        rows, parts = 80, 3
        size = NSLOT * CH // rows // parts
        zero = ctx.enter_context(nc.sbuf_tensor("zero", [rows, size], FP32))
        zeroed = ctx.enter_context(nc.semaphore("zero_made"))
        cleared = ctx.enter_context(nc.semaphore("cleared"))
        block = ctx.enter_context(nc.Block())
        flat = r.sent[0:NSLOT, :].rearrange("(p a) c -> p (a c)", p=rows)

        @block.vector
        def _(dve):
            dve.memset(zero[:, :], 0.0).then_inc(zeroed, 1)

        @block.sync
        def _(sp):
            sp.wait_ge(zeroed, 1)
            for i in range(parts):
                sp.dma_start(flat[:, i * size:(i + 1) * size], zero[:, :]).then_inc(cleared, 16)
            sp.wait_ge(cleared, 16 * parts)


def program(nc, a, out):
    ctx = ExitStack()
    with ctx:
        m = alloc(nc, ctx)
        r = Memory()
        r.gate = m.sb("gate", [P, TOPK, TILES])
        r.put = m.sb("put", [P, TOPK, TILES], I32)
        r.get = m.sb("get", [P, TOPK, TILES], I32)
        r.sent = nc.dram_tensor("sent", (NSLOT + TOPK * TOKENS, CH), FP32, kind="Internal").ap()
        r.back = nc.dram_tensor("results", (NSLOT, CH), FP32, kind="Internal").ap()
        clear(nc, r)
        prologue(nc, m, a)
        time_mix(nc, m, a)
        ffn_and_training(nc, m, a)
        routing(nc, m, r)
        experts(nc, m, r, a, out)
        combine(nc, m, r, out)


def kernel(**inputs):
    import concourse.bacc as _bacc
    from concourse.bass_utils import run_bass_kernel_spmd as _run

    nc = _bacc.Bacc("TRN2", target_bir_lowering=False, num_devices=1)
    used = [n for n in inputs if n not in ("L0_attn_key", "L0_attn_value")]
    arrays, aps = {}, {}
    for name in used:
        arr = np.ascontiguousarray(inputs[name])
        arrays[f"in_{name}"] = arr
        aps[name] = nc.dram_tensor(f"in_{name}", arr.shape, mybir.dt.from_np(arr.dtype), kind="ExternalInput").ap()
    out = nc.dram_tensor("out", (BATCH, TIME, CH), FP32, kind="ExternalOutput").ap()
    program(nc, aps, out)
    return _run(nc, [arrays], core_ids=[0]).results[0]["out"]
```

```python
import numpy as np
from contextlib import ExitStack

import concourse.bass as bass
from concourse import mybir

FP32 = mybir.dt.float32
I32 = mybir.dt.int32
ALU = mybir.AluOpType
ACT = mybir.ActivationFunctionType
AX = mybir.AxisListType

BATCH, TIME, CH = 2, 2048, 256
P = 128
KH = CH // P
STEPS = P // BATCH
TILES = TIME // STEPS
HEAD = 64
HEADS = CH // HEAD
MIX, MIXES = 32, 4
DECAY_RANK = 64
LEVELS = [1, 2, 4, 8, 16, 32]
RANK, DDIM, UDIM = 4, 100, 50
EXPERTS, TOPK, HIDDEN = 8, 2, 1024
TOKENS = BATCH * TIME
CAPACITY = int(np.ceil(1.2 * TOKENS * TOPK / EXPERTS))
ROWS = 123
GROUP = 2 * ROWS
GROUPS = -(-CAPACITY // GROUP)
SLOTS = GROUPS * GROUP
NSLOT = EXPERTS * SLOTS
DROPPED = NSLOT
FT = HIDDEN // P
LN_EPS, HEAD_EPS = 1e-5, 0.00064
LAST_STEP = 23


class Steps:

    def __init__(self, sem, names):
        self.sem, self.names, self.at = sem, names.split(), 0

    def __getitem__(self, name):
        assert self.names[self.at] == name, (self.names[self.at], name)
        self.at = (self.at + 1) % len(self.names)
        return self.sem

    def __call__(self, name, t):
        return self.sem, t * len(self.names) + (self.names.index(name) + 1)


def run_pipeline(eng, chains, tiles, slots):
    lag = max(l for _, l in chains)
    head = lag + slots
    turns = (tiles - head) // slots

    def one_round(parts):
        work = [f(*at) for f, *at in parts]
        place = [next(g) for g in work]
        for step in range(LAST_STEP + 1):
            for n, g in enumerate(work):
                while place[n] == step:
                    place[n] = next(g, None)
        assert not any(p is not None for p in place)

    def peeled(i):
        one_round([(f, i - l, (i - l) % slots, (i - l) // slots) for f, l in chains if 0 <= i - l < tiles])

    for i in range(head):
        peeled(i)
    with eng.Fori(0, turns, 1) as turn:
        for s in range(slots):
            one_round([(f, turn * slots + (head + s - l), (head + s - l) % slots, turn + (head + s - l) // slots)
                       for f, l in chains])
    for i in range(head + turns * slots, tiles + lag):
        peeled(i)


def begun(t, distance):
    return not isinstance(t, int) or t >= distance


def followed(t):
    return not isinstance(t, int) or t < TILES - 1


class Memory:
    pass


def alloc(nc, ctx):
    m = Memory()

    def sb(name, shape, dt=FP32):
        return ctx.enter_context(nc.sbuf_tensor(name, shape, dt))

    m.sb = sb
    m.ident = sb("ident", [P, P])
    m.x = sb("x_stream", [P, TILES, CH])
    m.y = sb("y_stream", [P, TILES, CH])
    m.mod = [sb(f"mod{l}", [P, 6, CH]) for l in range(2)]
    m.half = sb("minus_half", [P, 4])
    m.bank = [ctx.enter_context(nc.psum_tensor(f"bank{i}", [P, 512], FP32)) for i in range(8)]
    m.side = sb("side", [P, 2])
    m.maa = sb("maa", [P, 5, KH])
    m.w1 = sb("w1", [P, KH, P])
    m.w2 = sb("w2", [P, MIXES, CH])
    m.dw1 = sb("dw1", [P, KH, DECAY_RANK])
    m.dw2 = sb("dw2", [DECAY_RANK, CH])
    m.decay = sb("decay", [P, KH])
    m.bonus = sb("bonus", [P, KH])
    m.wr = sb("wr", [P, KH, CH])
    m.wk = sb("wk", [P, KH, CH])
    m.wv = sb("wv", [P, KH, CH])
    m.lmask = sb("lmask", [P, len(LEVELS), 2, STEPS], I32)
    m.dmask = sb("dmask", [P, 2, STEPS])
    m.wo = sb("wo", [P, KH, CH])
    m.wob = sb("wob", [P, CH])
    m.wf = sb("wf", [P, KH, CH])
    m.bf = sb("bf", [P, CH])
    m.wvt = sb("wvt", [P, KH, CH])
    m.bv = sb("bv", [P, CH])
    m.w0t = sb("w0t", [P, KH, CH])
    m.nbeta = sb("nbeta", [P, 1])
    m.later = sb("later", [P, P])
    m.earlier = sb("earlier", [P, P])
    m.wg = sb("wg", [P, KH, EXPERTS])
    m.bg = sb("bg", [P, EXPERTS])
    m.logits = sb("logits", [P, TILES, EXPERTS])
    return m


def prologue(nc, m, a):
    ctx = ExitStack()
    with ctx:
        def sb(name, shape, dt=FP32):
            return ctx.enter_context(nc.sbuf_tensor(name, shape, dt))

        def sem(name):
            return ctx.enter_context(nc.semaphore(name))

        wmod = [sb(f"wmod{l}", [P, KH, 6 * CH]) for l in range(2)]
        cT = sb("cT", [P, 2, KH, BATCH])
        ec = sb("ec", [P, 2, KH, BATCH])
        dc = sb("dc", [P, 2, KH, BATCH])
        rc = sb("rc", [P, 2, KH, BATCH])
        sc = sb("sc", [P, 2, KH, BATCH])
        cb = sb("cb", [P, 2, KH, P])
        big = sb("big", [P, 2, CH])
        sign = sb("sign", [P, 2, CH])
        wfr = sb("wfr", [P, KH, CH])
        wvr = sb("wvr", [P, KH, CH])
        w0r = sb("w0r", [P, KH, CH])
        down = sb("down", [DDIM, RANK])
        aux = sb("aux", [DDIM, CH])
        upT = sb("upT", [RANK, UDIM])
        uaT = sb("uaT", [UDIM, CH])
        d1 = sb("d1", [RANK, CH])
        r1 = sb("r1", [UDIM, CH])
        lnw = sb("lnw", [P, KH])
        lnb = sb("lnb", [P, KH])
        lnbb = sb("lnbb", [P, KH, P])
        wor = sb("wor", [P, KH, CH])
        eta = sb("eta", [P, 1])
        row = sb("row", [P, 1], I32)
        rows = sb("rows", [P, 1], I32)
        col = sb("col", [P, STEPS], I32)
        xor = sb("xor", [P, STEPS], I32)
        xorf = sb("xorf", [P, STEPS])
        colf = sb("colf", [P, STEPS])
        rowf = sb("rowf", [P, 1])
        prowf = sb("prowf", [P, 1])
        causal = sb("causal", [P, STEPS])
        lm = sb("lm", [P, len(LEVELS), STEPS])
        ones = sb("ones", [P, P])

        loaded = sem("loaded")
        loaded_mod = sem("loaded_mod")
        made = sem("made")
        v = sem("pro_dve")
        s_act = sem("pro_act")
        s_pe = sem("pro_pe")
        block = ctx.enter_context(nc.Block())
        count = {"w": 0}

        def halves(ap):
            return ap.rearrange("(k p) n -> p k n", p=P)

        def per_channel(ap):
            return ap.rearrange("(k p) -> p k", p=P)

        @block.sync
        def _(sp):
            def load(dst, src, s=loaded):
                sp.dma_start(dst, src).then_inc(s, 16)
                if s is loaded:
                    count["w"] += 16

            with nc.allow_non_contiguous_dma(reason="a few vectors and small weights, once"):
                for l, name in enumerate(("L0_c", "L1_c")):
                    for b in range(BATCH):
                        load(cT[:, l, :, b], per_channel(a[name][b, :]), loaded_mod)
                for l, name in enumerate(("L0_wmod", "L1_wmod")):
                    load(wmod[l][:, :, :], halves(a[name]), loaded_mod)
                for i, x in enumerate("xwkvr"):
                    load(m.maa[:, i, :], per_channel(a["L0_attn_time_maa_" + x]))
                load(m.decay[:, :], per_channel(a["L0_attn_time_decay"]))
                load(m.bonus[:, :], per_channel(a["L0_attn_time_faaaa"].rearrange("h i -> (h i)")))
                load(lnw[:, :], per_channel(a["L0_attn_ln_w"]))
                load(lnb[:, :], per_channel(a["L0_attn_ln_b"]))
                load(down[:, :], a["L0_ffn_lora_down"].rearrange("r d -> d r"))
                load(upT[:, :], a["L0_ffn_lora_up"].rearrange("u r -> r u"))
                load(uaT[:, :], a["L0_ffn_up_aux"].rearrange("o u -> u o"))
                load(aux[:, :], a["L0_ffn_down_aux"])
                load(m.w1[:, :, :], halves(a["L0_attn_time_maa_w1"]))
                load(m.dw1[:, :, :], halves(a["L0_attn_time_decay_w1"]))
                load(m.dw2[:, :], a["L0_attn_time_decay_w2"])
                for dst, name in ((m.wr, "W_r"), (m.wk, "W_k"), (m.wv, "W_v"), (wor, "W_o")):
                    load(dst[:, :, :], halves(a["L0_attn_" + name]))
                load(wfr[:, :, :], halves(a["L0_ffn_W"]))
                load(w0r[:, :, :], halves(a["L1_attn_W0"]))
                load(wvr[:, :, :], halves(a["L1_attn_Wkv"][CH:2 * CH, :]))
                load(m.wg[:, :, :], halves(a["L1_ffn_Wg"]))
                load(m.bf[:, :], a["L0_ffn_b"].partition_broadcast(P))
                load(m.bv[:, :], a["L1_attn_bkv"][CH:2 * CH].partition_broadcast(P))
                load(m.bg[:, :], a["L1_ffn_bg"].partition_broadcast(P))
                load(eta[:, :], a["L1_attn_eta"].partition_broadcast(P))
                sp.wait_ge(made, 1)
                for f in range(MIXES):
                    load(m.w2[f * MIX:(f + 1) * MIX, f, :], a["L0_attn_time_maa_w2"][f, :, :])

        all_loaded = count["w"]

        @block.gpsimd
        def _(pool):
            pool.memset(m.w2[:, :, :], 0.0).then_inc(made, 1)
            pool.memset(m.ident[:, :], 0.0)
            pool.memset(ones[:, :], 1.0)
            pool.memset(m.half[:, :], -0.5)
            pool.iota(row[:, :], pattern=[[0, 1]], base=0, channel_multiplier=1)
            pool.iota(col[:, :], pattern=[[1, STEPS]], base=0, channel_multiplier=0).then_inc(made, 1)
            pool.wait_ge(made, 2)
            pool.affine_select(out=m.ident[:, :], in_=m.ident[:, :], compare_op=ALU.not_equal, fill=1.0, base=0,
                               pattern=[[-1, P]], channel_multiplier=1).then_inc(made, 1)

        @block.scalar
        def _(act):
            act.wait_ge(loaded_mod, 16 * (2 * BATCH + 2))
            act.activation(ec[:, :, :, :], cT[:, :, :, :], ACT.Exp, scale=-1.0).then_inc(s_act, 1)

        def step_list(eng, s):
            state = [0]

            def then(ins):
                ins.then_inc(s, 1)
                state[0] += 1
                eng.wait_ge(s, state[0])
                return state[0]
            return then

        marks = {}

        @block.vector
        def _(dve):
            then = step_list(dve, v)
            dve.wait_ge(s_act, 1)
            then(dve.tensor_scalar_add(dc[:, :, :, :], ec[:, :, :, :], 1.0))
            then(dve.reciprocal(rc[:, :, :, :], dc[:, :, :, :]))
            then(dve.tensor_tensor(sc[:, :, :, :], cT[:, :, :, :], rc[:, :, :, :], ALU.mult))
            dve.wait_ge(made, 3)
            for l in range(2):
                for k in range(KH):
                    for b in range(BATCH):
                        n = then(dve.tensor_scalar(cb[:, l, k, b * STEPS:(b + 1) * STEPS], ones[:, 0:STEPS],
                                                   sc[:, l, k, b:b + 1], None, ALU.mult))
            marks["cb"] = n
            then(dve.tensor_single_scalar(rows[:, :], row[:, :], STEPS - 1, ALU.bitwise_and))
            then(dve.tensor_tensor(xor[:, :], col[:, :], rows[:, 0:1].to_broadcast([P, STEPS]), ALU.bitwise_xor))
            then(dve.tensor_copy(xorf[:, :], xor[:, :]))
            then(dve.tensor_copy(colf[:, :], col[:, :]))
            then(dve.tensor_copy(rowf[:, :], rows[:, :]))
            then(dve.tensor_copy(prowf[:, :], row[:, :]))
            then(dve.tensor_scalar(m.side[:, 0:1], prowf[:, :], float(STEPS), None, ALU.is_lt))
            then(dve.tensor_scalar(m.side[:, 1:2], prowf[:, :], float(STEPS), None, ALU.is_ge))
            then(dve.tensor_scalar(causal[:, :], colf[:, :], rowf[:, 0:1], None, ALU.is_gt))
            for n_, half in enumerate(LEVELS):
                then(dve.tensor_scalar(lm[:, n_, :], xorf[:, :], float(half), None, ALU.is_ge))
                then(dve.scalar_tensor_tensor(lm[:, n_, :], xorf[:, :], float(2 * half), lm[:, n_, :],
                                              ALU.is_lt, ALU.mult))
                then(dve.tensor_tensor(lm[:, n_, :], lm[:, n_, :], causal[:, :], ALU.mult))
                for q in range(2):
                    then(dve.tensor_copy(m.lmask[:, n_, q, :], lm[:, n_, :]))
            then(dve.tensor_tensor(lm[:, 5, :], lm[:, 5, :], lm[:, 4, :], ALU.add))
            for q in range(2):
                then(dve.tensor_copy(m.lmask[:, 5, q, :], lm[:, 5, :]))
            for q in range(2):
                then(dve.tensor_scalar(m.dmask[:, q, :], xorf[:, :], 0.0, None, ALU.is_equal))
            for b in range(BATCH):
                then(dve.tensor_scalar(m.later[:, b * STEPS:(b + 1) * STEPS], colf[:, :], rowf[:, 0:1], None,
                                       ALU.is_gt))
                then(dve.tensor_scalar(m.earlier[:, b * STEPS:(b + 1) * STEPS], colf[:, :], rowf[:, 0:1], None,
                                       ALU.is_lt))
            dve.wait_ge(loaded, all_loaded)
            then(dve.tensor_scalar(m.nbeta[:, :], eta[:, :], -2.0 / (BATCH * CH), None, ALU.mult))
            for k in range(KH):
                then(dve.tensor_scalar(m.wo[:, k, :], wor[:, k, :], lnw[:, k:k + 1], None, ALU.mult))
                n = then(dve.tensor_scalar(lnbb[:, k, :], ones[:, :], lnb[:, k:k + 1], None, ALU.mult))
            marks["lnbb"] = n
            for l in range(2):
                dve.wait_ge(s_pe, 3 * l + 3)
                for i in range(3):
                    n = then(dve.tensor_copy(m.mod[l][:, 2 * i:2 * i + 2, :].rearrange("p a c -> p (a c)"),
                                             m.bank[i][:, :]))
                marks[f"mod{l}"] = n
                for i in (1, 4):
                    then(dve.tensor_scalar_add(m.mod[l][:, i, :], m.mod[l][:, i, :], 1.0))
                g = m.mod[l][:, 2:6:3, :]
                then(dve.tensor_scalar(big[:, :, :], g, -1.0, None, ALU.mult))
                then(dve.tensor_tensor(big[:, :, :], big[:, :, :], g, ALU.max))
                then(dve.tensor_scalar(big[:, :, :], big[:, :, :], 0.25, None, ALU.max))
                then(dve.tensor_scalar(sign[:, :, :], g, 0.0, 2.0, ALU.is_ge, ALU.mult))
                then(dve.scalar_tensor_tensor(g, sign[:, :, :], -1.0, big[:, :, :], ALU.add, ALU.mult))
            then(dve.tensor_tensor(m.bf[:, :], m.bf[:, :], m.mod[0][:, 5, :], ALU.mult))
            dve.wait_ge(s_pe, 7)
            marks["d1"] = then(dve.tensor_copy(d1[:, :], m.bank[3][0:RANK, 0:CH]))
            dve.wait_ge(s_pe, 8)
            marks["r1"] = then(dve.tensor_copy(r1[:, :], m.bank[4][0:UDIM, 0:CH]))
            dve.wait_ge(s_pe, 9)
            then(dve.tensor_tensor(m.wob[:, :], m.bank[5][:, 0:CH], m.mod[0][:, 2, :], ALU.mult))
            for i, dst in enumerate((m.wf, m.wvt, m.w0t)):
                dve.wait_ge(s_pe, 10 + i)
                then(dve.tensor_copy(dst[:, :, :].rearrange("p k c -> p (k c)"), m.bank[(6, 7, 3)[i]][:, :]))

        @block.tensor
        def _(pe):
            pe.wait_ge(made, 3)
            pe.wait_ge(loaded_mod, 16 * (2 * BATCH + 2))
            pe.wait_ge(v, marks["cb"])
            for l in range(2):
                if l:
                    pe.wait_ge(v, marks["mod0"])
                for i in range(3):
                    for k in range(KH):
                        mm = pe.matmul(m.bank[i][:, :], cb[:, l, k, :], wmod[l][:, k, 512 * i:512 * i + 512],
                                       start=(k == 0), stop=(k == KH - 1))
                    mm.then_inc(s_pe, 1)
            pe.wait_ge(loaded, all_loaded)
            pe.matmul(m.bank[3][0:RANK, 0:CH], down[:, :], aux[:, :], start=True, stop=True).then_inc(s_pe, 1)
            pe.wait_ge(v, marks["d1"])
            pe.matmul(m.bank[4][0:UDIM, 0:CH], upT[:, :], d1[:, :], start=True, stop=True).then_inc(s_pe, 1)
            pe.wait_ge(v, marks["lnbb"])
            for k in range(KH):
                mm = pe.matmul(m.bank[5][:, 0:CH], lnbb[:, k, :], wor[:, k, :], start=(k == 0), stop=(k == KH - 1))
            mm.then_inc(s_pe, 1)
            pe.wait_ge(v, marks["r1"])
            for i, src in enumerate((wfr, wvr, w0r)):
                bank = m.bank[(6, 7, 3)[i]]
                for k in range(KH):
                    for o in range(KH):
                        out = bank[:, k * CH + o * P:k * CH + (o + 1) * P]
                        mm = pe.matmul(out, src[:, o, k * P:(k + 1) * P], m.ident[:, :], start=True, stop=(i > 0))
                        if i == 0:
                            mm = pe.matmul(out, r1[:, k * P:(k + 1) * P], uaT[:, o * P:(o + 1) * P],
                                           start=False, stop=True)
                mm.then_inc(s_pe, 1)


def time_mix(nc, m, a):
    ctx = ExitStack()
    with ctx:
        S = 4

        def sb(name, shape, dt=FP32):
            return ctx.enter_context(nc.sbuf_tensor(name, shape, dt))

        def slots(name, shape):
            return [sb(f"{name}{s}", shape) for s in range(S)]

        def sem(name):
            return ctx.enter_context(nc.semaphore(name))

        stats = sb("a_stats", [P, 6])
        mv = sb("a_mv", [P, 2])
        ve = sb("a_ve", [P, 1])
        rstd = sb("a_rstd", [P, 1])
        xm = sb("a_xm", [P, CH])
        h = sb("a_h", [P, CH])
        hT = slots("a_hT", [P, KH, BATCH, STEPS + 1])
        xx = slots("a_xx", [P, KH, BATCH, STEPS])
        xxx = sb("a_xxx", [P, KH, P])
        mt = slots("a_mt", [P, P])
        xf = sb("a_xf", [P, MIXES, KH, P])
        dt_ = sb("a_dt", [DECAY_RANK, P])
        ew = sb("a_ew", [P, KH, P])
        rp = slots("a_rp", [P, KH, P])
        kq = slots("a_kq", [P, KH, P])
        ru = slots("a_ru", [P, KH, P])
        vt = slots("a_vt", [P, CH])
        tots = [[sb(f"a_tot{i}_{s}", [P, KH * P >> i]) for i in range(len(LEVELS) + 1)] for s in range(S)]
        att = slots("a_att", [P, KH, 2, STEPS])
        blk = sb("a_blk", [P, HEADS, P])
        kt = sb("a_kt", [P, BATCH, CH])
        state = sb("a_state", [P, BATCH * KH, HEAD])
        sdec = sb("a_sdec", [P, BATCH * KH, HEAD])
        sblk = sb("a_sblk", [P, BATCH * KH, P])

        x_loaded = [sem(f"a_x_loaded{s}") for s in range(S)]
        ready = sem("a_ready")
        passed = {e: sem(f"a_passed_{e}") for e in ("dve", "pool", "pe", "act")}
        ND = Steps(sem("norm_dve"), "stats mv ve xm h xx xxx")
        NP = Steps(sem("norm_pool"), "rstd")
        NA = Steps(sem("norm_act"), "carry hT mt")
        NE = Steps(sem("norm_pe"), "hT m")
        FD = Steps(sem("mix_dve"), "xf0 xf1 xf2 xf3")
        FP = Steps(sem("mix_pool"), "add0 add1 add3 add2")
        FA = Steps(sem("mix_act"), "dt r k ru0 ru1 ew0 ew1 w v")
        FE = Steps(sem("mix_pe"), "x0 x1 x2 x3 d r k w v")
        LD = [Steps(sem("low_dve"), "rp0 tot0 diag0 diag1 cp0a cp0b rp1 tot1 cp1a cp1b rp2 tot2 cp2a cp2b"),
              Steps(sem("high_dve"), "rp3 tot3 cp3a cp3b rp4 tot4 rp5 tot5 cp5a cp5b")]
        LP = [Steps(sem("low_pool"), "kq0 kq1 kq2"), Steps(sem("high_pool"), "kq3 kq4 kq5")]
        LE = [Steps(sem("low_pe"), "l0 l1 l2"), Steps(sem("high_pe"), "l3 l4 l5")]
        YD = Steps(sem("out_dve"), "sdec state")
        YA = Steps(sem("out_act"), "blk0 blk1 kt0 kt1 sblk0 sblk1 y")
        YE = Steps(sem("out_pe"), "kT kv y")
        block = ctx.enter_context(nc.Block())

        hbank, xbank, ybank, kvbank = m.bank[0], m.bank[1], m.bank[6], m.bank[7]
        lbank = [(m.bank[2], m.bank[3]), (m.bank[4], m.bank[5])]

        def at(stream, t):
            return stream[:, bass.ds(t, 1), :].rearrange("p a c -> p (a c)")

        def by_head(bank, base=0):
            return bank[:, base:base + P].rearrange("p (k s) -> p k s", k=KH)

        @block.sync
        def _(sp):
            def load(t, slot, turn):
                yield 0
                if begun(t, S):
                    sp.wait_ge(x_loaded[slot], turn * 32)
                for b in range(BATCH):
                    sp.dma_start(at(m.x, t)[b * STEPS:(b + 1) * STEPS, :],
                                 a["L0_attn_query"][b, bass.ds(t * STEPS, STEPS), :]).then_inc(x_loaded[slot], 16)

            run_pipeline(sp, [(load, 0)], TILES, S)

        @block.gpsimd
        def _(pool):
            pool.memset(hT[S - 1][:, :, :, :], 0.0)
            pool.memset(kt[:, :, :], 0.0)
            pool.memset(state[:, :, :], 0.0).then_inc(ready, 1)
            pool.wait_ge(ready, 1)

            def norm(t, slot, turn):
                yield 1
                pool.wait_ge(*ND("ve", t))
                pool.tensor_tensor(rstd[:, :], ve[:, :], m.half[:, 0:1], ALU.pow).then_inc(NP["rstd"], 1)

            def mix(t, slot, turn):
                for step, f in ((1, 0), (1, 1), (4, 3), (4, 2)):
                    yield step
                    pool.wait_ge(*FD(f"xf{f}", t))
                    pool.tensor_tensor(xf[:, f, :, :].rearrange("p k (b s) -> p k b s", b=BATCH),
                                       xf[:, f, :, :].rearrange("p k (b s) -> p k b s", b=BATCH),
                                       hT[slot][:, :, :, 1:STEPS + 1], ALU.add).then_inc(FP[f"add{f}"], 1)

            def levels(c):
                def chain(t, slot, turn):
                    for j, step in enumerate((1, 4, 9)):
                        i = 3 * c + j
                        half = LEVELS[i]
                        yield step
                        pool.wait_ge(*LE[c](f"l{i}", t))
                        if i:
                            pool.wait_ge(*LD[(i - 1) // 3](f"tot{i - 1}", t))
                        n = KH * P // (2 * half)
                        view = kq[slot][:, :, :].rearrange("p k (n two s) -> p (k n) two s", two=2, s=half)[:, :, 0, :]
                        dec = tots[slot][i][:, :].rearrange("p (n two) -> p n two", two=2)[:, :, 1:2]
                        pool.tensor_tensor(view, view, dec.to_broadcast([P, n, half]), ALU.mult)\
                            .then_inc(LP[c][f"kq{i}"], 1)
                return chain

            run_pipeline(pool, [(levels(1), 3), (levels(0), 2), (mix, 1), (norm, 0)], TILES, S)

        @block.vector
        def _(dve):
            def norm(t, slot, turn):
                x = at(m.x, t)
                yield 0
                dve.wait_ge(x_loaded[slot], turn * 32 + 32)
                dve.sem_inc(passed["dve"], 1)
                dve.bn_stats(stats[:, :], x).then_inc(ND["stats"], 1)
                dve.wait_ge(*ND("stats", t))
                dve.sem_inc(passed["dve"], 1)
                dve.bn_aggr(mv[:, :], stats[:, :]).then_inc(ND["mv"], 1)
                dve.wait_ge(*ND("mv", t))
                dve.tensor_scalar_add(ve[:, :], mv[:, 1:2], LN_EPS).then_inc(ND["ve"], 1)
                dve.scalar_tensor_tensor(xm[:, :], x, mv[:, 0:1], m.mod[0][:, 1, :], ALU.subtract, ALU.mult)\
                   .then_inc(ND["xm"], 1)
                yield 2
                dve.wait_ge(*NP("rstd", t))
                dve.wait_ge(*ND("xm", t))
                dve.scalar_tensor_tensor(h[:, :], xm[:, :], rstd[:, 0:1], m.mod[0][:, 0, :], ALU.mult, ALU.add)\
                   .then_inc(ND["h"], 1)
                yield 6
                dve.wait_ge(*NA("hT", t))
                dve.tensor_tensor(xx[slot][:, :, :, :], hT[slot][:, :, :, 0:STEPS], hT[slot][:, :, :, 1:STEPS + 1],
                                  ALU.subtract).then_inc(ND["xx"], 1)
                dve.wait_ge(*ND("xx", t))
                for k in range(KH):
                    last = dve.scalar_tensor_tensor(
                        xxx[:, k, :].rearrange("p (b s) -> p b s", b=BATCH), xx[slot][:, k, :, :],
                        m.maa[:, 0, k:k + 1], hT[slot][:, k, :, 1:STEPS + 1], ALU.mult, ALU.add)
                last.then_inc(ND["xxx"], 1)

            def mix(t, slot, turn):
                for f in range(MIXES):
                    if f % 2 == 0:
                        yield (1, 4)[f // 2]
                        dve.wait_ge(*FE(f"x{f + 1}", t))
                    for k in range(KH):
                        last = dve.scalar_tensor_tensor(
                            xf[:, f, k, :], xbank[:, (f % 2) * CH + k * P:(f % 2) * CH + (k + 1) * P],
                            m.maa[:, 1 + f, k:k + 1], xx[slot][:, k, :, :].rearrange("p b s -> p (b s)"),
                            ALU.add, ALU.mult)
                    last.then_inc(FD[f"xf{f}"], 1)

            def levels(c):
                def chain(t, slot, turn):
                    for j, step in enumerate((1, 4, 9)):
                        i = 3 * c + j
                        half = LEVELS[i]
                        yield step
                        dve.wait_ge(*LE[c](f"l{i}", t))
                        if i:
                            dve.wait_ge(*LD[(i - 1) // 3](f"tot{i - 1}", t))
                        n = KH * P // (2 * half)
                        src = tots[slot][i][:, :].rearrange("p (n two) -> p n two", two=2)
                        view = rp[slot][:, :, :].rearrange("p k (n two s) -> p (k n) two s", two=2, s=half)[:, :, 1, :]
                        dve.tensor_tensor(view, view, src[:, :, 0:1].to_broadcast([P, n, half]), ALU.mult)\
                           .then_inc(LD[c][f"rp{i}"], 1)
                        dve.tensor_tensor(tots[slot][i + 1][:, :].rearrange("p (n one) -> p n one", one=1),
                                          src[:, :, 0:1], src[:, :, 1:2], ALU.mult).then_inc(LD[c][f"tot{i}"], 1)
                        if i == 0:
                            for q in range(2):
                                dve.tensor_tensor(att[slot][:, :, q, :], by_head(lbank[0][q], P), m.dmask[:, :, :],
                                                  ALU.mult).then_inc(LD[c][f"diag{q}"], 1)
                            dve.wait_ge(*LD[c]("diag1", t))
                            dve.sem_inc(passed["dve"], 1)
                        if i != 4:
                            for q in range(2):
                                dve.copy_predicated(att[slot][:, :, q, :], m.lmask[:, i, :, :], by_head(lbank[c][q]))\
                                   .then_inc(LD[c][f"cp{i}{'ab'[q]}"], 1)
                return chain

            def output(t, slot, turn):
                yield 0
                dve.wait_ge(*LD[1]("tot5", t))
                if begun(t, 1):
                    dve.wait_ge(*YD("state", t - 1))
                dve.tensor_tensor(sdec[:, :, :], state[:, :, :],
                                  tots[slot][6][:, :].rearrange("p (n one) -> p n one", one=1)
                                  .to_broadcast([P, KH * BATCH, HEAD]), ALU.mult).then_inc(YD["sdec"], 1)
                yield 6
                dve.wait_ge(*YE("kv", t))
                dve.wait_ge(*YD("sdec", t))
                dve.wait_ge(*YA("sblk1", t))
                dve.tensor_tensor(state[:, :, :], sdec[:, :, :],
                                  kvbank[:, CH:2 * CH].rearrange("p (n j) -> p n j", j=HEAD), ALU.add)\
                   .then_inc(YD["state"], 1)

            dve.wait_ge(ready, 1)
            run_pipeline(dve, [(output, 4), (levels(1), 3), (levels(0), 2), (mix, 1), (norm, 0)], TILES, S)

        @block.scalar
        def _(act):
            def norm(t, slot, turn):
                yield 5
                act.activation(hT[slot][:, :, :, 0:1], hT[slot - 1][:, :, :, STEPS:STEPS + 1], ACT.Copy)\
                   .then_inc(NA["carry"], 1)
                act.wait_ge(*NE("hT", t))
                act.activation(hT[slot][:, :, :, 1:STEPS + 1],
                               hbank[:, 0:CH].rearrange("p (k b s) -> p k b s", k=KH, b=BATCH), ACT.Copy)\
                   .then_inc(NA["hT"], 1)
                yield 10
                act.wait_ge(*NE("m", t))
                act.activation(mt[slot][:, :], hbank[:, CH:CH + P], ACT.Tanh).then_inc(NA["mt"], 1)

            def mix(t, slot, turn):
                yield 4
                act.wait_ge(*FE("d", t))
                act.activation(dt_[:, :], hbank[0:DECAY_RANK, CH + P:CH + 2 * P], ACT.Tanh).then_inc(FA["dt"], 1)
                yield 7
                act.wait_ge(*FE("k", t))
                act.activation(rp[slot][:, :, :], xbank[:, 0:CH].rearrange("p (k s) -> p k s", k=KH), ACT.Copy)\
                   .then_inc(FA["r"], 1)
                act.activation(kq[slot][:, :, :], xbank[:, CH:2 * CH].rearrange("p (k s) -> p k s", k=KH), ACT.Copy)\
                   .then_inc(FA["k"], 1)
                act.wait_ge(*FA("r", t))
                for k in range(KH):
                    act.activation(ru[slot][:, k, :], rp[slot][:, k, :], ACT.Copy, scale=m.bonus[:, k:k + 1])\
                       .then_inc(FA[f"ru{k}"], 1)
                act.wait_ge(*FE("w", t))
                for k in range(KH):
                    act.activation(ew[:, k, :], hbank[:, k * P:(k + 1) * P], ACT.Exp, bias=m.decay[:, k:k + 1])\
                       .then_inc(FA[f"ew{k}"], 1)
                act.wait_ge(*FA("ew1", t))
                act.activation(tots[slot][0][:, :], ew[:, :, :].rearrange("p k s -> p (k s)"), ACT.Exp, scale=-1.0)\
                   .then_inc(FA["w"], 1)
                yield 9
                act.wait_ge(*FE("v", t))
                act.activation(vt[slot][:, :], xbank[:, 0:CH], ACT.Copy).then_inc(FA["v"], 1)

            def output(t, slot, turn):
                yield 0
                act.wait_ge(*LD[1]("cp5b", t))
                for b in range(BATCH):
                    act.activation(blk[:, :, b * STEPS:(b + 1) * STEPS],
                                   att[slot][:, :, :, :].rearrange("p k q s -> p (k q) s"), ACT.Copy,
                                   scale=m.side[:, b:b + 1]).then_inc(YA[f"blk{b}"], 1)
                yield 1
                act.wait_ge(*YE("kT", t))
                for b in range(BATCH):
                    rows = slice(b * STEPS, (b + 1) * STEPS)
                    act.activation(kt[rows, b, :], kvbank[rows, 0:CH], ACT.Copy).then_inc(YA[f"kt{b}"], 1)
                yield 2
                if begun(t, 1):
                    act.wait_ge(*YD("state", t - 1))
                for q in range(2):
                    act.activation(sblk[:, :, q * HEAD:(q + 1) * HEAD], state[:, :, :], ACT.Copy,
                                   scale=m.side[:, q:q + 1]).then_inc(YA[f"sblk{q}"], 1)
                yield 6
                act.wait_ge(*YE("y", t))
                act.activation(at(m.y, t), ybank[:, 0:CH], ACT.Copy).then_inc(YA["y"], 1)

            act.wait_ge(ready, 1)
            run_pipeline(act, [(output, 4), (mix, 1), (norm, 0)], TILES, S)

        @block.tensor
        def _(pe):
            def norm(t, slot, turn):
                yield 5
                pe.wait_ge(*ND("h", t))
                if begun(t, 1):
                    pe.wait_ge(*FA("dt", t - 1))
                for k in range(KH):
                    last = pe.transpose(hbank[:, k * P:(k + 1) * P], h[:, k * P:(k + 1) * P], m.ident[:, :])
                last.then_inc(NE["hT"], 1)
                yield 10
                pe.wait_ge(*ND("xxx", t))
                if begun(t, 1):
                    pe.wait_ge(*FA("ew1", t - 1))
                for k in range(KH):
                    last = pe.matmul(hbank[:, CH:CH + P], m.w1[:, k, :], xxx[:, k, :], start=(k == 0),
                                     stop=(k == KH - 1))
                last.then_inc(NE["m"], 1)

            def mix(t, slot, turn):
                yield 0
                pe.wait_ge(*NA("mt", t))
                if begun(t, 1):
                    pe.wait_ge(*FA("v", t - 1))
                for f in range(MIXES):
                    if f == 2:
                        yield 3
                        pe.wait_ge(*FD("xf1", t))
                    for k in range(KH):
                        last = pe.matmul(xbank[:, (f % 2) * CH + k * P:(f % 2) * CH + (k + 1) * P],
                                         m.w2[:, f, k * P:(k + 1) * P], mt[slot][:, :], start=True, stop=True)
                    last.then_inc(FE[f"x{f}"], 1)
                pe.wait_ge(*FP("add0", t))
                if begun(t, 1):
                    pe.wait_ge(*NA("mt", t))
                for k in range(KH):
                    last = pe.matmul(hbank[0:DECAY_RANK, CH + P:CH + 2 * P], m.dw1[:, k, :], xf[:, 0, k, :],
                                     start=(k == 0), stop=(k == KH - 1))
                last.then_inc(FE["d"], 1)
                yield 7
                for name, f, w, base in (("r", 3, m.wr, 0), ("k", 1, m.wk, CH)):
                    pe.wait_ge(*FP(f"add{f}", t))
                    for o in range(KH):
                        for k in range(KH):
                            last = pe.matmul(xbank[:, base + o * P:base + (o + 1) * P],
                                             w[:, k, o * P:(o + 1) * P], xf[:, f, k, :], start=(k == 0),
                                             stop=(k == KH - 1))
                    last.then_inc(FE[name], 1)
                pe.wait_ge(*FA("dt", t))
                if followed(t):
                    pe.wait_ge(*NA("hT", t + 1))
                for k in range(KH):
                    last = pe.matmul(hbank[:, k * P:(k + 1) * P], m.dw2[:, k * P:(k + 1) * P], dt_[:, :],
                                     start=True, stop=True)
                last.then_inc(FE["w"], 1)
                yield 9
                pe.wait_ge(*FP("add2", t))
                pe.wait_ge(*FA("k", t))
                for k in range(KH):
                    last = pe.matmul(xbank[:, 0:CH], xf[:, 2, k, :], m.wv[:, k, :], start=(k == 0),
                                     stop=(k == KH - 1))
                last.then_inc(FE["v"], 1)

            def products(out, keys, queries, base=0, half=STEPS):
                for k in range(KH):
                    for b in range(BATCH):
                        keyed = slice(b * STEPS, b * STEPS + half)
                        asked = slice((b + 1) * STEPS - half, (b + 1) * STEPS)
                        for q in range(2):
                            ch = slice(q * HEAD, (q + 1) * HEAD)
                            last = pe.matmul(out[q][keyed, base + (k + 1) * STEPS - half:base + (k + 1) * STEPS],
                                             keys[ch, k, keyed], queries[ch, k, asked], start=True, stop=True)
                return last

            def levels(c):
                def chain(t, slot, turn):
                    for j, step in enumerate((0, 3, 8)):
                        i = 3 * c + j
                        yield step
                        if i == 0:
                            pe.wait_ge(*FA("v", t))
                        elif j:
                            pe.wait_ge(*LD[c](f"rp{i - 1}", t))
                            pe.wait_ge(*LP[c](f"kq{i - 1}", t))
                            if i < 5:
                                pe.wait_ge(*LD[c](f"cp{i - 1}b", t))
                        else:
                            pe.wait_ge(*LD[0]("cp2b", t))
                            pe.wait_ge(*LP[0]("kq2", t))
                        if j == 0 and begun(t, 1):
                            pe.wait_ge(*LD[c](("cp2b", "cp5b")[c], t - 1))
                        pe.sem_inc(passed["pe"], 1)
                        if i == 0:
                            products(lbank[0], kq[slot], ru[slot], P)
                        products(lbank[c], kq[slot], rp[slot], 0, LEVELS[5] if i == 5 else STEPS)\
                            .then_inc(LE[c][f"l{i}"], 1)
                return chain

            def output(t, slot, turn):
                yield 1
                pe.wait_ge(*LP[1]("kq5", t))
                if begun(t, 1):
                    pe.wait_ge(*YD("state", t - 1))
                for k in range(KH):
                    last = pe.transpose(kvbank[:, k * P:(k + 1) * P], kq[slot][:, k, :], m.ident[:, :])
                last.then_inc(YE["kT"], 1)
                yield 4
                pe.wait_ge(*YA("kt1", t))
                for k in range(KH):
                    for b in range(BATCH):
                        for q in range(2):
                            ch = slice(k * P + q * HEAD, k * P + (q + 1) * HEAD)
                            n = k * BATCH + b
                            last = pe.matmul(kvbank[q * HEAD:(q + 1) * HEAD, CH + n * HEAD:CH + (n + 1) * HEAD],
                                             kt[:, b, ch], vt[slot][:, ch], start=True, stop=True)
                last.then_inc(YE["kv"], 1)
                pe.wait_ge(*YA("sblk1", t))
                pe.wait_ge(*LD[1]("rp5", t))
                if begun(t, 1):
                    pe.wait_ge(*YA("y", t - 1))
                for hd in range(HEADS):
                    pe.matmul(ybank[:, hd * HEAD:(hd + 1) * HEAD], blk[:, hd, :],
                              vt[slot][:, hd * HEAD:(hd + 1) * HEAD], start=(hd == 0), stop=False,
                              skip_group_check=True)
                for k in range(KH):
                    for b in range(BATCH):
                        tok = slice(b * STEPS, (b + 1) * STEPS)
                        last = pe.matmul(ybank[tok, k * P:(k + 1) * P], rp[slot][:, k, tok], sblk[:, k * BATCH + b, :],
                                         start=False, stop=True, skip_group_check=True)
                last.then_inc(YE["y"], 1)

            run_pipeline(pe, [(output, 4), (levels(1), 3), (levels(0), 2), (mix, 1), (norm, 0)], TILES, S)


def ffn_and_training(nc, m, a):
    ctx = ExitStack()
    with ctx:
        def sb(name, shape, dt=FP32):
            return ctx.enter_context(nc.sbuf_tensor(name, shape, dt))

        def sem(name):
            return ctx.enter_context(nc.semaphore(name))

        S = 4

        def slots(name, shape):
            return [sb(f"{name}_{s}", shape) for s in range(S)]

        s1 = sb("b_s1", [P, HEADS])
        yc = sb("b_yc", [P, CH])
        sq = sb("b_sq", [P, CH])
        s2 = sb("b_s2", [P, HEADS])
        vh = sb("b_vh", [P, HEADS])
        rh = sb("b_rh", [P, HEADS])
        yn = sb("b_yn", [P, CH])
        ynT = sb("b_ynT", [P, KH, P])
        xb = sb("b_xb", [P, CH])
        t1 = sb("b_t1", [P, CH])
        x1 = slots("b_x1", [P, CH])
        x1b = sb("b_x1b", [P, CH])
        h2 = sb("b_h2", [P, CH])
        h2T = sb("b_h2T", [P, KH, P])
        t2 = sb("b_t2", [P, CH])
        x2 = slots("b_x2", [P, CH])
        h3 = slots("b_h3", [P, CH])
        h3T = slots("b_h3T", [P, KH, P])
        v3 = slots("b_v3", [P, CH])
        x3 = slots("b_x3", [P, CH])
        h4 = sb("b_h4", [P, CH])
        h4T = sb("b_h4T", [P, KH, P])
        stats = [sb(f"b_stats{i}", [P, 6]) for i in range(3)]
        mv = [sb(f"b_mv{i}", [P, 2]) for i in range(3)]
        ve = [sb(f"b_ve{i}", [P, 1]) for i in range(3)]
        rstd = [sb(f"b_rstd{i}", [P, 1]) for i in range(3)]
        xm = [sb(f"b_xm{i}", [P, CH]) for i in range(3)]
        p0 = sb("b_p0", [P, 2, P])
        pw = [sb(f"b_pw{s}", [P, 2, P]) for s in range(2)]
        inv = slots("b_inv", [P, P])
        diff = sb("b_diff", [P, CH])
        es = sb("b_es", [P, CH])
        yl = sb("b_yl", [P, CH])
        t3 = sb("b_t3", [P, CH])
        wt = m.w0t

        passed = {e: sem(f"b_passed_{e}") for e in ("dve", "pool", "act")}
        HD = Steps(sem("heads_dve"), "s1 yc s2 vh yn t1 x1")
        HP = Steps(sem("heads_pool"), "sq xb rh")
        HA = Steps(sem("heads_act"), "ynT")
        HE = Steps(sem("heads_pe"), "ynT z")
        FD = Steps(sem("ffn_dve"), "stats mv ve xm h t2 x2")
        FP = Steps(sem("ffn_pool"), "x1b rstd")
        FA = Steps(sem("ffn_act"), "h2T")
        FE = Steps(sem("ffn_pe"), "h2T f")
        VD = Steps(sem("value_dve"), "stats mv ve xm h v")
        VP = Steps(sem("value_pool"), "rstd")
        VA = Steps(sem("value_act"), "h3T")
        VE = Steps(sem("value_pe"), "h3T v")
        MD = Steps(sem("inverse_dve"), "p pT t0 " + " ".join(f"t{j}" for j in range(1, 6)))
        MA = Steps(sem("inverse_act"), " ".join(f"pw{j}" for j in range(1, 6)))
        ME = Steps(sem("inverse_pe"), "g sq1 " + " ".join(f"sq{j + 1} up{j}" for j in range(1, 5)) + " up5")
        BD = Steps(sem("train_dve"), "diff es yl")
        BP = Steps(sem("train_pool"), "t3 x3")
        BA = Steps(sem("train_act"), "w")
        BE = Steps(sem("train_pe"), "xw err dw")
        RD = Steps(sem("route_dve"), "stats mv ve xm h logits")
        RP = Steps(sem("route_pool"), "rstd")
        RA = Steps(sem("route_act"), "h4T keep x3")
        RE = Steps(sem("route_pe"), "h4T logits")
        block = ctx.enter_context(nc.Block())
        hbank, fbank, vbank, sqbank, upbank, ebank, wbank, rbank = m.bank
        CHAINS = dict(heads=0, ffn=1, value=2, gram=2, inverse=3, train=4, route=5)

        def at(stream, t):
            return stream[:, bass.ds(t, 1), :].rearrange("p a c -> p (a c)")

        def heads_of(ap):
            return ap.rearrange("p (h i) -> p h i", h=HEADS)

        def spread(ap, n):
            return ap.rearrange("p (h one) -> p h one", one=1).to_broadcast([P, ap.shape[1], n])

        def in_order(*parts):
            return sorted(((f, CHAINS[f.__name__]) for f in parts), key=lambda c: -c[1])

        @block.gpsimd
        def _(pool):
            def heads(t, slot, turn):
                yield 1
                pool.wait_ge(*HD("yc", t))
                pool.tensor_tensor(sq[:, :], yc[:, :], yc[:, :], ALU.mult).then_inc(HP["sq"], 1)
                pool.tensor_tensor(xb[:, :], at(m.x, t), m.wob[:, :], ALU.add).then_inc(HP["xb"], 1)
                yield 4
                pool.wait_ge(*HD("vh", t))
                pool.tensor_tensor(rh[:, :], vh[:, :], m.half[:, :], ALU.pow).then_inc(HP["rh"], 1)

            def ffn(t, slot, turn):
                yield 0
                pool.wait_ge(*HD("x1", t))
                if begun(t, 1):
                    pool.wait_ge(*FD("x2", t - 1))
                pool.tensor_tensor(x1b[:, :], x1[slot][:, :], m.bf[:, :], ALU.add).then_inc(FP["x1b"], 1)
                yield 3
                pool.wait_ge(*FD("ve", t))
                pool.tensor_tensor(rstd[0][:, :], ve[0][:, :], m.half[:, 0:1], ALU.pow).then_inc(FP["rstd"], 1)

            def value(t, slot, turn):
                yield 5
                pool.wait_ge(*VD("ve", t))
                pool.tensor_tensor(rstd[1][:, :], ve[1][:, :], m.half[:, 0:1], ALU.pow).then_inc(VP["rstd"], 1)

            def train(t, slot, turn):
                yield 6
                pool.wait_ge(*BD("yl", t))
                pool.tensor_tensor(t3[:, :], yl[:, :], m.mod[1][:, 2, :], ALU.mult).then_inc(BP["t3"], 1)
                pool.wait_ge(*BP("t3", t))
                pool.tensor_tensor(x3[slot][:, :], t3[:, :], x2[slot][:, :], ALU.add).then_inc(BP["x3"], 1)

            def route(t, slot, turn):
                yield 2
                pool.wait_ge(*RD("ve", t))
                pool.tensor_tensor(rstd[2][:, :], ve[2][:, :], m.half[:, 0:1], ALU.pow).then_inc(RP["rstd"], 1)

            run_pipeline(pool, in_order(heads, ffn, value, train, route), TILES, S)

        @block.vector
        def _(dve):
            def heads(t, slot, turn):
                y = at(m.y, t)
                yield 1
                dve.tensor_reduce(s1[:, :], heads_of(y), AX.X, ALU.add).then_inc(HD["s1"], 1)
                dve.wait_ge(*HD("s1", t))
                dve.sem_inc(passed["dve"], 1)
                dve.scalar_tensor_tensor(heads_of(yc[:, :]), spread(s1[:, :], HEAD), -1.0 / HEAD, heads_of(y), ALU.mult,
                                         ALU.add).then_inc(HD["yc"], 1)
                yield 3
                dve.wait_ge(*HP("sq", t))
                dve.tensor_reduce(s2[:, :], heads_of(sq[:, :]), AX.X, ALU.add).then_inc(HD["s2"], 1)
                dve.wait_ge(*HD("s2", t))
                dve.tensor_scalar(vh[:, :], s2[:, :], 1.0 / HEAD, HEAD_EPS, ALU.mult, ALU.add).then_inc(HD["vh"], 1)
                yield 9
                dve.wait_ge(*HP("rh", t))
                dve.tensor_tensor(heads_of(yn[:, :]), heads_of(yc[:, :]), spread(rh[:, :], HEAD), ALU.mult)\
                   .then_inc(HD["yn"], 1)
                yield 18
                dve.wait_ge(*HE("z", t))
                dve.tensor_tensor(t1[:, :], hbank[:, CH:2 * CH], m.mod[0][:, 2, :], ALU.mult).then_inc(HD["t1"], 1)
                dve.wait_ge(*HD("t1", t))
                dve.wait_ge(*HP("xb", t))
                dve.tensor_tensor(x1[slot][:, :], t1[:, :], xb[:, :], ALU.add).then_inc(HD["x1"], 1)

            def norm(steps, i, x, scale, t):
                dve.bn_stats(stats[i][:, :], x).then_inc(steps["stats"], 1)
                dve.wait_ge(*steps("stats", t))
                dve.sem_inc(passed["dve"], 1)
                dve.bn_aggr(mv[i][:, :], stats[i][:, :]).then_inc(steps["mv"], 1)
                dve.wait_ge(*steps("mv", t))
                dve.tensor_scalar_add(ve[i][:, :], mv[i][:, 1:2], LN_EPS).then_inc(steps["ve"], 1)
                dve.scalar_tensor_tensor(xm[i][:, :], x, mv[i][:, 0:1], scale, ALU.subtract, ALU.mult)\
                   .then_inc(steps["xm"], 1)

            def ffn(t, slot, turn):
                yield 5
                dve.wait_ge(*HD("x1", t))
                norm(FD, 0, x1[slot][:, :], m.mod[0][:, 4, :], t)
                yield 8
                dve.wait_ge(*FP("rstd", t))
                dve.wait_ge(*FD("xm", t))
                dve.scalar_tensor_tensor(h2[:, :], xm[0][:, :], rstd[0][:, 0:1], m.mod[0][:, 3, :], ALU.mult, ALU.add)\
                   .then_inc(FD["h"], 1)
                yield 14
                dve.wait_ge(*FE("f", t))
                dve.tensor_tensor(t2[:, :], fbank[:, CH:2 * CH], m.mod[0][:, 5, :], ALU.mult).then_inc(FD["t2"], 1)
                dve.wait_ge(*FD("t2", t))
                dve.wait_ge(*FP("x1b", t))
                dve.tensor_tensor(x2[slot][:, :], t2[:, :], x1b[:, :], ALU.add).then_inc(FD["x2"], 1)

            def value(t, slot, turn):
                yield 10
                dve.wait_ge(*FD("x2", t))
                norm(VD, 1, x2[slot][:, :], m.mod[1][:, 1, :], t)
                yield 13
                dve.wait_ge(*VP("rstd", t))
                dve.wait_ge(*VD("xm", t))
                dve.scalar_tensor_tensor(h3[slot][:, :], xm[1][:, :], rstd[1][:, 0:1], m.mod[1][:, 0, :], ALU.mult,
                                         ALU.add).then_inc(VD["h"], 1)
                yield 20
                dve.wait_ge(*VE("v", t))
                dve.tensor_tensor(v3[slot][:, :], vbank[:, CH:2 * CH], m.bv[:, :], ALU.add).then_inc(VD["v"], 1)

            def inverse(t, slot, turn):
                yield 0
                dve.wait_ge(*ME("g", t))
                dve.scalar_tensor_tensor(p0[:, 0, :], sqbank[:, 0:P], m.nbeta[:, 0:1], m.earlier[:, :], ALU.mult,
                                         ALU.mult).then_inc(MD["p"], 1)
                dve.scalar_tensor_tensor(p0[:, 1, :], sqbank[:, 0:P], m.nbeta[:, 0:1], m.later[:, :], ALU.mult,
                                         ALU.mult).then_inc(MD["pT"], 1)
                dve.wait_ge(*MD("pT", t))
                dve.tensor_tensor(inv[slot][:, :], p0[:, 1, :], m.ident[:, :], ALU.add).then_inc(MD["t0"], 1)
                for j in range(1, 6):
                    yield (4, 7, 12, 15, 17)[j - 1]
                    dve.wait_ge(*ME(f"up{j}", t))
                    dve.tensor_tensor(inv[slot][:, :], upbank[:, 0:P], inv[slot][:, :], ALU.add)\
                       .then_inc(MD[f"t{j}"], 1)

            def train(t, slot, turn):
                yield 6
                dve.wait_ge(*BE("xw", t))
                dve.tensor_tensor(diff[:, :], ebank[:, 0:CH], v3[slot][:, :], ALU.subtract).then_inc(BD["diff"], 1)
                yield 16
                dve.wait_ge(*BE("err", t))
                dve.tensor_scalar(es[:, :], ebank[:, CH:2 * CH], m.nbeta[:, 0:1], None, ALU.mult)\
                   .then_inc(BD["es"], 1)
                dve.tensor_tensor(yl[:, :], ebank[:, CH:2 * CH], v3[slot][:, :], ALU.add).then_inc(BD["yl"], 1)

            def route(t, slot, turn):
                yield 2
                dve.wait_ge(*BP("x3", t))
                norm(RD, 2, x3[slot][:, :], m.mod[1][:, 4, :], t)
                yield 11
                dve.wait_ge(*RP("rstd", t))
                dve.wait_ge(*RD("xm", t))
                dve.scalar_tensor_tensor(h4[:, :], xm[2][:, :], rstd[2][:, 0:1], m.mod[1][:, 3, :], ALU.mult, ALU.add)\
                   .then_inc(RD["h"], 1)
                yield 19
                dve.wait_ge(*RE("logits", t))
                dve.sem_inc(passed["dve"], 1)
                dve.tensor_tensor(at(m.logits, t), rbank[:, CH:CH + EXPERTS], m.bg[:, :], ALU.add)\
                   .then_inc(RD["logits"], 1)

            run_pipeline(dve, in_order(heads, ffn, value, inverse, train, route), TILES, S)

        @block.scalar
        def _(act):
            def halves(bank):
                return bank[:, 0:CH].rearrange("p (k s) -> p k s", k=KH)

            def heads(t, slot, turn):
                yield 4
                act.wait_ge(*HE("ynT", t))
                act.activation(ynT[:, :, :], halves(hbank), ACT.Copy).then_inc(HA["ynT"], 1)

            def ffn(t, slot, turn):
                yield 3
                act.wait_ge(*FE("h2T", t))
                act.activation(h2T[:, :, :], halves(fbank), ACT.Copy).then_inc(FA["h2T"], 1)

            def value(t, slot, turn):
                yield 6
                act.wait_ge(*VE("h3T", t))
                act.activation(h3T[slot][:, :, :], halves(vbank), ACT.Copy).then_inc(VA["h3T"], 1)

            def inverse(t, slot, turn):
                for j in range(1, 6):
                    yield (0, 1, 2, 5, 7)[j - 1]
                    act.wait_ge(*ME(f"sq{j}", t))
                    n = 2 if j < 5 else 1
                    act.activation(pw[j % 2][:, 0:n, :], sqbank[:, 0:n * P].rearrange("p (n s) -> p n s", n=n),
                                   ACT.Copy).then_inc(MA[f"pw{j}"], 1)

            def train(t, slot, turn):
                yield 9
                act.wait_ge(*BE("dw", t))
                act.activation(wt[:, :, :], wbank[:, :].rearrange("p (k c) -> p k c", k=KH), ACT.Copy)\
                   .then_inc(BA["w"], 1)

            def route(t, slot, turn):
                yield 8
                act.wait_ge(*RE("h4T", t))
                act.activation(h4T[:, :, :], halves(rbank), ACT.Copy).then_inc(RA["h4T"], 1)
                act.activation(at(m.y, t), h4[:, :], ACT.Copy).then_inc(RA["keep"], 1)
                act.activation(at(m.x, t), x3[slot][:, :], ACT.Copy).then_inc(RA["x3"], 1)

            run_pipeline(act, in_order(heads, ffn, value, inverse, train, route), TILES, S)

        @block.tensor
        def _(pe):
            for k in range(KH):
                pe.matmul(wbank[:, k * CH:(k + 1) * CH], m.ident[:, :], m.w0t[:, k, :], start=(k == 0), stop=False,
                          skip_group_check=True)

            def turned(out, src):
                for k in range(KH):
                    last = pe.transpose(out[:, k * P:(k + 1) * P], src[:, k * P:(k + 1) * P], m.ident[:, :])
                return last

            def project(out, lhs, w):
                for k in range(KH):
                    last = pe.matmul(out, lhs[:, k, :], w[:, k, :], start=(k == 0), stop=(k == KH - 1))
                return last

            def heads(t, slot, turn):
                yield 6
                pe.wait_ge(*HD("yn", t))
                turned(hbank, yn).then_inc(HE["ynT"], 1)
                yield 12
                pe.wait_ge(*HA("ynT", t))
                project(hbank[:, CH:2 * CH], ynT, m.wo).then_inc(HE["z"], 1)

            def ffn(t, slot, turn):
                yield 5
                pe.wait_ge(*FD("h", t))
                turned(fbank, h2).then_inc(FE["h2T"], 1)
                yield 8
                pe.wait_ge(*FA("h2T", t))
                project(fbank[:, CH:2 * CH], h2T, m.wf).then_inc(FE["f"], 1)

            def value(t, slot, turn):
                yield 11
                pe.wait_ge(*VD("h", t))
                turned(vbank, h3[slot]).then_inc(VE["h3T"], 1)
                yield 15
                pe.wait_ge(*VA("h3T", t))
                project(vbank[:, CH:2 * CH], h3T[slot], m.wvt).then_inc(VE["v"], 1)

            def gram(t, slot, turn):
                yield 16
                pe.wait_ge(*VA("h3T", t))
                if begun(t, 1):
                    pe.wait_ge(*MA("pw5", t - 1))
                for k in range(KH):
                    last = pe.matmul(sqbank[:, 0:P], h3T[slot][:, k, :], h3T[slot][:, k, :], start=(k == 0),
                                     stop=(k == KH - 1))
                last.then_inc(ME["g"], 1)

            def inverse(t, slot, turn):
                for j in range(1, 6):
                    yield (0, 1, 3, 4, 9)[j - 1]
                    src = p0 if j == 1 else pw[(j - 1) % 2]
                    if j == 1:
                        pe.wait_ge(*MD("t0", t))
                    else:
                        pe.wait_ge(*MA(f"pw{j - 1}", t))
                    last = pe.matmul(sqbank[:, 0:P], src[:, 1, :], src[:, 0, :], start=True, stop=True)
                    if j < 5:
                        last = pe.matmul(sqbank[:, P:2 * P], src[:, 0, :], src[:, 1, :], start=True, stop=True)
                    last.then_inc(ME[f"sq{j}"], 1)
                    if j > 1:
                        pe.wait_ge(*MD(f"t{j - 2}", t))
                        pe.matmul(upbank[:, 0:P], src[:, 0, :], inv[slot][:, :], start=True, stop=True)\
                          .then_inc(ME[f"up{j - 1}"], 1)
                yield 13
                pe.wait_ge(*MA("pw5", t))
                pe.wait_ge(*MD("t4", t))
                pe.matmul(upbank[:, 0:P], pw[1][:, 0, :], inv[slot][:, :], start=True, stop=True)\
                  .then_inc(ME["up5"], 1)

            def train(t, slot, turn):
                yield 2
                if begun(t, 1):
                    pe.wait_ge(*BA("w", t - 1))
                    pe.wait_ge(*BD("yl", t - 1))
                pe.wait_ge(*VD("v", t))
                project(ebank[:, 0:CH], h3T[slot], wt).then_inc(BE["xw"], 1)
                yield 7
                pe.wait_ge(*BD("diff", t))
                pe.wait_ge(*MD("t5", t))
                pe.matmul(ebank[:, CH:2 * CH], inv[slot][:, :], diff[:, :], start=True, stop=True)\
                  .then_inc(BE["err"], 1)
                yield 17
                pe.wait_ge(*BD("es", t))
                for k in range(KH):
                    last = pe.matmul(wbank[:, k * CH:(k + 1) * CH], h3[slot][:, k * P:(k + 1) * P], es[:, :],
                                     start=False, stop=False, skip_group_check=True)
                last.then_inc(BE["dw"], 1)

            def route(t, slot, turn):
                yield 10
                pe.wait_ge(*RD("h", t))
                turned(rbank, h4).then_inc(RE["h4T"], 1)
                yield 14
                pe.wait_ge(*RA("keep", t))
                for k in range(KH):
                    last = pe.matmul(rbank[:, CH:CH + EXPERTS], h4T[:, k, :], m.wg[:, k, :], start=(k == 0),
                                     stop=(k == KH - 1))
                last.then_inc(RE["logits"], 1)

            run_pipeline(pe, in_order(heads, ffn, value, gram, inverse, train, route), TILES, S)


def routing(nc, m, r):
    ctx = ExitStack()
    with ctx:
        def sb(name, shape, dt=FP32):
            return ctx.enter_context(nc.sbuf_tensor(name, shape, dt))

        E, T = EXPERTS, TILES
        KET = TOPK * E * T
        number = sb("c_number", [P, E], I32)
        eight = sb("c_eight", [P, T, E])
        base = sb("c_base", [P, E])
        own = sb("c_own", [P, TOPK, T])
        owni = sb("c_owni", [P, TOPK, T], I32)
        numf = sb("c_numf", [P, E])
        best = [sb(f"c_best{k}", [P, T]) for k in range(TOPK)]
        eq = sb("c_eq", [P, T, E])
        first = sb("c_first", [P, T])
        oh = [sb(f"c_oh{k}", [P, T, E]) for k in range(TOPK)]
        rest = sb("c_rest", [P, T, E])
        gap = sb("c_gap", [P, T])
        expg = sb("c_expg", [P, T])
        den = sb("c_den", [P, T])
        ohs = sb("c_ohs", [P, TOPK, E, T])
        same = sb("c_same", [P, P])
        before = sb("c_before", [P, P])
        prior = sb("c_prior", [P, P])
        every = sb("c_every", [P, P])
        keepon = sb("c_keepon", [P, TOPK, E, T])
        tiles_ = sb("c_tiles", [P, KET])
        upto = sb("c_upto", [P, KET])
        pos = sb("c_pos", [P, TOPK, E, T])
        batch0 = sb("c_batch0", [P, TOPK * E])
        choice0 = sb("c_choice0", [P, E])
        picked = sb("c_picked", [P, TOPK, E, T])
        spot = sb("c_spot", [P, TOPK, T])
        keep = sb("c_keep", [P, TOPK, T])
        row = sb("c_row", [P, TOPK, T])
        dest = sb("c_dest", [P, TOPK, T])

        done = ctx.enter_context(nc.semaphore("c_dve"))
        made = ctx.enter_context(nc.semaphore("c_pool"))
        counted = ctx.enter_context(nc.semaphore("c_pe"))
        expd = ctx.enter_context(nc.semaphore("c_act"))
        block = ctx.enter_context(nc.Block())
        marks = {}

        @block.gpsimd
        def _(pool):
            pool.iota(number[:, :], pattern=[[1, E]], base=0, channel_multiplier=0)
            pool.iota(owni[:, :, :], pattern=[[T * P, TOPK], [P, T]], base=DROPPED, channel_multiplier=1)
            pool.memset(every[:, :], 1.0)
            pool.memset(keepon[:, :, :, :], 1.0)
            pool.memset(prior[:, :], 0.0).then_inc(made, 1)

        @block.vector
        def _(dve):
            state = [0]

            def then(ins):
                ins.then_inc(done, 1)
                state[0] += 1
                dve.wait_ge(done, state[0])
                return state[0]

            def over_e(ap):
                return ap.rearrange("p (t one) -> p t one", one=1).to_broadcast([P, T, E])

            def by_expert(ap):
                return ap.rearrange("p t e -> p e t")

            dve.wait_ge(made, 1)
            then(dve.tensor_copy(numf[:, :], number[:, :]))
            then(dve.tensor_copy(own[:, :, :], owni[:, :, :]))
            then(dve.tensor_scalar(base[:, :], numf[:, :], float(SLOTS), None, ALU.mult))
            for t in range(T):
                last = dve.tensor_scalar(eight[:, t, :], numf[:, :], -1.0, float(E), ALU.mult, ALU.add)
            then(last)
            scores = m.logits
            for k in range(TOPK):
                then(dve.tensor_reduce(best[k][:, :], scores[:, :, :], AX.X, ALU.max))
                then(dve.tensor_tensor(eq[:, :, :], scores[:, :, :], over_e(best[k][:, :]), ALU.is_equal))
                then(dve.tensor_tensor(eq[:, :, :], eq[:, :, :], eight[:, :, :], ALU.mult))
                then(dve.tensor_reduce(first[:, :], eq[:, :, :], AX.X, ALU.max))
                then(dve.tensor_tensor(oh[k][:, :, :], eight[:, :, :], over_e(first[:, :]), ALU.is_equal))
                then(dve.tensor_copy(ohs[:, k, :, :], by_expert(oh[k][:, :, :])))
                if k == 0:
                    then(dve.scalar_tensor_tensor(rest[:, :, :], oh[0][:, :, :], -3e38, m.logits[:, :, :], ALU.mult,
                                                  ALU.add))
                    scores = rest
            for b in range(BATCH):
                cols = slice(b * STEPS, (b + 1) * STEPS)
                then(dve.tensor_scalar(same[:, cols], every[:, cols], m.side[:, b:b + 1], None, ALU.mult))
            then(dve.tensor_tensor(before[:, :], same[:, :], m.later[:, :], ALU.mult))
            then(dve.tensor_scalar(prior[:, STEPS:P], every[:, STEPS:P], m.side[:, 0:1], None, ALU.mult))
            then(dve.memset(keepon[:, :, :, 0:1], 0.0))
            marks["pe"] = state[0]
            marks["gap"] = then(dve.tensor_tensor(gap[:, :], best[1][:, :], best[0][:, :], ALU.subtract))
            dve.wait_ge(expd, 1)
            then(dve.tensor_scalar_add(den[:, :], expg[:, :], 1.0))
            then(dve.reciprocal(r.gate[:, 0, :], den[:, :]))
            then(dve.tensor_tensor(r.gate[:, 1, :], r.gate[:, 0, :], expg[:, :], ALU.mult))
            dve.wait_ge(counted, 4)
            then(dve.tensor_copy(tiles_[:, :], m.bank[1][:, :]))
            then(dve.tensor_tensor_scan(upto[:, :], keepon[:, :, :, :].rearrange("p k e t -> p (k e t)"), tiles_[:, :],
                                        0.0, ALU.mult, ALU.add))
            flat = pos[:, :, :, :].rearrange("p k e t -> p (k e t)")
            then(dve.tensor_tensor(flat, upto[:, :], tiles_[:, :], ALU.subtract))
            then(dve.tensor_tensor(flat, m.bank[0][:, :], flat, ALU.add))
            then(dve.tensor_reduce(batch0[:, :], m.bank[2][:, :].rearrange("p (n t) -> p n t", t=T), AX.X, ALU.add))
            then(dve.tensor_reduce(choice0[:, :], m.bank[3][:, 0:E * T].rearrange("p (n t) -> p n t", t=T), AX.X,
                                   ALU.add))
            pket = pos[:, :, :, :].rearrange("p k e t -> p (k e) t")
            then(dve.tensor_tensor(pket, pket, batch0[:, :].rearrange("p (n one) -> p n one", one=1)
                                   .to_broadcast([P, TOPK * E, T]), ALU.add))
            then(dve.tensor_tensor(pos[:, 1, :, :], pos[:, 1, :, :], choice0[:, :].rearrange("p (n one) -> p n one", one=1)
                                   .to_broadcast([P, E, T]), ALU.add))
            for k in range(TOPK):
                then(dve.tensor_tensor(picked[:, k, :, :], pos[:, k, :, :], ohs[:, k, :, :], ALU.mult))
                then(dve.tensor_reduce(spot[:, k, :], picked[:, k, :, :].rearrange("p e t -> p t e"), AX.X, ALU.add))
                then(dve.tensor_tensor(picked[:, k, :, :], ohs[:, k, :, :],
                                       base[:, :].rearrange("p (n one) -> p n one", one=1).to_broadcast([P, E, T]),
                                       ALU.mult))
                then(dve.tensor_reduce(row[:, k, :], picked[:, k, :, :].rearrange("p e t -> p t e"), AX.X, ALU.add))
            then(dve.tensor_tensor(row[:, :, :], row[:, :, :], spot[:, :, :], ALU.add))
            then(dve.tensor_scalar(keep[:, :, :], spot[:, :, :], float(CAPACITY), None, ALU.is_lt))
            then(dve.tensor_tensor(r.gate[:, :, :], r.gate[:, :, :], keep[:, :, :], ALU.mult))
            then(dve.tensor_tensor(dest[:, :, :], row[:, :, :], own[:, :, :], ALU.subtract))
            then(dve.tensor_tensor(dest[:, :, :], dest[:, :, :], keep[:, :, :], ALU.mult))
            then(dve.tensor_tensor(dest[:, :, :], dest[:, :, :], own[:, :, :], ALU.add))
            then(dve.tensor_copy(r.put[:, :, :], dest[:, :, :]))
            then(dve.tensor_tensor(row[:, :, :], row[:, :, :], keep[:, :, :], ALU.mult))
            then(dve.tensor_copy(r.get[:, :, :], row[:, :, :]))

        @block.scalar
        def _(act):
            act.wait_ge(done, marks["gap"])
            act.activation(expg[:, :], gap[:, :], ACT.Exp).then_inc(expd, 1)

        @block.tensor
        def _(pe):
            pe.wait_ge(made, 1)
            pe.wait_ge(done, marks["pe"])
            chosen = ohs[:, :, :, :].rearrange("p k e t -> p (k e t)")
            for i, mask in enumerate((before, same, prior, every)):
                pe.matmul(m.bank[i][:, :], mask[:, :], chosen, start=True, stop=True).then_inc(counted, 1)


def experts(nc, m, r, a, out):
    ctx = ExitStack()
    with ctx:
        def sb(name, shape, dt=FP32):
            return ctx.enter_context(nc.sbuf_tensor(name, shape, dt))

        def sem(name):
            return ctx.enter_context(nc.semaphore(name))

        SPLIT = ((0, ROWS // 16 * 16), (ROWS // 16 * 16, ROWS))
        E2 = 2
        w1 = [sb(f"d_w1_{s}", [P, KH, HIDDEN]) for s in range(E2)]
        w2 = [sb(f"d_w2_{s}", [P, FT, CH]) for s in range(E2)]
        b1 = [sb(f"d_b1_{s}", [P, FT]) for s in range(E2)]
        b2 = [sb(f"d_b2_{s}", [P, CH]) for s in range(E2)]
        rows = [sb(f"d_rows{s}", [ROWS, 2, CH]) for s in range(2)]
        xg = [sb(f"d_xg{s}", [P, KH, GROUP]) for s in range(2)]
        hid = [sb(f"d_hid{s}", [P, FT, GROUP]) for s in range(2)]
        res = [sb(f"d_res{s}", [ROWS, 2, CH]) for s in range(2)]

        put_done = sem("d_put")
        w_in = [sem(f"d_w_in{s}") for s in range(E2)]
        rows_in = [sem(f"d_rows_in{s}") for s in range(2)]
        res_out = [sem(f"d_res_out{s}") for s in range(2)]
        passed = {e: sem(f"d_passed_{e}") for e in ("dve", "pe", "act")}
        TD = Steps(sem("turn_dve"), "xg")
        TE = Steps(sem("turn_pe"), "turned")
        ED = Steps(sem("expert_dve"), "res")
        EA = Steps(sem("expert_act"), " ".join(f"gelu{f}" for f in range(FT)))
        EE = Steps(sem("expert_pe"), " ".join(f"up{f}" for f in range(0, FT, 2)) + " down")
        block = ctx.enter_context(nc.Block())
        N = EXPERTS * GROUPS
        U = E2 * GROUPS

        @block.gpsimd
        def _(pool):
            for t in range(TILES):
                for k in range(TOPK):
                    pool.indirect_dma_start(
                        out=r.sent[:, :], out_offset=bass.IndirectOffsetOnAxis(ap=r.put[:, k, t:t + 1], axis=0),
                        in_=m.y[:, t, :], in_offset=None).then_inc(put_done, 16)

        @block.sync
        def _(sp):
            def weights(e, s):
                sp.dma_start(w1[s][:, :, :], a["L1_ffn_W1"][bass.ds(e, 1), :, :]
                             .rearrange("a (k p) f -> p (a k) f", p=P)).then_inc(w_in[s], 16)
                sp.dma_start(w2[s][:, :, :], a["L1_ffn_W2"][bass.ds(e, 1), :, :]
                             .rearrange("a (k p) f -> p (a k) f", p=P)).then_inc(w_in[s], 16)
                with nc.allow_non_contiguous_dma(reason="an expert's bias, by hidden unit"):
                    sp.dma_start(b1[s][:, :], a["L1_ffn_b1"][bass.ds(e, 1), :]
                                 .rearrange("a (k p) -> p (a k)", p=P)).then_inc(w_in[s], 16)
                sp.dma_start(b2[s][:, :], a["L1_ffn_b2"][bass.ds(e, 1), :].to_broadcast([P, CH]))\
                  .then_inc(w_in[s], 16)

            for s in range(E2):
                weights(s, s)
            sp.wait_ge(put_done, 16 * TILES * TOPK)

            def fetch(n, slot, turn):
                yield 0
                if slot % GROUPS == 0 and begun(n, U):
                    sp.wait_ge(*EE("down", n - GROUPS - 1))
                    sp.wait_ge(*ED("res", n - GROUPS - 1))
                    weights(turn * E2 + slot // GROUPS, slot // GROUPS)
                if begun(n, 2):
                    sp.wait_ge(*TE("turned", n - 2))
                for lo, hi in SPLIT:
                    sp.dma_start(rows[slot % 2][lo:hi, :, :], r.sent[bass.ds(n * GROUP, GROUP), :]
                                 .rearrange("(a p) c -> p a c", p=ROWS)[lo:hi, :, :]).then_inc(rows_in[slot % 2], 16)

            def store(n, slot, turn):
                yield 0
                sp.wait_ge(*ED("res", n))
                for lo, hi in SPLIT:
                    sp.dma_start(r.back[bass.ds(n * GROUP, GROUP), :].rearrange("(a p) c -> p a c", p=ROWS)[lo:hi, :, :],
                                 res[slot % 2][lo:hi, :, :]).then_inc(res_out[slot % 2], 16)

            run_pipeline(sp, [(fetch, 0), (store, 2)], N, U)
            for s in range(2):
                sp.wait_ge(res_out[s], 32 * (N // 2))

        @block.vector
        def _(dve):
            def turn_in(n, slot, turn):
                yield 0
                dve.wait_ge(*TE("turned", n))
                dve.sem_inc(passed["dve"], 1)
                dve.tensor_copy(xg[slot % 2][:, :, :].rearrange("p k s -> p (k s)"),
                                m.bank[0][:, 0:KH * GROUP]).then_inc(TD["xg"], 1)

            def result(n, slot, turn):
                yield 0
                s = slot // GROUPS
                dve.wait_ge(w_in[s], turn * 64 + 64)
                dve.wait_ge(*EE("down", n))
                if begun(n, 2):
                    dve.wait_ge(res_out[slot % 2], (turn * (U // 2) + slot // 2) * 32)
                for i in range(2):
                    last = dve.tensor_tensor(res[slot % 2][:, i, :], m.bank[5 + slot % 2][0:ROWS, i * CH:(i + 1) * CH],
                                             b2[s][0:ROWS, :], ALU.add)
                last.then_inc(ED["res"], 1)

            run_pipeline(dve, [(turn_in, 0), (result, 1)], N, U)

        @block.scalar
        def _(act):
            def gelu(n, slot, turn):
                yield 0
                s = slot // GROUPS
                act.wait_ge(w_in[s], turn * 64 + 64)
                for f in range(FT):
                    if f % 2 == 0:
                        act.wait_ge(*EE(f"up{f}", n))
                    act.activation(hid[slot % 2][:, f, :], m.bank[1 + f // 2][:, (f % 2) * GROUP:(f % 2 + 1) * GROUP],
                                   ACT.Gelu_apprx_tanh, bias=b1[s][:, f:f + 1]).then_inc(EA[f"gelu{f}"], 1)

            run_pipeline(act, [(gelu, 1)], N, U)

        @block.tensor
        def _(pe):
            def turn_in(n, slot, turn):
                yield 0
                pe.wait_ge(rows_in[slot % 2], (turn * (U // 2) + (slot // 2 + 1)) * 32)
                if begun(n, 1):
                    pe.wait_ge(*TD("xg", n - 1))
                for k in range(KH):
                    for i in range(2):
                        last = pe.transpose(m.bank[0][:, k * GROUP + i * ROWS:k * GROUP + (i + 1) * ROWS],
                                            rows[slot % 2][:, i, k * P:(k + 1) * P], m.ident[0:ROWS, 0:ROWS])
                last.then_inc(TE["turned"], 1)

            def up(n, slot, turn):
                yield 0
                s = slot // GROUPS
                pe.wait_ge(w_in[s], turn * 64 + 64)
                pe.wait_ge(*TD("xg", n))
                for f in range(FT):
                    if f % 2 == 0 and begun(n, 1):
                        pe.wait_ge(*EA(f"gelu{f + 1}", n - 1))
                    for k in range(KH):
                        last = pe.matmul(m.bank[1 + f // 2][:, (f % 2) * GROUP:(f % 2 + 1) * GROUP],
                                         w1[s][:, k, f * P:(f + 1) * P], xg[slot % 2][:, k, :], start=(k == 0),
                                         stop=(k == KH - 1))
                    if f % 2:
                        last.then_inc(EE[f"up{f - 1}"], 1)

            def down(n, slot, turn):
                yield 0
                s = slot // GROUPS
                if begun(n, 2):
                    pe.wait_ge(*ED("res", n - 2))
                pe.wait_ge(*EA("gelu7", n))
                for i in range(2):
                    for f in range(FT):
                        last = pe.matmul(m.bank[5 + slot % 2][0:ROWS, i * CH:(i + 1) * CH],
                                         hid[slot % 2][:, f, i * ROWS:(i + 1) * ROWS], w2[s][:, f, :],
                                         start=(f == 0), stop=(f == FT - 1))
                last.then_inc(EE["down"], 1)

            run_pipeline(pe, [(up, 1), (turn_in, 0), (down, 1)], N, U)


def combine(nc, m, r, out):
    ctx = ExitStack()
    with ctx:
        def sb(name, shape, dt=FP32):
            return ctx.enter_context(nc.sbuf_tensor(name, shape, dt))

        def sem(name):
            return ctx.enter_context(nc.semaphore(name))

        S = 4
        got = [sb(f"e_got{s}", [P, TOPK, CH]) for s in range(S)]
        one = [sb(f"e_one{s}", [P, CH]) for s in range(2)]
        two = [sb(f"e_two{s}", [P, CH]) for s in range(2)]
        gated = [sb(f"e_gated{s}", [P, CH]) for s in range(2)]
        final = [sb(f"e_final{s}", [P, CH]) for s in range(S)]
        got_in = [sem(f"e_got_in{s}") for s in range(S)]
        stored = [sem(f"e_stored{s}") for s in range(S)]
        CD = Steps(sem("combine_dve"), "one two gated final")
        block = ctx.enter_context(nc.Block())

        @block.gpsimd
        def _(pool):
            for t in range(TILES):
                if t >= S:
                    pool.wait_ge(*CD("two", t - S))
                for k in range(TOPK):
                    pool.indirect_dma_start(
                        out=got[t % S][:, k, :], out_offset=None, in_=r.back[:, :],
                        in_offset=bass.IndirectOffsetOnAxis(ap=r.get[:, k, t:t + 1], axis=0)).then_inc(got_in[t % S], 16)

        @block.vector
        def _(dve):
            def add(t, slot, turn):
                yield 0
                x = m.x[:, bass.ds(t, 1), :].rearrange("p a c -> p (a c)")
                dve.wait_ge(got_in[slot], turn * 32 + 32)
                dve.tensor_scalar(one[slot % 2][:, :], got[slot][:, 0, :], r.gate[:, 0, bass.ds(t, 1)], None, ALU.mult)\
                   .then_inc(CD["one"], 1)
                dve.wait_ge(*CD("one", t))
                dve.scalar_tensor_tensor(two[slot % 2][:, :], got[slot][:, 1, :], r.gate[:, 1, bass.ds(t, 1)],
                                         one[slot % 2][:, :], ALU.mult, ALU.add).then_inc(CD["two"], 1)
                dve.wait_ge(*CD("two", t))
                dve.tensor_tensor(gated[slot % 2][:, :], two[slot % 2][:, :], m.mod[1][:, 5, :], ALU.mult)\
                   .then_inc(CD["gated"], 1)
                dve.wait_ge(*CD("gated", t))
                if begun(t, S):
                    dve.wait_ge(stored[slot], turn * 32)
                dve.tensor_tensor(final[slot][:, :], gated[slot % 2][:, :], x, ALU.add).then_inc(CD["final"], 1)

            run_pipeline(dve, [(add, 0)], TILES, S)

        @block.sync
        def _(sp):
            def store(t, slot, turn):
                yield 0
                sp.wait_ge(*CD("final", t))
                for b in range(BATCH):
                    sp.dma_start(out[b, bass.ds(t * STEPS, STEPS), :], final[slot][b * STEPS:(b + 1) * STEPS, :])\
                      .then_inc(stored[slot], 16)

            run_pipeline(sp, [(store, 0)], TILES, S)
            for s in range(S):
                sp.wait_ge(stored[s], 32 * (TILES // S))


def clear(nc, r):
    ctx = ExitStack()
    with ctx:
        rows, parts = 80, 3
        size = NSLOT * CH // rows // parts
        zero = ctx.enter_context(nc.sbuf_tensor("zero", [rows, size], FP32))
        zeroed = ctx.enter_context(nc.semaphore("zero_made"))
        cleared = ctx.enter_context(nc.semaphore("cleared"))
        block = ctx.enter_context(nc.Block())
        flat = r.sent[0:NSLOT, :].rearrange("(p a) c -> p (a c)", p=rows)

        @block.vector
        def _(dve):
            dve.memset(zero[:, :], 0.0).then_inc(zeroed, 1)

        @block.sync
        def _(sp):
            sp.wait_ge(zeroed, 1)
            for i in range(parts):
                sp.dma_start(flat[:, i * size:(i + 1) * size], zero[:, :]).then_inc(cleared, 16)
            sp.wait_ge(cleared, 16 * parts)


def program(nc, a, out):
    ctx = ExitStack()
    with ctx:
        m = alloc(nc, ctx)
        r = Memory()
        r.gate = m.sb("gate", [P, TOPK, TILES])
        r.put = m.sb("put", [P, TOPK, TILES], I32)
        r.get = m.sb("get", [P, TOPK, TILES], I32)
        r.sent = nc.dram_tensor("sent", (NSLOT + TOPK * TOKENS, CH), FP32, kind="Internal").ap()
        r.back = nc.dram_tensor("results", (NSLOT, CH), FP32, kind="Internal").ap()
        clear(nc, r)
        prologue(nc, m, a)
        time_mix(nc, m, a)
        ffn_and_training(nc, m, a)
        routing(nc, m, r)
        experts(nc, m, r, a, out)
        combine(nc, m, r, out)


def kernel(**inputs):
    import concourse.bacc as _bacc
    from concourse.bass_utils import run_bass_kernel_spmd as _run

    nc = _bacc.Bacc("TRN2", target_bir_lowering=False, num_devices=1)
    used = [n for n in inputs if n not in ("L0_attn_key", "L0_attn_value")]
    arrays, aps = {}, {}
    for name in used:
        arr = np.ascontiguousarray(inputs[name])
        arrays[f"in_{name}"] = arr
        aps[name] = nc.dram_tensor(f"in_{name}", arr.shape, mybir.dt.from_np(arr.dtype), kind="ExternalInput").ap()
    out = nc.dram_tensor("out", (BATCH, TIME, CH), FP32, kind="ExternalOutput").ap()
    program(nc, aps, out)
    return _run(nc, [arrays], core_ids=[0]).results[0]["out"]
```

```python
import numpy as np
from contextlib import ExitStack

import concourse.bass as bass
from concourse import mybir

FP32 = mybir.dt.float32
FP32R = mybir.dt.float32r
I32 = mybir.dt.int32
ALU = mybir.AluOpType
ACT = mybir.ActivationFunctionType
AX = mybir.AxisListType

BATCH, TIME, CH = 2, 2048, 256
P = 128
KH = CH // P
STEPS = P // BATCH
TILES = TIME // STEPS
HEAD = 64
HEADS = CH // HEAD
MIX, MIXES = 32, 4
DECAY_RANK = 64
LEVELS = [1, 2, 4, 8, 16, 32]
RANK, DDIM, UDIM = 4, 100, 50
EXPERTS, TOPK, HIDDEN = 8, 2, 1024
TOKENS = BATCH * TIME
CAPACITY = int(np.ceil(1.2 * TOKENS * TOPK / EXPERTS))
ROWS = 123
GROUP = 2 * ROWS
GROUPS = -(-CAPACITY // GROUP)
SLOTS = GROUPS * GROUP
NSLOT = EXPERTS * SLOTS
DROPPED = NSLOT
FT = HIDDEN // P
LN_EPS, HEAD_EPS = 1e-5, 0.00064
LAST_STEP = 23


class Steps:

    def __init__(self, sem, names):
        self.sem, self.names, self.at = sem, names.split(), 0

    def __getitem__(self, name):
        assert self.names[self.at] == name, (self.names[self.at], name)
        self.at = (self.at + 1) % len(self.names)
        return self.sem

    def __call__(self, name, t):
        return self.sem, t * len(self.names) + (self.names.index(name) + 1)


def run_pipeline(eng, chains, tiles, slots):
    lag = max(l for _, l in chains)
    head = lag + slots
    turns = (tiles - head) // slots

    def one_round(parts):
        work = [f(*at) for f, *at in parts]
        place = [next(g) for g in work]
        for step in range(LAST_STEP + 1):
            for n, g in enumerate(work):
                while place[n] == step:
                    place[n] = next(g, None)
        assert not any(p is not None for p in place)

    def peeled(i):
        one_round([(f, i - l, (i - l) % slots, (i - l) // slots) for f, l in chains if 0 <= i - l < tiles])

    for i in range(head):
        peeled(i)
    with eng.Fori(0, turns, 1) as turn:
        for s in range(slots):
            one_round([(f, turn * slots + (head + s - l), (head + s - l) % slots, turn + (head + s - l) // slots)
                       for f, l in chains])
    for i in range(head + turns * slots, tiles + lag):
        peeled(i)


def begun(t, distance):
    return not isinstance(t, int) or t >= distance


def followed(t):
    return not isinstance(t, int) or t < TILES - 1


class Memory:
    pass


def alloc(nc, ctx):
    m = Memory()

    def sb(name, shape, dt=FP32):
        return ctx.enter_context(nc.sbuf_tensor(name, shape, dt))

    m.ident = sb("ident", [P, P])
    m.x = sb("x_stream", [P, TILES, CH])
    m.y = sb("y_stream", [P, TILES, CH])
    m.mod = [None, sb("mod1", [P, 6, CH])]
    m.half = sb("minus_half", [P, 4])
    m.eps = sb("eps", [P, 1])
    m.head_eps = sb("head_eps", [P, HEADS])
    m.side = sb("side", [P, 2])
    m.later = sb("later", [P, P])
    m.logits = sb("logits", [P, TILES, EXPERTS])
    m.gate = sb("gate", [P, TOPK, TILES])
    m.put = sb("put", [P, TOPK, TILES], I32)
    m.get = sb("get", [P, TOPK, TILES], I32)
    m.w1 = sb("expert_w1", [P, KH, HIDDEN])
    m.w2 = sb("expert_w2", [P, FT, CH])
    m.b1 = [sb(f"expert_b1_{s}", [P, FT]) for s in range(2)]
    m.b2 = [sb(f"expert_b2_{s}", [P, CH]) for s in range(2)]
    m.w1_in = ctx.enter_context(nc.semaphore("w1_in"))
    m.w2_in = ctx.enter_context(nc.semaphore("w2_in"))
    m.bank = [ctx.enter_context(nc.psum_tensor(f"bank{i}", [P, 512], FP32)) for i in range(8)]
    return m


def alloc_ffn(nc, ctx, m):
    def sb(name, shape, dt=FP32):
        return ctx.enter_context(nc.sbuf_tensor(name, shape, dt))

    m.mod[0] = sb("mod0", [P, 6, CH])
    m.wo = sb("wo", [P, KH, CH])
    m.wob = sb("wob", [P, CH])
    m.wf = sb("wf", [P, KH, CH])
    m.bf = sb("bf", [P, CH])
    m.wvt = sb("wvt", [P, KH, CH])
    m.bv = sb("bv", [P, CH])
    m.w0t = sb("w0t", [P, KH, CH])
    m.nbeta = sb("nbeta", [P, 1])
    m.earlier = sb("earlier", [P, P])
    m.wg = sb("wg", [P, KH, EXPERTS])
    m.bg = sb("bg", [P, EXPERTS])


def alloc_mix(nc, ctx, m):
    def sb(name, shape, dt=FP32):
        return ctx.enter_context(nc.sbuf_tensor(name, shape, dt))

    m.maa = sb("maa", [P, 5, KH])
    m.mw1 = sb("mix_w1", [P, KH, P])
    m.mw2 = sb("mix_w2", [P, MIXES, CH])
    m.dw1 = sb("dw1", [P, KH, DECAY_RANK])
    m.dw2 = sb("dw2", [DECAY_RANK, CH])
    m.decay = sb("decay", [P, KH])
    m.bonus = sb("bonus", [P, KH])
    m.wr = sb("wr", [P, KH, CH])
    m.wk = sb("wk", [P, KH, CH])
    m.wv = sb("wv", [P, KH, CH])
    m.lmask = sb("lmask", [P, len(LEVELS), 2, STEPS], I32)
    m.dmask = sb("dmask", [P, 2, STEPS])


def load_w1(sp, nc, m, a, e, s):
    sp.dma_start(m.w1[:, :, :], a["L1_ffn_W1"][bass.ds(e, 1), :, :]
                 .rearrange("a (k p) f -> p (a k) f", p=P)).then_inc(m.w1_in, 16)
    with nc.allow_non_contiguous_dma(reason="an expert's bias, by hidden unit"):
        sp.dma_start(m.b1[s][:, :], a["L1_ffn_b1"][bass.ds(e, 1), :]
                     .rearrange("a (k p) -> p (a k)", p=P)).then_inc(m.w1_in, 16)


def load_w2(sp, m, a, e, s):
    sp.dma_start(m.w2[:, :, :], a["L1_ffn_W2"][bass.ds(e, 1), :, :]
                 .rearrange("a (k p) f -> p (a k) f", p=P)).then_inc(m.w2_in, 16)
    sp.dma_start(m.b2[s][:, :], a["L1_ffn_b2"][bass.ds(e, 1), :].to_broadcast([P, CH])).then_inc(m.w2_in, 16)


def prologue(nc, m, a):
    ctx = ExitStack()
    with ctx:
        def sb(name, shape, dt=FP32):
            return ctx.enter_context(nc.sbuf_tensor(name, shape, dt))

        def sem(name):
            return ctx.enter_context(nc.semaphore(name))

        wmod = [sb(f"wmod{l}", [P, KH, 6 * CH]) for l in range(2)]
        cT = sb("cT", [P, 2, KH, BATCH])
        ec = sb("ec", [P, 2, KH, BATCH])
        dc = sb("dc", [P, 2, KH, BATCH])
        rc = sb("rc", [P, 2, KH, BATCH])
        sc = sb("sc", [P, 2, KH, BATCH])
        cb = sb("cb", [P, 2, KH, P])
        big = sb("big", [P, 2, CH])
        sign = sb("sign", [P, 2, CH])
        wfr = sb("wfr", [P, KH, CH])
        wvr = sb("wvr", [P, KH, CH])
        w0r = sb("w0r", [P, KH, CH])
        down = sb("down", [DDIM, RANK])
        aux = sb("aux", [DDIM, CH])
        upT = sb("upT", [RANK, UDIM])
        uaT = sb("uaT", [UDIM, CH])
        d1 = sb("d1", [RANK, CH])
        r1 = sb("r1", [UDIM, CH])
        lnw = sb("lnw", [P, KH])
        lnb = sb("lnb", [P, KH])
        lnbb = sb("lnbb", [P, KH, P])
        wor = sb("wor", [P, KH, CH])
        eta = sb("eta", [P, 1])
        row = sb("row", [P, 1], I32)
        rows = sb("rows", [P, 1], I32)
        col = sb("col", [P, STEPS], I32)
        xor = sb("xor", [P, STEPS], I32)
        xorf = sb("xorf", [P, STEPS])
        colf = sb("colf", [P, STEPS])
        rowf = sb("rowf", [P, 1])
        prowf = sb("prowf", [P, 1])
        causal = sb("causal", [P, STEPS])
        lm = sb("lm", [P, len(LEVELS), STEPS])
        ones = sb("ones", [P, P])

        loaded = sem("loaded")
        loaded_mod = sem("loaded_mod")
        made = sem("made")
        v = sem("pro_dve")
        s_act = sem("pro_act")
        s_pe = sem("pro_pe")
        block = ctx.enter_context(nc.Block())
        count = {"w": 0}

        def halves(ap):
            return ap.rearrange("(k p) n -> p k n", p=P)

        def per_channel(ap):
            return ap.rearrange("(k p) -> p k", p=P)

        @block.sync
        def _(sp):
            def load(dst, src, s=loaded):
                sp.dma_start(dst, src).then_inc(s, 16)
                if s is loaded:
                    count["w"] += 16

            with nc.allow_non_contiguous_dma(reason="a few vectors and small weights, once"):
                for l, name in enumerate(("L0_c", "L1_c")):
                    for b in range(BATCH):
                        load(cT[:, l, :, b], per_channel(a[name][b, :]), loaded_mod)
                for l, name in enumerate(("L0_wmod", "L1_wmod")):
                    load(wmod[l][:, :, :], halves(a[name]), loaded_mod)
                for i, x in enumerate("xwkvr"):
                    load(m.maa[:, i, :], per_channel(a["L0_attn_time_maa_" + x]))
                load(m.decay[:, :], per_channel(a["L0_attn_time_decay"]))
                load(m.bonus[:, :], per_channel(a["L0_attn_time_faaaa"].rearrange("h i -> (h i)")))
                load(lnw[:, :], per_channel(a["L0_attn_ln_w"]))
                load(lnb[:, :], per_channel(a["L0_attn_ln_b"]))
                load(down[:, :], a["L0_ffn_lora_down"].rearrange("r d -> d r"))
                load(upT[:, :], a["L0_ffn_lora_up"].rearrange("u r -> r u"))
                load(uaT[:, :], a["L0_ffn_up_aux"].rearrange("o u -> u o"))
                load(aux[:, :], a["L0_ffn_down_aux"])
                load(m.mw1[:, :, :], halves(a["L0_attn_time_maa_w1"]))
                load(m.dw1[:, :, :], halves(a["L0_attn_time_decay_w1"]))
                load(m.dw2[:, :], a["L0_attn_time_decay_w2"])
                for dst, name in ((m.wr, "W_r"), (m.wk, "W_k"), (m.wv, "W_v"), (wor, "W_o")):
                    load(dst[:, :, :], halves(a["L0_attn_" + name]))
                load(wfr[:, :, :], halves(a["L0_ffn_W"]))
                load(w0r[:, :, :], halves(a["L1_attn_W0"]))
                load(wvr[:, :, :], halves(a["L1_attn_Wkv"][CH:2 * CH, :]))
                load(m.wg[:, :, :], halves(a["L1_ffn_Wg"]))
                load(m.bf[:, :], a["L0_ffn_b"].partition_broadcast(P))
                load(m.bv[:, :], a["L1_attn_bkv"][CH:2 * CH].partition_broadcast(P))
                load(m.bg[:, :], a["L1_ffn_bg"].partition_broadcast(P))
                load(eta[:, :], a["L1_attn_eta"].partition_broadcast(P))
                sp.wait_ge(made, 1)
                for f in range(MIXES):
                    load(m.mw2[f * MIX:(f + 1) * MIX, f, :], a["L0_attn_time_maa_w2"][f, :, :])

        all_loaded = count["w"]

        @block.gpsimd
        def _(pool):
            pool.memset(m.mw2[:, :, :], 0.0).then_inc(made, 1)
            pool.memset(m.ident[:, :], 0.0)
            pool.memset(ones[:, :], 1.0)
            pool.memset(m.half[:, :], -0.5)
            pool.memset(m.eps[:, :], LN_EPS)
            pool.memset(m.head_eps[:, :], HEAD * HEAD_EPS)
            pool.iota(row[:, :], pattern=[[0, 1]], base=0, channel_multiplier=1)
            pool.iota(col[:, :], pattern=[[1, STEPS]], base=0, channel_multiplier=0).then_inc(made, 1)
            pool.wait_ge(made, 2)
            pool.affine_select(out=m.ident[:, :], in_=m.ident[:, :], compare_op=ALU.not_equal, fill=1.0, base=0,
                               pattern=[[-1, P]], channel_multiplier=1).then_inc(made, 1)

        @block.scalar
        def _(act):
            act.wait_ge(loaded_mod, 16 * (2 * BATCH + 2))
            act.activation(ec[:, :, :, :], cT[:, :, :, :], ACT.Exp, scale=-1.0).then_inc(s_act, 1)

        def step_list(eng, s):
            state = [0]

            def then(ins):
                ins.then_inc(s, 1)
                state[0] += 1
                eng.wait_ge(s, state[0])
                return state[0]
            return then

        marks = {}

        @block.vector
        def _(dve):
            then = step_list(dve, v)
            dve.wait_ge(s_act, 1)
            then(dve.tensor_scalar_add(dc[:, :, :, :], ec[:, :, :, :], 1.0))
            then(dve.reciprocal(rc[:, :, :, :], dc[:, :, :, :]))
            then(dve.tensor_tensor(sc[:, :, :, :], cT[:, :, :, :], rc[:, :, :, :], ALU.mult))
            dve.wait_ge(made, 3)
            for l in range(2):
                for k in range(KH):
                    for b in range(BATCH):
                        n = then(dve.tensor_scalar(cb[:, l, k, b * STEPS:(b + 1) * STEPS], ones[:, 0:STEPS],
                                                   sc[:, l, k, b:b + 1], None, ALU.mult))
            marks["cb"] = n
            then(dve.tensor_single_scalar(rows[:, :], row[:, :], STEPS - 1, ALU.bitwise_and))
            then(dve.tensor_tensor(xor[:, :], col[:, :], rows[:, 0:1].to_broadcast([P, STEPS]), ALU.bitwise_xor))
            then(dve.tensor_copy(xorf[:, :], xor[:, :]))
            then(dve.tensor_copy(colf[:, :], col[:, :]))
            then(dve.tensor_copy(rowf[:, :], rows[:, :]))
            then(dve.tensor_copy(prowf[:, :], row[:, :]))
            then(dve.tensor_scalar(m.side[:, 0:1], prowf[:, :], float(STEPS), None, ALU.is_lt))
            then(dve.tensor_scalar(m.side[:, 1:2], prowf[:, :], float(STEPS), None, ALU.is_ge))
            then(dve.tensor_scalar(causal[:, :], colf[:, :], rowf[:, 0:1], None, ALU.is_gt))
            for n_, half in enumerate(LEVELS):
                then(dve.tensor_scalar(lm[:, n_, :], xorf[:, :], float(half), None, ALU.is_ge))
                then(dve.scalar_tensor_tensor(lm[:, n_, :], xorf[:, :], float(2 * half), lm[:, n_, :],
                                              ALU.is_lt, ALU.mult))
                then(dve.tensor_tensor(lm[:, n_, :], lm[:, n_, :], causal[:, :], ALU.mult))
                for q in range(2):
                    then(dve.tensor_copy(m.lmask[:, n_, q, :], lm[:, n_, :]))
            then(dve.tensor_tensor(lm[:, 5, :], lm[:, 5, :], lm[:, 4, :], ALU.add))
            for q in range(2):
                then(dve.tensor_copy(m.lmask[:, 5, q, :], lm[:, 5, :]))
            for q in range(2):
                then(dve.tensor_scalar(m.dmask[:, q, :], xorf[:, :], 0.0, None, ALU.is_equal))
            for b in range(BATCH):
                then(dve.tensor_scalar(m.later[:, b * STEPS:(b + 1) * STEPS], colf[:, :], rowf[:, 0:1], None,
                                       ALU.is_gt))
                then(dve.tensor_scalar(m.earlier[:, b * STEPS:(b + 1) * STEPS], colf[:, :], rowf[:, 0:1], None,
                                       ALU.is_lt))
            dve.wait_ge(loaded, all_loaded)
            then(dve.tensor_scalar(m.nbeta[:, :], eta[:, :], -2.0 / (BATCH * CH), None, ALU.mult))
            for k in range(KH):
                then(dve.tensor_scalar(m.wo[:, k, :], wor[:, k, :], lnw[:, k:k + 1], None, ALU.mult))
                n = then(dve.tensor_scalar(lnbb[:, k, :], ones[:, :], lnb[:, k:k + 1], None, ALU.mult))
            marks["lnbb"] = n
            dve.wait_ge(s_pe, 7)
            marks["d1"] = then(dve.tensor_copy(d1[:, :], m.bank[6][0:RANK, 0:CH]))
            dve.wait_ge(s_pe, 8)
            marks["r1"] = then(dve.tensor_copy(r1[:, :], m.bank[7][0:UDIM, 0:CH]))
            for l in range(2):
                dve.wait_ge(s_pe, 3 * l + 3)
                for i in range(3):
                    n = then(dve.tensor_copy(m.mod[l][:, 2 * i:2 * i + 2, :].rearrange("p a c -> p (a c)"),
                                             m.bank[3 * l + i][:, :]))
                marks[f"mod{l}"] = n
                for i in (1, 4):
                    then(dve.tensor_scalar_add(m.mod[l][:, i, :], m.mod[l][:, i, :], 1.0))
                g = m.mod[l][:, 2:6:3, :]
                then(dve.tensor_scalar(big[:, :, :], g, -1.0, None, ALU.mult))
                then(dve.tensor_tensor(big[:, :, :], big[:, :, :], g, ALU.max))
                then(dve.tensor_scalar(big[:, :, :], big[:, :, :], 0.25, None, ALU.max))
                then(dve.tensor_scalar(sign[:, :, :], g, 0.0, 2.0, ALU.is_ge, ALU.mult))
                then(dve.scalar_tensor_tensor(g, sign[:, :, :], -1.0, big[:, :, :], ALU.add, ALU.mult))
            then(dve.tensor_tensor(m.bf[:, :], m.bf[:, :], m.mod[0][:, 5, :], ALU.mult))
            dve.wait_ge(s_pe, 9)
            then(dve.tensor_tensor(m.wob[:, :], m.bank[6][:, 0:CH], m.mod[0][:, 2, :], ALU.mult))
            for i, dst in enumerate((m.wf, m.wvt, m.w0t)):
                dve.wait_ge(s_pe, 10 + i)
                then(dve.tensor_copy(dst[:, :, :].rearrange("p k c -> p (k c)"), m.bank[i][:, :]))

        @block.tensor
        def _(pe):
            pe.wait_ge(made, 3)
            pe.wait_ge(loaded_mod, 16 * (2 * BATCH + 2))
            pe.wait_ge(v, marks["cb"])
            for l in range(2):
                for i in range(3):
                    for k in range(KH):
                        mm = pe.matmul(m.bank[3 * l + i][:, :], cb[:, l, k, :], wmod[l][:, k, 512 * i:512 * i + 512],
                                       start=(k == 0), stop=(k == KH - 1))
                    mm.then_inc(s_pe, 1)
            pe.wait_ge(loaded, all_loaded)
            pe.matmul(m.bank[6][0:RANK, 0:CH], down[:, :], aux[:, :], start=True, stop=True).then_inc(s_pe, 1)
            pe.wait_ge(v, marks["d1"])
            pe.matmul(m.bank[7][0:UDIM, 0:CH], upT[:, :], d1[:, :], start=True, stop=True).then_inc(s_pe, 1)
            pe.wait_ge(v, marks["lnbb"])
            for k in range(KH):
                mm = pe.matmul(m.bank[6][:, 0:CH], lnbb[:, k, :], wor[:, k, :], start=(k == 0), stop=(k == KH - 1))
            mm.then_inc(s_pe, 1)
            pe.wait_ge(v, marks["mod0"])
            for i, src in enumerate((wfr, wvr, w0r)):
                bank = m.bank[i]
                for k in range(KH):
                    for o in range(KH):
                        out = bank[:, k * CH + o * P:k * CH + (o + 1) * P]
                        mm = pe.matmul(out, src[:, o, k * P:(k + 1) * P], m.ident[:, :], start=True, stop=(i > 0))
                        if i == 0:
                            mm = pe.matmul(out, r1[:, k * P:(k + 1) * P], uaT[:, o * P:(o + 1) * P],
                                           start=False, stop=True)
                mm.then_inc(s_pe, 1)


def time_mix(nc, m, a):
    ctx = ExitStack()
    with ctx:
        S = 4

        def sb(name, shape, dt=FP32):
            return ctx.enter_context(nc.sbuf_tensor(name, shape, dt))

        def slots(name, shape):
            return [sb(f"{name}{s}", shape) for s in range(S)]

        def sem(name):
            return ctx.enter_context(nc.semaphore(name))

        stats = sb("a_stats", [P, 6])
        mv = sb("a_mv", [P, 2])
        ve = sb("a_ve", [P, 1])
        rstd = sb("a_rstd", [P, 1])
        xm = sb("a_xm", [P, CH])
        h = sb("a_h", [P, CH])
        hT = slots("a_hT", [P, KH, BATCH, STEPS + 1])
        xx = slots("a_xx", [P, KH, BATCH, STEPS])
        xxx = sb("a_xxx", [P, KH, P])
        mt = slots("a_mt", [P, P])
        xf = sb("a_xf", [P, MIXES, KH, P])
        dt_ = sb("a_dt", [DECAY_RANK, P])
        ew = sb("a_ew", [P, KH, P])
        rp = slots("a_rp", [P, KH, P])
        kq = slots("a_kq", [P, KH, P])
        ru = slots("a_ru", [P, KH, P])
        vt = slots("a_vt", [P, CH])
        tots = [[sb(f"a_tot{i}_{s}", [P, KH * P >> i]) for i in range(len(LEVELS) + 1)] for s in range(S)]
        att = slots("a_att", [P, KH, 2, STEPS])
        blk = sb("a_blk", [P, HEADS, P])
        kt = sb("a_kt", [P, BATCH, CH])
        state = sb("a_state", [P, BATCH * KH, HEAD])
        sdec = sb("a_sdec", [P, BATCH * KH, HEAD])
        sblk = sb("a_sblk", [P, BATCH * KH, P])

        x_loaded = [sem(f"a_x_loaded{s}") for s in range(S)]
        ready = sem("a_ready")
        passed = {e: sem(f"a_passed_{e}") for e in ("dve", "pool", "pe", "act")}
        ND = Steps(sem("norm_dve"), "stats mv ve xm h xx xxx")
        NP = Steps(sem("norm_pool"), "rstd")
        NA = Steps(sem("norm_act"), "carry hT mt")
        NE = Steps(sem("norm_pe"), "hT m")
        FD = Steps(sem("mix_dve"), "xf0 xf1 xf2 xf3")
        FP = Steps(sem("mix_pool"), "add0 add1 add3 add2")
        FA = Steps(sem("mix_act"), "dt r k ru0 ru1 ew0 ew1 w v")
        FE = Steps(sem("mix_pe"), "x0 x1 x2 x3 d r k w v")
        LD = [Steps(sem("low_dve"), "rp0 tot0 diag0 diag1 cp0a cp0b rp1 tot1 cp1a cp1b rp2 tot2 cp2a cp2b"),
              Steps(sem("high_dve"), "rp3 tot3 cp3a cp3b rp4 tot4 rp5 tot5 cp5a cp5b")]
        LP = [Steps(sem("low_pool"), "kq0 kq1 kq2"), Steps(sem("high_pool"), "kq3 kq4 kq5")]
        LE = [Steps(sem("low_pe"), "l0 l1 l2"), Steps(sem("high_pe"), "l3 l4 l5")]
        YD = Steps(sem("out_dve"), "sdec state")
        YA = Steps(sem("out_act"), "blk0 blk1 kt0 kt1 sblk0 sblk1 y")
        YE = Steps(sem("out_pe"), "kT kv y")
        block = ctx.enter_context(nc.Block())

        hbank, xbank, ybank, kvbank = m.bank[0], m.bank[1], m.bank[6], m.bank[7]
        lbank = [(m.bank[2], m.bank[3]), (m.bank[4], m.bank[5])]

        def at(stream, t):
            return stream[:, bass.ds(t, 1), :].rearrange("p a c -> p (a c)")

        def by_head(bank, base=0):
            return bank[:, base:base + P].rearrange("p (k s) -> p k s", k=KH)

        @block.sync
        def _(sp):
            def load(t, slot, turn):
                yield 0
                if begun(t, S):
                    sp.wait_ge(x_loaded[slot], turn * 32)
                for b in range(BATCH):
                    sp.dma_start(at(m.x, t)[b * STEPS:(b + 1) * STEPS, :],
                                 a["L0_attn_query"][b, bass.ds(t * STEPS, STEPS), :]).then_inc(x_loaded[slot], 16)

            run_pipeline(sp, [(load, 0)], TILES, S)

        @block.gpsimd
        def _(pool):
            pool.memset(hT[S - 1][:, :, :, :], 0.0)
            pool.memset(kt[:, :, :], 0.0)
            pool.memset(state[:, :, :], 0.0).then_inc(ready, 1)
            pool.wait_ge(ready, 1)

            def norm(t, slot, turn):
                yield 0
                pool.wait_ge(*ND("ve", t))
                pool.tensor_tensor(rstd[:, :], ve[:, :], m.half[:, 0:1], ALU.pow).then_inc(NP["rstd"], 1)

            def mix(t, slot, turn):
                for step, f in ((2, 0), (2, 1), (5, 3), (5, 2)):
                    yield step
                    pool.wait_ge(*FD(f"xf{f}", t))
                    pool.tensor_tensor(xf[:, f, :, :].rearrange("p k (b s) -> p k b s", b=BATCH),
                                       xf[:, f, :, :].rearrange("p k (b s) -> p k b s", b=BATCH),
                                       hT[slot][:, :, :, 1:STEPS + 1], ALU.add).then_inc(FP[f"add{f}"], 1)

            def levels(c):
                def chain(t, slot, turn):
                    for j, step in enumerate(((3, 6, 7), (1, 4, 8))[c]):
                        i = 3 * c + j
                        half = LEVELS[i]
                        yield step
                        pool.wait_ge(*LE[c](f"l{i}", t))
                        if i:
                            pool.wait_ge(*LD[(i - 1) // 3](f"tot{i - 1}", t))
                        n = KH * P // (2 * half)
                        view = kq[slot][:, :, :].rearrange("p k (n two s) -> p (k n) two s", two=2, s=half)[:, :, 0, :]
                        dec = tots[slot][i][:, :].rearrange("p (n two) -> p n two", two=2)[:, :, 1:2]
                        pool.tensor_tensor(view, view, dec.to_broadcast([P, n, half]), ALU.mult)\
                            .then_inc(LP[c][f"kq{i}"], 1)
                return chain

            run_pipeline(pool, [(levels(1), 3), (levels(0), 2), (mix, 1), (norm, 0)], TILES, S)

        @block.vector
        def _(dve):
            def norm(t, slot, turn):
                x = at(m.x, t)
                yield 0
                dve.wait_ge(x_loaded[slot], turn * 32 + 32)
                dve.sem_inc(passed["dve"], 1)
                dve.bn_stats(stats[:, :], x).then_inc(ND["stats"], 1)
                dve.wait_ge(*ND("stats", t))
                dve.sem_inc(passed["dve"], 1)
                dve.bn_aggr(mv[:, :], stats[:, :]).then_inc(ND["mv"], 1)
                dve.wait_ge(*ND("mv", t))
                dve.tensor_scalar_add(ve[:, :], mv[:, 1:2], LN_EPS).then_inc(ND["ve"], 1)
                dve.scalar_tensor_tensor(xm[:, :], x, mv[:, 0:1], m.mod[0][:, 1, :], ALU.subtract, ALU.mult)\
                   .then_inc(ND["xm"], 1)
                yield 1
                dve.wait_ge(*NP("rstd", t))
                dve.wait_ge(*ND("xm", t))
                dve.scalar_tensor_tensor(h[:, :], xm[:, :], rstd[:, 0:1], m.mod[0][:, 0, :], ALU.mult, ALU.add)\
                   .then_inc(ND["h"], 1)
                yield 9
                dve.wait_ge(*NA("hT", t))
                dve.tensor_tensor(xx[slot][:, :, :, :], hT[slot][:, :, :, 0:STEPS], hT[slot][:, :, :, 1:STEPS + 1],
                                  ALU.subtract).then_inc(ND["xx"], 1)
                dve.wait_ge(*ND("xx", t))
                for k in range(KH):
                    last = dve.scalar_tensor_tensor(
                        xxx[:, k, :].rearrange("p (b s) -> p b s", b=BATCH), xx[slot][:, k, :, :],
                        m.maa[:, 0, k:k + 1], hT[slot][:, k, :, 1:STEPS + 1], ALU.mult, ALU.add)
                last.then_inc(ND["xxx"], 1)

            def mix(t, slot, turn):
                for f in range(MIXES):
                    if f % 2 == 0:
                        yield (4, 7)[f // 2]
                        dve.wait_ge(*FE(f"x{f + 1}", t))
                    for k in range(KH):
                        last = dve.scalar_tensor_tensor(
                            xf[:, f, k, :], xbank[:, (f % 2) * CH + k * P:(f % 2) * CH + (k + 1) * P],
                            m.maa[:, 1 + f, k:k + 1], xx[slot][:, k, :, :].rearrange("p b s -> p (b s)"),
                            ALU.add, ALU.mult)
                    last.then_inc(FD[f"xf{f}"], 1)

            def levels(c):
                def chain(t, slot, turn):
                    for j, step in enumerate(((5, 8, 12), (3, 6, 10))[c]):
                        i = 3 * c + j
                        half = LEVELS[i]
                        yield step
                        dve.wait_ge(*LE[c](f"l{i}", t))
                        if i:
                            dve.wait_ge(*LD[(i - 1) // 3](f"tot{i - 1}", t))
                        n = KH * P // (2 * half)
                        src = tots[slot][i][:, :].rearrange("p (n two) -> p n two", two=2)
                        view = rp[slot][:, :, :].rearrange("p k (n two s) -> p (k n) two s", two=2, s=half)[:, :, 1, :]
                        dve.tensor_tensor(view, view, src[:, :, 0:1].to_broadcast([P, n, half]), ALU.mult)\
                           .then_inc(LD[c][f"rp{i}"], 1)
                        dve.tensor_tensor(tots[slot][i + 1][:, :].rearrange("p (n one) -> p n one", one=1),
                                          src[:, :, 0:1], src[:, :, 1:2], ALU.mult).then_inc(LD[c][f"tot{i}"], 1)
                        if i == 0:
                            for q in range(2):
                                dve.tensor_tensor(att[slot][:, :, q, :], by_head(lbank[0][q], P), m.dmask[:, :, :],
                                                  ALU.mult).then_inc(LD[c][f"diag{q}"], 1)
                            dve.wait_ge(*LD[c]("diag1", t))
                            dve.sem_inc(passed["dve"], 1)
                        if i != 4:
                            for q in range(2):
                                dve.copy_predicated(att[slot][:, :, q, :], m.lmask[:, i, :, :], by_head(lbank[c][q]))\
                                   .then_inc(LD[c][f"cp{i}{'ab'[q]}"], 1)
                return chain

            def output(t, slot, turn):
                yield 2
                dve.wait_ge(*LD[1]("tot5", t))
                if begun(t, 1):
                    dve.wait_ge(*YD("state", t - 1))
                dve.tensor_tensor(sdec[:, :, :], state[:, :, :],
                                  tots[slot][6][:, :].rearrange("p (n one) -> p n one", one=1)
                                  .to_broadcast([P, KH * BATCH, HEAD]), ALU.mult).then_inc(YD["sdec"], 1)
                yield 11
                dve.wait_ge(*YE("kv", t))
                dve.wait_ge(*YD("sdec", t))
                dve.wait_ge(*YA("sblk1", t))
                dve.tensor_tensor(state[:, :, :], sdec[:, :, :],
                                  kvbank[:, CH:2 * CH].rearrange("p (n j) -> p n j", j=HEAD), ALU.add)\
                   .then_inc(YD["state"], 1)

            dve.wait_ge(ready, 1)
            run_pipeline(dve, [(output, 4), (levels(1), 3), (levels(0), 2), (mix, 1), (norm, 0)], TILES, S)

        @block.scalar
        def _(act):
            def norm(t, slot, turn):
                yield 4
                act.activation(hT[slot][:, :, :, 0:1], hT[slot - 1][:, :, :, STEPS:STEPS + 1], ACT.Copy)\
                   .then_inc(NA["carry"], 1)
                act.wait_ge(*NE("hT", t))
                act.activation(hT[slot][:, :, :, 1:STEPS + 1],
                               hbank[:, 0:CH].rearrange("p (k b s) -> p k b s", k=KH, b=BATCH), ACT.Copy)\
                   .then_inc(NA["hT"], 1)
                yield 8
                act.wait_ge(*NE("m", t))
                act.activation(mt[slot][:, :], hbank[:, CH:CH + P], ACT.Tanh).then_inc(NA["mt"], 1)

            def mix(t, slot, turn):
                yield 3
                act.wait_ge(*FE("d", t))
                act.activation(dt_[:, :], hbank[0:DECAY_RANK, CH + P:CH + 2 * P], ACT.Tanh).then_inc(FA["dt"], 1)
                yield 6
                act.wait_ge(*FE("k", t))
                act.activation(rp[slot][:, :, :], xbank[:, 0:CH].rearrange("p (k s) -> p k s", k=KH), ACT.Copy)\
                   .then_inc(FA["r"], 1)
                act.activation(kq[slot][:, :, :], xbank[:, CH:2 * CH].rearrange("p (k s) -> p k s", k=KH), ACT.Copy)\
                   .then_inc(FA["k"], 1)
                act.wait_ge(*FA("r", t))
                for k in range(KH):
                    act.activation(ru[slot][:, k, :], rp[slot][:, k, :], ACT.Copy, scale=m.bonus[:, k:k + 1])\
                       .then_inc(FA[f"ru{k}"], 1)
                yield 7
                act.wait_ge(*FE("w", t))
                for k in range(KH):
                    act.activation(ew[:, k, :], hbank[:, k * P:(k + 1) * P], ACT.Exp, bias=m.decay[:, k:k + 1])\
                       .then_inc(FA[f"ew{k}"], 1)
                act.wait_ge(*FA("ew1", t))
                act.activation(tots[slot][0][:, :], ew[:, :, :].rearrange("p k s -> p (k s)"), ACT.Exp, scale=-1.0)\
                   .then_inc(FA["w"], 1)
                yield 9
                act.wait_ge(*FE("v", t))
                act.activation(vt[slot][:, :], xbank[:, 0:CH], ACT.Copy).then_inc(FA["v"], 1)

            def output(t, slot, turn):
                yield 0
                act.wait_ge(*LD[1]("cp5b", t))
                for b in range(BATCH):
                    act.activation(blk[:, :, b * STEPS:(b + 1) * STEPS],
                                   att[slot][:, :, :, :].rearrange("p k q s -> p (k q) s"), ACT.Copy,
                                   scale=m.side[:, b:b + 1]).then_inc(YA[f"blk{b}"], 1)
                yield 1
                act.wait_ge(*YE("kT", t))
                for b in range(BATCH):
                    rows = slice(b * STEPS, (b + 1) * STEPS)
                    act.activation(kt[rows, b, :], kvbank[rows, 0:CH], ACT.Copy).then_inc(YA[f"kt{b}"], 1)
                yield 2
                if begun(t, 1):
                    act.wait_ge(*YD("state", t - 1))
                for q in range(2):
                    act.activation(sblk[:, :, q * HEAD:(q + 1) * HEAD], state[:, :, :], ACT.Copy,
                                   scale=m.side[:, q:q + 1]).then_inc(YA[f"sblk{q}"], 1)
                yield 5
                act.wait_ge(*YE("y", t))
                act.activation(at(m.y, t), ybank[:, 0:CH], ACT.Copy).then_inc(YA["y"], 1)

            act.wait_ge(ready, 1)
            run_pipeline(act, [(output, 4), (mix, 1), (norm, 0)], TILES, S)

        @block.tensor
        def _(pe):
            def norm(t, slot, turn):
                yield 9
                pe.wait_ge(*ND("h", t))
                if begun(t, 1):
                    pe.wait_ge(*FA("dt", t - 1))
                for k in range(KH):
                    last = pe.transpose(hbank[:, k * P:(k + 1) * P], h[:, k * P:(k + 1) * P], m.ident[:, :])
                last.then_inc(NE["hT"], 1)
                yield 16
                pe.wait_ge(*ND("xxx", t))
                if begun(t, 1):
                    pe.wait_ge(*FA("ew1", t - 1))
                for k in range(KH):
                    last = pe.matmul(hbank[:, CH:CH + P], m.mw1[:, k, :], xxx[:, k, :], start=(k == 0),
                                     stop=(k == KH - 1))
                last.then_inc(NE["m"], 1)

            def mix(t, slot, turn):
                yield 2
                pe.wait_ge(*NA("mt", t))
                if begun(t, 1):
                    pe.wait_ge(*FA("v", t - 1))
                for f in range(MIXES):
                    if f == 2:
                        yield 5
                        pe.wait_ge(*FD("xf1", t))
                    for k in range(KH):
                        last = pe.matmul(xbank[:, (f % 2) * CH + k * P:(f % 2) * CH + (k + 1) * P],
                                         m.mw2[:, f, k * P:(k + 1) * P], mt[slot][:, :], start=True, stop=True)
                    last.then_inc(FE[f"x{f}"], 1)
                yield 6
                pe.wait_ge(*FP("add0", t))
                for k in range(KH):
                    last = pe.matmul(hbank[0:DECAY_RANK, CH + P:CH + 2 * P], m.dw1[:, k, :], xf[:, 0, k, :],
                                     start=(k == 0), stop=(k == KH - 1))
                last.then_inc(FE["d"], 1)
                yield 11
                for name, f, w, base in (("r", 3, m.wr, 0), ("k", 1, m.wk, CH)):
                    pe.wait_ge(*FP(f"add{f}", t))
                    for o in range(KH):
                        for k in range(KH):
                            last = pe.matmul(xbank[:, base + o * P:base + (o + 1) * P],
                                             w[:, k, o * P:(o + 1) * P], xf[:, f, k, :], start=(k == 0),
                                             stop=(k == KH - 1))
                    last.then_inc(FE[name], 1)
                yield 13
                pe.wait_ge(*FA("dt", t))
                if followed(t):
                    pe.wait_ge(*NA("hT", t + 1))
                for k in range(KH):
                    last = pe.matmul(hbank[:, k * P:(k + 1) * P], m.dw2[:, k * P:(k + 1) * P], dt_[:, :],
                                     start=True, stop=True)
                last.then_inc(FE["w"], 1)
                yield 15
                pe.wait_ge(*FP("add2", t))
                pe.wait_ge(*FA("k", t))
                for k in range(KH):
                    last = pe.matmul(xbank[:, 0:CH], xf[:, 2, k, :], m.wv[:, k, :], start=(k == 0),
                                     stop=(k == KH - 1))
                last.then_inc(FE["v"], 1)

            def products(out, keys, queries, base=0, half=STEPS):
                for k in range(KH):
                    for b in range(BATCH):
                        keyed = slice(b * STEPS, b * STEPS + half)
                        asked = slice((b + 1) * STEPS - half, (b + 1) * STEPS)
                        for q in range(2):
                            ch = slice(q * HEAD, (q + 1) * HEAD)
                            last = pe.matmul(out[q][keyed, base + (k + 1) * STEPS - half:base + (k + 1) * STEPS],
                                             keys[ch, k, keyed], queries[ch, k, asked], start=True, stop=True)
                return last

            def levels(c):
                def chain(t, slot, turn):
                    for j, step in enumerate(((3, 10, 14), (0, 4, 12))[c]):
                        i = 3 * c + j
                        yield step
                        if i == 0:
                            pe.wait_ge(*FA("v", t))
                        elif j:
                            pe.wait_ge(*LD[c](f"rp{i - 1}", t))
                            pe.wait_ge(*LP[c](f"kq{i - 1}", t))
                            if i < 5:
                                pe.wait_ge(*LD[c](f"cp{i - 1}b", t))
                        else:
                            pe.wait_ge(*LD[0]("cp2b", t))
                            pe.wait_ge(*LP[0]("kq2", t))
                        if j == 0 and begun(t, 1):
                            pe.wait_ge(*LD[c](("cp2b", "cp5b")[c], t - 1))
                        pe.sem_inc(passed["pe"], 1)
                        if i == 0:
                            products(lbank[0], kq[slot], ru[slot], P)
                        products(lbank[c], kq[slot], rp[slot], 0, LEVELS[5] if i == 5 else STEPS)\
                            .then_inc(LE[c][f"l{i}"], 1)
                return chain

            def output(t, slot, turn):
                yield 1
                pe.wait_ge(*LP[1]("kq5", t))
                if begun(t, 1):
                    pe.wait_ge(*YD("state", t - 1))
                for k in range(KH):
                    last = pe.transpose(kvbank[:, k * P:(k + 1) * P], kq[slot][:, k, :], m.ident[:, :])
                last.then_inc(YE["kT"], 1)
                yield 7
                pe.wait_ge(*YA("kt1", t))
                for k in range(KH):
                    for b in range(BATCH):
                        for q in range(2):
                            ch = slice(k * P + q * HEAD, k * P + (q + 1) * HEAD)
                            n = k * BATCH + b
                            last = pe.matmul(kvbank[q * HEAD:(q + 1) * HEAD, CH + n * HEAD:CH + (n + 1) * HEAD],
                                             kt[:, b, ch], vt[slot][:, ch], start=True, stop=True)
                last.then_inc(YE["kv"], 1)
                yield 8
                pe.wait_ge(*YA("sblk1", t))
                pe.wait_ge(*LD[1]("rp5", t))
                if begun(t, 1):
                    pe.wait_ge(*YA("y", t - 1))
                for hd in range(HEADS):
                    pe.matmul(ybank[:, hd * HEAD:(hd + 1) * HEAD], blk[:, hd, :],
                              vt[slot][:, hd * HEAD:(hd + 1) * HEAD], start=(hd == 0), stop=False,
                              skip_group_check=True)
                for k in range(KH):
                    for b in range(BATCH):
                        tok = slice(b * STEPS, (b + 1) * STEPS)
                        last = pe.matmul(ybank[tok, k * P:(k + 1) * P], rp[slot][:, k, tok], sblk[:, k * BATCH + b, :],
                                         start=False, stop=True, skip_group_check=True)
                last.then_inc(YE["y"], 1)

            run_pipeline(pe, [(output, 4), (levels(1), 3), (levels(0), 2), (mix, 1), (norm, 0)], TILES, S)


def ffn_and_training(nc, m, r, a):
    ctx = ExitStack()
    with ctx:
        def sb(name, shape, dt=FP32):
            return ctx.enter_context(nc.sbuf_tensor(name, shape, dt))

        def sem(name):
            return ctx.enter_context(nc.semaphore(name))

        S = 4

        def slots(name, shape):
            return [sb(f"{name}_{s}", shape) for s in range(S)]

        s1 = sb("b_s1", [P, HEADS])
        yc = sb("b_yc", [P, CH])
        sq = sb("b_sq", [P, CH])
        s2 = sb("b_s2", [P, HEADS])
        vh = sb("b_vh", [P, HEADS])
        rh = sb("b_rh", [P, HEADS])
        yn = sb("b_yn", [P, CH])
        ynT = sb("b_ynT", [P, KH, P])
        xb = sb("b_xb", [P, CH])
        t1 = sb("b_t1", [P, CH])
        x1 = slots("b_x1", [P, CH])
        x1b = sb("b_x1b", [P, CH])
        h2 = sb("b_h2", [P, CH])
        h2T = sb("b_h2T", [P, KH, P])
        t2 = sb("b_t2", [P, CH])
        x2 = slots("b_x2", [P, CH])
        h3 = slots("b_h3", [P, CH])
        h3T = slots("b_h3T", [P, KH, P])
        v3 = slots("b_v3", [P, CH])
        x3 = slots("b_x3", [P, CH])
        h4 = sb("b_h4", [P, CH])
        h4T = sb("b_h4T", [P, KH, P])
        stats = [sb(f"b_stats{i}", [P, 6]) for i in range(3)]
        mv = [sb(f"b_mv{i}", [P, 2]) for i in range(3)]
        ve = [sb(f"b_ve{i}", [P, 1]) for i in range(3)]
        rstd = [sb(f"b_rstd{i}", [P, 1]) for i in range(3)]
        xm = [sb(f"b_xm{i}", [P, CH]) for i in range(3)]
        p0 = sb("b_p0", [P, 2, P])
        pw = [sb(f"b_pw{s}", [P, 2, P]) for s in range(2)]
        inv = slots("b_inv", [P, P])
        diff = sb("b_diff", [P, CH])
        es = sb("b_es", [P, CH])
        yl = sb("b_yl", [P, CH])
        t3 = sb("b_t3", [P, CH])
        wt = m.w0t

        ZERO_ROWS, ZERO_PARTS = 80, 24
        zero_size = NSLOT * CH // ZERO_ROWS // ZERO_PARTS
        zero = sb("b_zero", [ZERO_ROWS, zero_size])
        zeroed, cleared = sem("b_zeroed"), sem("b_cleared")

        passed = {e: sem(f"b_passed_{e}") for e in ("dve", "pool", "act")}
        HD = Steps(sem("heads_dve"), "s1 yc s2 yn t1 x1")
        HP = Steps(sem("heads_pool"), "sq xb vh rh")
        HA = Steps(sem("heads_act"), "ynT")
        HE = Steps(sem("heads_pe"), "ynT z")
        FD = Steps(sem("ffn_dve"), "stats mv xm h t2 x2")
        FP = Steps(sem("ffn_pool"), "x1b ve rstd")
        FA = Steps(sem("ffn_act"), "h2T")
        FE = Steps(sem("ffn_pe"), "h2T f")
        VD = Steps(sem("value_dve"), "stats mv xm h v")
        VP = Steps(sem("value_pool"), "ve rstd")
        VA = Steps(sem("value_act"), "h3T")
        VE = Steps(sem("value_pe"), "h3T v")
        MD = Steps(sem("inverse_dve"), "p pT t0 " + " ".join(f"t{j}" for j in range(1, 6)))
        MA = Steps(sem("inverse_act"), " ".join(f"pw{j}" for j in range(1, 6)))
        ME = Steps(sem("inverse_pe"), "g sq1 " + " ".join(f"sq{j + 1} up{j}" for j in range(1, 5)) + " up5")
        BD = Steps(sem("train_dve"), "diff yl")
        BP = Steps(sem("train_pool"), "t3 x3")
        BA = Steps(sem("train_act"), "es w")
        BE = Steps(sem("train_pe"), "xw err dw")
        RD = Steps(sem("route_dve"), "stats mv xm h logits")
        RP = Steps(sem("route_pool"), "ve rstd")
        RA = Steps(sem("route_act"), "h4T keep x3")
        RE = Steps(sem("route_pe"), "h4T logits")
        block = ctx.enter_context(nc.Block())
        hbank, fbank, vbank, sqbank, upbank, ebank, wbank, rbank = m.bank
        CHAINS = dict(heads=0, ffn=1, value=2, gram=2, inverse=3, train=4, route=5)

        def at(stream, t):
            return stream[:, bass.ds(t, 1), :].rearrange("p a c -> p (a c)")

        def heads_of(ap):
            return ap.rearrange("p (h i) -> p h i", h=HEADS)

        def spread(ap, n):
            return ap.rearrange("p (h one) -> p h one", one=1).to_broadcast([P, ap.shape[1], n])

        def in_order(*parts):
            return sorted(((f, CHAINS[f.__name__]) for f in parts), key=lambda c: -c[1])

        @block.sync
        def _(sp):
            load_w1(sp, nc, m, a, 0, 0)
            load_w2(sp, m, a, 0, 0)
            sp.wait_ge(zeroed, 1)
            slots_ = r.sent[0:NSLOT, :].rearrange("(p a) c -> p (a c)", p=ZERO_ROWS)
            for i in range(ZERO_PARTS):
                sp.dma_start(slots_[:, i * zero_size:(i + 1) * zero_size], zero[:, :]).then_inc(cleared, 16)
            sp.wait_ge(cleared, 16 * ZERO_PARTS)

        @block.gpsimd
        def _(pool):
            pool.memset(zero[:, :], 0.0).then_inc(zeroed, 1)

            def heads(t, slot, turn):
                yield 3
                pool.wait_ge(*HD("yc", t))
                pool.tensor_tensor(sq[:, :], yc[:, :], yc[:, :], ALU.mult).then_inc(HP["sq"], 1)
                pool.tensor_tensor(xb[:, :], at(m.x, t), m.wob[:, :], ALU.add).then_inc(HP["xb"], 1)
                yield 4
                pool.wait_ge(*HD("s2", t))
                pool.tensor_tensor(vh[:, :], s2[:, :], m.head_eps[:, :], ALU.add).then_inc(HP["vh"], 1)
                pool.wait_ge(*HP("vh", t))
                pool.tensor_tensor(rh[:, :], vh[:, :], m.half[:, :], ALU.pow).then_inc(HP["rh"], 1)

            def ffn(t, slot, turn):
                yield 0
                pool.wait_ge(*HD("x1", t))
                if begun(t, 1):
                    pool.wait_ge(*FD("x2", t - 1))
                pool.tensor_tensor(x1b[:, :], x1[slot][:, :], m.bf[:, :], ALU.add).then_inc(FP["x1b"], 1)
                yield 2
                pool.wait_ge(*FD("mv", t))
                pool.tensor_tensor(ve[0][:, :], mv[0][:, 1:2], m.eps[:, :], ALU.add).then_inc(FP["ve"], 1)
                pool.wait_ge(*FP("ve", t))
                pool.tensor_tensor(rstd[0][:, :], ve[0][:, :], m.half[:, 0:1], ALU.pow).then_inc(FP["rstd"], 1)

            def value(t, slot, turn):
                yield 1
                pool.wait_ge(*VD("mv", t))
                pool.tensor_tensor(ve[1][:, :], mv[1][:, 1:2], m.eps[:, :], ALU.add).then_inc(VP["ve"], 1)
                pool.wait_ge(*VP("ve", t))
                pool.tensor_tensor(rstd[1][:, :], ve[1][:, :], m.half[:, 0:1], ALU.pow).then_inc(VP["rstd"], 1)

            def train(t, slot, turn):
                yield 6
                pool.wait_ge(*BD("yl", t))
                pool.tensor_tensor(t3[:, :], yl[:, :], m.mod[1][:, 2, :], ALU.mult).then_inc(BP["t3"], 1)
                pool.wait_ge(*BP("t3", t))
                pool.tensor_tensor(x3[slot][:, :], t3[:, :], x2[slot][:, :], ALU.add).then_inc(BP["x3"], 1)

            def route(t, slot, turn):
                yield 5
                pool.wait_ge(*RD("mv", t))
                pool.tensor_tensor(ve[2][:, :], mv[2][:, 1:2], m.eps[:, :], ALU.add).then_inc(RP["ve"], 1)
                pool.wait_ge(*RP("ve", t))
                pool.tensor_tensor(rstd[2][:, :], ve[2][:, :], m.half[:, 0:1], ALU.pow).then_inc(RP["rstd"], 1)

            run_pipeline(pool, in_order(heads, ffn, value, train, route), TILES, S)

        @block.vector
        def _(dve):
            def heads(t, slot, turn):
                y = at(m.y, t)
                yield 3
                dve.tensor_reduce(s1[:, :], heads_of(y), AX.X, ALU.add).then_inc(HD["s1"], 1)
                dve.wait_ge(*HD("s1", t))
                dve.sem_inc(passed["dve"], 1)
                dve.scalar_tensor_tensor(heads_of(yc[:, :]), spread(s1[:, :], HEAD), -1.0 / HEAD, heads_of(y), ALU.mult,
                                         ALU.add).then_inc(HD["yc"], 1)
                yield 9
                dve.wait_ge(*HP("sq", t))
                dve.tensor_reduce(s2[:, :], heads_of(sq[:, :]), AX.X, ALU.add).then_inc(HD["s2"], 1)
                yield 12
                dve.wait_ge(*HP("rh", t))
                dve.sem_inc(passed["dve"], 1)
                dve.scalar_tensor_tensor(heads_of(yn[:, :]), spread(rh[:, :], HEAD), HEAD ** 0.5, heads_of(yc[:, :]),
                                         ALU.mult, ALU.mult).then_inc(HD["yn"], 1)
                yield 18
                dve.wait_ge(*HE("z", t))
                dve.tensor_tensor(t1[:, :], hbank[:, CH:2 * CH], m.mod[0][:, 2, :], ALU.mult).then_inc(HD["t1"], 1)
                dve.wait_ge(*HD("t1", t))
                dve.wait_ge(*HP("xb", t))
                dve.tensor_tensor(x1[slot][:, :], t1[:, :], xb[:, :], ALU.add).then_inc(HD["x1"], 1)

            def norm(steps, i, x, scale, t):
                dve.bn_stats(stats[i][:, :], x).then_inc(steps["stats"], 1)
                dve.wait_ge(*steps("stats", t))
                dve.sem_inc(passed["dve"], 1)
                dve.bn_aggr(mv[i][:, :], stats[i][:, :]).then_inc(steps["mv"], 1)
                dve.wait_ge(*steps("mv", t))
                dve.scalar_tensor_tensor(xm[i][:, :], x, mv[i][:, 0:1], scale, ALU.subtract, ALU.mult)\
                   .then_inc(steps["xm"], 1)

            def ffn(t, slot, turn):
                yield 2
                dve.wait_ge(*HD("x1", t))
                norm(FD, 0, x1[slot][:, :], m.mod[0][:, 4, :], t)
                yield 5
                dve.wait_ge(*FP("rstd", t))
                dve.wait_ge(*FD("xm", t))
                dve.scalar_tensor_tensor(h2[:, :], xm[0][:, :], rstd[0][:, 0:1], m.mod[0][:, 3, :], ALU.mult, ALU.add)\
                   .then_inc(FD["h"], 1)
                yield 14
                dve.wait_ge(*FE("f", t))
                dve.tensor_tensor(t2[:, :], fbank[:, CH:2 * CH], m.mod[0][:, 5, :], ALU.mult).then_inc(FD["t2"], 1)
                dve.wait_ge(*FD("t2", t))
                dve.wait_ge(*FP("x1b", t))
                dve.tensor_tensor(x2[slot][:, :], t2[:, :], x1b[:, :], ALU.add).then_inc(FD["x2"], 1)

            def value(t, slot, turn):
                yield 1
                dve.wait_ge(*FD("x2", t))
                norm(VD, 1, x2[slot][:, :], m.mod[1][:, 1, :], t)
                yield 6
                dve.wait_ge(*VP("rstd", t))
                dve.wait_ge(*VD("xm", t))
                dve.scalar_tensor_tensor(h3[slot][:, :], xm[1][:, :], rstd[1][:, 0:1], m.mod[1][:, 0, :], ALU.mult,
                                         ALU.add).then_inc(VD["h"], 1)
                yield 17
                dve.wait_ge(*VE("v", t))
                dve.tensor_tensor(v3[slot][:, :], vbank[:, CH:2 * CH], m.bv[:, :], ALU.add).then_inc(VD["v"], 1)

            def inverse(t, slot, turn):
                yield 0
                dve.wait_ge(*ME("g", t))
                dve.scalar_tensor_tensor(p0[:, 0, :], sqbank[:, 0:P], m.nbeta[:, 0:1], m.earlier[:, :], ALU.mult,
                                         ALU.mult).then_inc(MD["p"], 1)
                dve.scalar_tensor_tensor(p0[:, 1, :], sqbank[:, 0:P], m.nbeta[:, 0:1], m.later[:, :], ALU.mult,
                                         ALU.mult).then_inc(MD["pT"], 1)
                dve.wait_ge(*MD("pT", t))
                dve.tensor_tensor(inv[slot][:, :], p0[:, 1, :], m.ident[:, :], ALU.add).then_inc(MD["t0"], 1)
                for j in range(1, 6):
                    yield (4, 8, 11, 16, 20)[j - 1]
                    dve.wait_ge(*ME(f"up{j}", t))
                    dve.tensor_tensor(inv[slot][:, :], upbank[:, 0:P], inv[slot][:, :], ALU.add)\
                       .then_inc(MD[f"t{j}"], 1)

            def train(t, slot, turn):
                yield 7
                dve.wait_ge(*BE("xw", t))
                dve.tensor_tensor(diff[:, :], ebank[:, 0:CH], v3[slot][:, :], ALU.subtract).then_inc(BD["diff"], 1)
                yield 15
                dve.wait_ge(*BA("es", t))
                dve.tensor_tensor(yl[:, :], ebank[:, CH:2 * CH], v3[slot][:, :], ALU.add).then_inc(BD["yl"], 1)

            def route(t, slot, turn):
                yield 10
                dve.wait_ge(*BP("x3", t))
                norm(RD, 2, x3[slot][:, :], m.mod[1][:, 4, :], t)
                yield 13
                dve.wait_ge(*RP("rstd", t))
                dve.wait_ge(*RD("xm", t))
                dve.scalar_tensor_tensor(h4[:, :], xm[2][:, :], rstd[2][:, 0:1], m.mod[1][:, 3, :], ALU.mult, ALU.add)\
                   .then_inc(RD["h"], 1)
                yield 19
                dve.wait_ge(*RE("logits", t))
                dve.sem_inc(passed["dve"], 1)
                dve.tensor_tensor(at(m.logits, t), rbank[:, CH:CH + EXPERTS], m.bg[:, :], ALU.add)\
                   .then_inc(RD["logits"], 1)

            run_pipeline(dve, in_order(heads, ffn, value, inverse, train, route), TILES, S)

        @block.scalar
        def _(act):
            def halves(bank):
                return bank[:, 0:CH].rearrange("p (k s) -> p k s", k=KH)

            def heads(t, slot, turn):
                yield 8
                act.wait_ge(*HE("ynT", t))
                act.activation(ynT[:, :, :], halves(hbank), ACT.Copy).then_inc(HA["ynT"], 1)

            def ffn(t, slot, turn):
                yield 3
                act.wait_ge(*FE("h2T", t))
                act.activation(h2T[:, :, :], halves(fbank), ACT.Copy).then_inc(FA["h2T"], 1)

            def value(t, slot, turn):
                yield 5
                act.wait_ge(*VE("h3T", t))
                act.activation(h3T[slot][:, :, :], halves(vbank), ACT.Copy).then_inc(VA["h3T"], 1)

            def inverse(t, slot, turn):
                for j in range(1, 6):
                    yield (0, 1, 2, 4, 6)[j - 1]
                    act.wait_ge(*ME(f"sq{j}", t))
                    n = 2 if j < 5 else 1
                    act.activation(pw[j % 2][:, 0:n, :], sqbank[:, 0:n * P].rearrange("p (n s) -> p n s", n=n),
                                   ACT.Copy).then_inc(MA[f"pw{j}"], 1)

            def train(t, slot, turn):
                yield 7
                act.wait_ge(*BE("err", t))
                act.activation(es[:, :], ebank[:, CH:2 * CH], ACT.Copy, scale=m.nbeta[:, 0:1]).then_inc(BA["es"], 1)
                yield 10
                act.wait_ge(*BE("dw", t))
                act.activation(wt[:, :, :], wbank[:, :].rearrange("p (k c) -> p k c", k=KH), ACT.Copy)\
                   .then_inc(BA["w"], 1)

            def route(t, slot, turn):
                yield 9
                act.wait_ge(*RE("h4T", t))
                act.activation(h4T[:, :, :], halves(rbank), ACT.Copy).then_inc(RA["h4T"], 1)
                act.activation(at(m.y, t), h4[:, :], ACT.Copy).then_inc(RA["keep"], 1)
                act.activation(at(m.x, t), x3[slot][:, :], ACT.Copy).then_inc(RA["x3"], 1)

            run_pipeline(act, in_order(heads, ffn, value, inverse, train, route), TILES, S)

        @block.tensor
        def _(pe):
            for k in range(KH):
                pe.matmul(wbank[:, k * CH:(k + 1) * CH], m.ident[:, :], m.w0t[:, k, :], start=(k == 0), stop=False,
                          skip_group_check=True)

            def turned(out, src):
                for k in range(KH):
                    last = pe.transpose(out[:, k * P:(k + 1) * P], src[:, k * P:(k + 1) * P], m.ident[:, :])
                return last

            def project(out, lhs, w):
                for k in range(KH):
                    last = pe.matmul(out, lhs[:, k, :], w[:, k, :], start=(k == 0), stop=(k == KH - 1))
                return last

            def heads(t, slot, turn):
                yield 10
                pe.wait_ge(*HD("yn", t))
                turned(hbank, yn).then_inc(HE["ynT"], 1)
                yield 13
                pe.wait_ge(*HA("ynT", t))
                project(hbank[:, CH:2 * CH], ynT, m.wo).then_inc(HE["z"], 1)

            def ffn(t, slot, turn):
                yield 4
                pe.wait_ge(*FD("h", t))
                turned(fbank, h2).then_inc(FE["h2T"], 1)
                yield 7
                pe.wait_ge(*FA("h2T", t))
                project(fbank[:, CH:2 * CH], h2T, m.wf).then_inc(FE["f"], 1)

            def value(t, slot, turn):
                yield 5
                pe.wait_ge(*VD("h", t))
                turned(vbank, h3[slot]).then_inc(VE["h3T"], 1)
                yield 11
                pe.wait_ge(*VA("h3T", t))
                project(vbank[:, CH:2 * CH], h3T[slot], m.wvt).then_inc(VE["v"], 1)

            def gram(t, slot, turn):
                yield 16
                pe.wait_ge(*VA("h3T", t))
                if begun(t, 1):
                    pe.wait_ge(*MA("pw5", t - 1))
                for k in range(KH):
                    last = pe.matmul(sqbank[:, 0:P], h3T[slot][:, k, :], h3T[slot][:, k, :], start=(k == 0),
                                     stop=(k == KH - 1))
                last.then_inc(ME["g"], 1)

            def inverse(t, slot, turn):
                for j in range(1, 6):
                    yield (0, 1, 3, 6, 9)[j - 1]
                    src = p0 if j == 1 else pw[(j - 1) % 2]
                    if j == 1:
                        pe.wait_ge(*MD("t0", t))
                    else:
                        pe.wait_ge(*MA(f"pw{j - 1}", t))
                    last = pe.matmul(sqbank[:, 0:P], src[:, 1, :], src[:, 0, :], start=True, stop=True)
                    if j < 5:
                        last = pe.matmul(sqbank[:, P:2 * P], src[:, 0, :], src[:, 1, :], start=True, stop=True)
                    last.then_inc(ME[f"sq{j}"], 1)
                    if j > 1:
                        pe.wait_ge(*MD(f"t{j - 2}", t))
                        pe.matmul(upbank[:, 0:P], src[:, 0, :], inv[slot][:, :], start=True, stop=True)\
                          .then_inc(ME[f"up{j - 1}"], 1)
                yield 14
                pe.wait_ge(*MA("pw5", t))
                pe.wait_ge(*MD("t4", t))
                pe.matmul(upbank[:, 0:P], pw[1][:, 0, :], inv[slot][:, :], start=True, stop=True)\
                  .then_inc(ME["up5"], 1)

            def train(t, slot, turn):
                yield 2
                if begun(t, 1):
                    pe.wait_ge(*BA("w", t - 1))
                    pe.wait_ge(*BD("yl", t - 1))
                pe.wait_ge(*VD("v", t))
                project(ebank[:, 0:CH], h3T[slot], wt).then_inc(BE["xw"], 1)
                yield 8
                pe.wait_ge(*BD("diff", t))
                pe.wait_ge(*MD("t5", t))
                pe.matmul(ebank[:, CH:2 * CH], inv[slot][:, :], diff[:, :], start=True, stop=True)\
                  .then_inc(BE["err"], 1)
                yield 17
                pe.wait_ge(*BA("es", t))
                for k in range(KH):
                    last = pe.matmul(wbank[:, k * CH:(k + 1) * CH], h3[slot][:, k * P:(k + 1) * P], es[:, :],
                                     start=False, stop=False, skip_group_check=True)
                last.then_inc(BE["dw"], 1)

            def route(t, slot, turn):
                yield 12
                pe.wait_ge(*RD("h", t))
                turned(rbank, h4).then_inc(RE["h4T"], 1)
                yield 15
                pe.wait_ge(*RA("keep", t))
                for k in range(KH):
                    last = pe.matmul(rbank[:, CH:CH + EXPERTS], h4T[:, k, :], m.wg[:, k, :], start=(k == 0),
                                     stop=(k == KH - 1))
                last.then_inc(RE["logits"], 1)

            run_pipeline(pe, in_order(heads, ffn, value, gram, inverse, train, route), TILES, S)


def routing(nc, m, r):
    ctx = ExitStack()
    with ctx:
        def sb(name, shape, dt=FP32):
            return ctx.enter_context(nc.sbuf_tensor(name, shape, dt))

        E, T = EXPERTS, TILES
        KET = TOPK * E * T
        number = sb("c_number", [P, T, E], I32)
        ones = sb("c_ones", [P, P])
        eight = sb("c_eight", [P, T, E])
        base = sb("c_base", [P, E])
        own = sb("c_own", [P, TOPK, T])
        owni = sb("c_owni", [P, TOPK, T], I32)
        best = [sb(f"c_best{k}", [P, T]) for k in range(TOPK)]
        eq = sb("c_eq", [P, T, E])
        first = sb("c_first", [P, T])
        oh = [sb(f"c_oh{k}", [P, T, E]) for k in range(TOPK)]
        rest = sb("c_rest", [P, T, E])
        gap = sb("c_gap", [P, T])
        expg = sb("c_expg", [P, T])
        den = sb("c_den", [P, T])
        ohs = sb("c_ohs", [P, TOPK, E, T], FP32R)
        same = sb("c_same", [P, P], FP32R)
        before = sb("c_before", [P, P], FP32R)
        prior = sb("c_prior", [P, P], FP32R)
        every = sb("c_every", [P, P], FP32R)
        keepon = sb("c_keepon", [P, TOPK, E, T])
        tiles_ = sb("c_tiles", [P, KET])
        upto = sb("c_upto", [P, KET])
        pos = sb("c_pos", [P, TOPK, E, T])
        batch0 = sb("c_batch0", [P, TOPK * E])
        choice0 = sb("c_choice0", [P, E])
        picked = sb("c_picked", [P, TOPK, E, T])
        spot = sb("c_spot", [P, TOPK, T])
        keep = sb("c_keep", [P, TOPK, T])
        row = sb("c_row", [P, TOPK, T])
        dest = sb("c_dest", [P, TOPK, T])

        done = ctx.enter_context(nc.semaphore("c_dve"))
        made = ctx.enter_context(nc.semaphore("c_pool"))
        counted = ctx.enter_context(nc.semaphore("c_pe"))
        expd = ctx.enter_context(nc.semaphore("c_act"))
        block = ctx.enter_context(nc.Block())
        marks = {}

        @block.gpsimd
        def _(pool):
            pool.iota(number[:, :, :], pattern=[[0, T], [1, E]], base=0, channel_multiplier=0)
            pool.iota(owni[:, :, :], pattern=[[T * P, TOPK], [P, T]], base=DROPPED, channel_multiplier=1)
            pool.memset(ones[:, :], 1.0)
            pool.memset(keepon[:, :, :, 1:T], 1.0)
            pool.memset(keepon[:, :, :, 0:1], 0.0).then_inc(made, 1)

        @block.vector
        def _(dve):
            state = [0]

            def then(ins):
                ins.then_inc(done, 1)
                state[0] += 1
                dve.wait_ge(done, state[0])
                return state[0]

            def over_e(ap):
                return ap.rearrange("p (t one) -> p t one", one=1).to_broadcast([P, T, E])

            def by_expert(ap):
                return ap.rearrange("p t e -> p e t")

            dve.wait_ge(made, 1)
            then(dve.tensor_copy(own[:, :, :], owni[:, :, :]))
            dve.tensor_scalar(base[:, :], number[:, 0, :], float(SLOTS), None, ALU.mult)
            then(dve.tensor_scalar(eight[:, :, :], number[:, :, :], -1.0, float(E), ALU.mult, ALU.add))
            scores = m.logits
            for k in range(TOPK):
                then(dve.tensor_reduce(best[k][:, :], scores[:, :, :], AX.X, ALU.max))
                then(dve.tensor_tensor(eq[:, :, :], scores[:, :, :], over_e(best[k][:, :]), ALU.is_equal))
                then(dve.tensor_tensor(eq[:, :, :], eq[:, :, :], eight[:, :, :], ALU.mult))
                then(dve.tensor_reduce(first[:, :], eq[:, :, :], AX.X, ALU.max))
                then(dve.tensor_tensor(oh[k][:, :, :], eight[:, :, :], over_e(first[:, :]), ALU.is_equal))
                then(dve.tensor_copy(ohs[:, k, :, :], by_expert(oh[k][:, :, :])))
                if k == 0:
                    then(dve.scalar_tensor_tensor(rest[:, :, :], oh[0][:, :, :], -3e38, m.logits[:, :, :], ALU.mult,
                                                  ALU.add))
                    scores = rest
            for b in range(BATCH):
                cols = slice(b * STEPS, (b + 1) * STEPS)
                then(dve.tensor_scalar(same[:, cols], ones[:, cols], m.side[:, b:b + 1], None, ALU.mult))
            then(dve.tensor_tensor(before[:, :], same[:, :], m.later[:, :], ALU.mult))
            dve.tensor_scalar(prior[:, 0:STEPS], ones[:, 0:STEPS], 0.0, None, ALU.mult)
            dve.tensor_copy(every[:, :], ones[:, :])
            then(dve.tensor_scalar(prior[:, STEPS:P], ones[:, STEPS:P], m.side[:, 0:1], None, ALU.mult))
            marks["pe"] = state[0]
            marks["gap"] = then(dve.tensor_tensor(gap[:, :], best[1][:, :], best[0][:, :], ALU.subtract))
            dve.wait_ge(expd, 1)
            then(dve.tensor_scalar_add(den[:, :], expg[:, :], 1.0))
            then(dve.reciprocal(m.gate[:, 0, :], den[:, :]))
            then(dve.tensor_tensor(m.gate[:, 1, :], m.gate[:, 0, :], expg[:, :], ALU.mult))
            dve.wait_ge(counted, 4)
            then(dve.tensor_copy(tiles_[:, :], m.bank[1][:, :]))
            then(dve.tensor_tensor_scan(upto[:, :], keepon[:, :, :, :].rearrange("p k e t -> p (k e t)"), tiles_[:, :],
                                        0.0, ALU.mult, ALU.add))
            flat = pos[:, :, :, :].rearrange("p k e t -> p (k e t)")
            then(dve.tensor_tensor(flat, upto[:, :], tiles_[:, :], ALU.subtract))
            then(dve.tensor_tensor(flat, m.bank[0][:, :], flat, ALU.add))
            then(dve.tensor_reduce(batch0[:, :], m.bank[2][:, :].rearrange("p (n t) -> p n t", t=T), AX.X, ALU.add))
            then(dve.tensor_reduce(choice0[:, :], m.bank[3][:, 0:E * T].rearrange("p (n t) -> p n t", t=T), AX.X,
                                   ALU.add))
            pket = pos[:, :, :, :].rearrange("p k e t -> p (k e) t")
            then(dve.tensor_tensor(pket, pket, batch0[:, :].rearrange("p (n one) -> p n one", one=1)
                                   .to_broadcast([P, TOPK * E, T]), ALU.add))
            then(dve.tensor_tensor(pos[:, 1, :, :], pos[:, 1, :, :], choice0[:, :].rearrange("p (n one) -> p n one", one=1)
                                   .to_broadcast([P, E, T]), ALU.add))
            for k in range(TOPK):
                then(dve.tensor_tensor(picked[:, k, :, :], pos[:, k, :, :], ohs[:, k, :, :], ALU.mult))
                then(dve.tensor_reduce(spot[:, k, :], picked[:, k, :, :].rearrange("p e t -> p t e"), AX.X, ALU.add))
                then(dve.tensor_tensor(picked[:, k, :, :], ohs[:, k, :, :],
                                       base[:, :].rearrange("p (n one) -> p n one", one=1).to_broadcast([P, E, T]),
                                       ALU.mult))
                then(dve.tensor_reduce(row[:, k, :], picked[:, k, :, :].rearrange("p e t -> p t e"), AX.X, ALU.add))
            then(dve.tensor_tensor(row[:, :, :], row[:, :, :], spot[:, :, :], ALU.add))
            then(dve.tensor_scalar(keep[:, :, :], spot[:, :, :], float(CAPACITY), None, ALU.is_lt))
            then(dve.tensor_tensor(m.gate[:, :, :], m.gate[:, :, :], keep[:, :, :], ALU.mult))
            then(dve.tensor_tensor(dest[:, :, :], row[:, :, :], own[:, :, :], ALU.subtract))
            then(dve.tensor_tensor(dest[:, :, :], dest[:, :, :], keep[:, :, :], ALU.mult))
            then(dve.tensor_tensor(dest[:, :, :], dest[:, :, :], own[:, :, :], ALU.add))
            then(dve.tensor_copy(m.put[:, :, :], dest[:, :, :]))
            then(dve.tensor_tensor(row[:, :, :], row[:, :, :], keep[:, :, :], ALU.mult))
            then(dve.tensor_copy(m.get[:, :, :], row[:, :, :]))

        @block.scalar
        def _(act):
            act.wait_ge(done, marks["gap"])
            act.activation(expg[:, :], gap[:, :], ACT.Exp).then_inc(expd, 1)

        @block.tensor
        def _(pe):
            pe.wait_ge(made, 1)
            pe.wait_ge(done, marks["pe"])
            chosen = ohs[:, :, :, :].rearrange("p k e t -> p (k e t)")
            for i, mask in enumerate((before, same, prior, every)):
                pe.matmul(m.bank[i][:, :], mask[:, :], chosen, start=True, stop=True).then_inc(counted, 1)


def experts(nc, m, r, a):
    ctx = ExitStack()
    with ctx:
        def sb(name, shape, dt=FP32):
            return ctx.enter_context(nc.sbuf_tensor(name, shape, dt))

        def sem(name):
            return ctx.enter_context(nc.semaphore(name))

        def pair(name, shape):
            return [sb(f"{name}_{part}", shape, FP32R) for part in ("upper", "lower")]

        SPLIT = ((0, ROWS // 16 * 16), (ROWS // 16 * 16, ROWS))
        w1 = pair("d_w1", [P, KH, HIDDEN])
        w2 = pair("d_w2", [P, FT, CH])
        rows = [sb(f"d_rows{s}", [ROWS, 2, CH]) for s in range(2)]
        xg = [pair(f"d_xg{s}", [P, KH * GROUP]) for s in range(2)]
        hid = sb("d_hid", [P, FT, GROUP])
        hs = [pair(f"d_hid{s}", [P, FT, GROUP]) for s in range(2)]
        res = [sb(f"d_res{s}", [ROWS, 2, CH]) for s in range(2)]
        PARTS = ((0, 0), (1, 0), (0, 1))

        put_done = sem("d_put")
        rows_in = [sem(f"d_rows_in{s}") for s in range(2)]
        res_out = [sem(f"d_res_out{s}") for s in range(2)]
        passed = {e: sem(f"d_passed_{e}") for e in ("dve", "pe", "act")}
        TD = Steps(sem("turn_dve"), "upper lower")
        TE = Steps(sem("turn_pe"), "turned")
        W1A = Steps(sem("w1_act"), "upper0 upper1")
        W1D = Steps(sem("w1_dve"), "lower0 lower1")
        W2A = Steps(sem("w2_act"), "upper0 upper1")
        W2D = Steps(sem("w2_dve"), "lower0 lower1")
        HD = Steps(sem("hidden_dve"), "lower0 lower1 lower2 lower3")
        ED = Steps(sem("expert_dve"), "res")
        EA = Steps(sem("expert_act"), "gelu0 gelu1 gelu2 gelu3 upper0 gelu4 gelu5 upper1 gelu6 gelu7 upper2 upper3")
        EE = Steps(sem("expert_pe"), "up0 up1 up2 up3")
        FE = Steps(sem("down_pe"), "down")
        block = ctx.enter_context(nc.Block())
        N = EXPERTS * GROUPS
        U = 2 * GROUPS

        def expert(slot, turn):
            return turn * 2 + slot // GROUPS

        def comes(e):
            return not isinstance(e, int) or e < EXPERTS

        def halves(ap, i):
            n = ap.shape[1] // 2
            return ap[:, i * n:(i + 1) * n, :].rearrange("p k c -> p (k c)")

        @block.gpsimd
        def _(pool):
            for k in range(TOPK):
                for t in range(TILES):
                    pool.indirect_dma_start(
                        out=r.sent[:, :], out_offset=bass.IndirectOffsetOnAxis(ap=m.put[:, k, t:t + 1], axis=0),
                        in_=m.y[:, t, :], in_offset=None).then_inc(put_done, 16)

        @block.sync
        def _(sp):
            sp.wait_ge(put_done, 16 * TILES * TOPK)

            def fetch(n, slot, turn):
                yield 0
                if begun(n, 2):
                    sp.wait_ge(*TE("turned", n - 2))
                for lo, hi in SPLIT:
                    sp.dma_start(rows[slot % 2][lo:hi, :, :], r.sent[bass.ds(n * GROUP, GROUP), :]
                                 .rearrange("(a p) c -> p a c", p=ROWS)[lo:hi, :, :]).then_inc(rows_in[slot % 2], 16)

            def weights(n, slot, turn):
                yield 1
                e = expert(slot, turn)
                s = (slot // GROUPS + 1) % 2
                if slot % GROUPS == 1 and comes(e + 1):
                    sp.wait_ge(*W1D("lower1", e))
                    if begun(n, GROUPS):
                        sp.wait_ge(*EA("gelu7", n - 2))
                    load_w1(sp, nc, m, a, e + 1, s)
                if slot % GROUPS == 4 and comes(e + 1):
                    sp.wait_ge(*W2D("lower1", e))
                    if begun(n, GROUPS):
                        sp.wait_ge(*ED("res", n - 5))
                    load_w2(sp, m, a, e + 1, s)

            def store(n, slot, turn):
                yield 2
                sp.wait_ge(*ED("res", n))
                for lo, hi in SPLIT:
                    sp.dma_start(r.back[bass.ds(n * GROUP, GROUP), :].rearrange("(a p) c -> p a c", p=ROWS)[lo:hi, :, :],
                                 res[slot % 2][lo:hi, :, :]).then_inc(res_out[slot % 2], 16)

            run_pipeline(sp, [(fetch, 0), (weights, 1), (store, 4)], N, U)
            for s in range(2):
                sp.wait_ge(res_out[s], 32 * (N // 2))

        @block.vector
        def _(dve):
            def split_w1(n, slot, turn):
                yield 6
                if slot % GROUPS == 0:
                    e = expert(slot, turn)
                    for i in range(2):
                        dve.wait_ge(*W1A(f"upper{i}", e))
                        dve.tensor_tensor(halves(w1[1], i), halves(m.w1, i), halves(w1[0], i), ALU.subtract)\
                           .then_inc(W1D[f"lower{i}"], 1)

            def split_w2(n, slot, turn):
                yield 0
                if slot % GROUPS == 0:
                    e = expert(slot, turn)
                    for i in range(2):
                        dve.wait_ge(*W2A(f"upper{i}", e))
                        dve.tensor_tensor(halves(w2[1], i), halves(m.w2, i), halves(w2[0], i), ALU.subtract)\
                           .then_inc(W2D[f"lower{i}"], 1)

            def turn_in(n, slot, turn):
                yield 7
                dve.wait_ge(*TE("turned", n))
                dve.sem_inc(passed["dve"], 1)
                dve.tensor_copy(xg[slot % 2][0][:, :], m.bank[0][:, 0:KH * GROUP]).then_inc(TD["upper"], 1)
                dve.wait_ge(*TD("upper", n))
                dve.tensor_tensor(xg[slot % 2][1][:, :], m.bank[0][:, 0:KH * GROUP], xg[slot % 2][0][:, :],
                                  ALU.subtract).then_inc(TD["lower"], 1)

            def hidden(n, slot, turn):
                for j in range(4):
                    yield 1 + j
                    fs = slice(2 * j, 2 * j + 2)
                    dve.wait_ge(*EA(f"upper{j}", n))
                    dve.tensor_tensor(hs[slot % 2][1][:, fs, :], hid[:, fs, :], hs[slot % 2][0][:, fs, :],
                                      ALU.subtract).then_inc(HD[f"lower{j}"], 1)

            def result(n, slot, turn):
                yield 1
                s = slot // GROUPS
                dve.wait_ge(*FE("down", n))
                if begun(n, 2):
                    dve.wait_ge(res_out[slot % 2], (turn * (U // 2) + slot // 2) * 32)
                for i in range(2):
                    last = dve.tensor_tensor(res[slot % 2][:, i, :], m.bank[5 + slot % 2][0:ROWS, i * CH:(i + 1) * CH],
                                             m.b2[s][0:ROWS, :], ALU.add)
                last.then_inc(ED["res"], 1)

            run_pipeline(dve, [(split_w2, 2), (result, 3), (hidden, 1), (turn_in, 0), (split_w1, 0)], N, U)

        @block.scalar
        def _(act):
            def split_w1(n, slot, turn):
                yield 8
                if slot % GROUPS == 0:
                    e = expert(slot, turn)
                    act.wait_ge(m.w1_in, e * 32 + 32)
                    if begun(n, 1):
                        act.wait_ge(*EE("up3", n - 1))
                    for i in range(2):
                        act.activation(halves(w1[0], i), halves(m.w1, i), ACT.Copy).then_inc(W1A[f"upper{i}"], 1)

            def split_w2(n, slot, turn):
                yield 0
                if slot % GROUPS == 0:
                    e = expert(slot, turn)
                    act.wait_ge(m.w2_in, e * 32 + 32)
                    if begun(n, 1):
                        act.wait_ge(*FE("down", n - 1))
                    for i in range(2):
                        act.activation(halves(w2[0], i), halves(m.w2, i), ACT.Copy).then_inc(W2A[f"upper{i}"], 1)

            def gelu(n, slot, turn):
                yield 1
                s = slot // GROUPS

                def upper(j):
                    if j == 0 and begun(n, 2):
                        act.wait_ge(*FE("down", n - 2))
                    act.wait_ge(*EA(f"gelu{2 * j + 1}", n))
                    act.activation(hs[slot % 2][0][:, 2 * j:2 * j + 2, :], hid[:, 2 * j:2 * j + 2, :], ACT.Copy)\
                       .then_inc(EA[f"upper{j}"], 1)

                for j in range(4):
                    act.wait_ge(*EE(f"up{j}", n))
                    if begun(n, 1):
                        act.wait_ge(*HD(f"lower{j}", n - 1))
                    for f in (2 * j, 2 * j + 1):
                        act.activation(hid[:, f, :], m.bank[1 + j][:, (f % 2) * GROUP:(f % 2 + 1) * GROUP],
                                       ACT.Gelu_apprx_tanh, bias=m.b1[s][:, f:f + 1]).then_inc(EA[f"gelu{f}"], 1)
                    if j:
                        upper(j - 1)
                upper(3)

            run_pipeline(act, [(split_w2, 2), (gelu, 1), (split_w1, 0)], N, U)

        @block.tensor
        def _(pe):
            def turn_in(n, slot, turn):
                yield 1
                pe.wait_ge(rows_in[slot % 2], (turn * (U // 2) + (slot // 2 + 1)) * 32)
                if begun(n, 1):
                    pe.wait_ge(*TD("lower", n - 1))
                for k in range(KH):
                    for i in range(2):
                        last = pe.transpose(m.bank[0][:, k * GROUP + i * ROWS:k * GROUP + (i + 1) * ROWS],
                                            rows[slot % 2][:, i, k * P:(k + 1) * P], m.ident[0:ROWS, 0:ROWS])
                last.then_inc(TE["turned"], 1)

            def up(n, slot, turn):
                yield 0
                if slot % GROUPS == 0:
                    pe.wait_ge(*W1D("lower1", expert(slot, turn)))
                pe.wait_ge(*TD("lower", n))
                for f in range(FT):
                    if f % 2 == 0 and begun(n, 1):
                        pe.wait_ge(*EA(f"gelu{f + 1}", n - 1))
                    for k in range(KH):
                        for x, w in PARTS:
                            last = pe.matmul(m.bank[1 + f // 2][:, (f % 2) * GROUP:(f % 2 + 1) * GROUP],
                                             w1[w][:, k, f * P:(f + 1) * P],
                                             xg[slot % 2][x][:, k * GROUP:(k + 1) * GROUP],
                                             start=(k == 0 and (x, w) == PARTS[0]),
                                             stop=(k == KH - 1 and (x, w) == PARTS[-1]))
                    if f % 2:
                        last.then_inc(EE[f"up{f // 2}"], 1)

            def down(n, slot, turn):
                yield 2
                if slot % GROUPS == 0:
                    pe.wait_ge(*W2D("lower1", expert(slot, turn)))
                if begun(n, 2):
                    pe.wait_ge(*ED("res", n - 2))
                pe.wait_ge(*HD("lower3", n))
                for i in range(2):
                    for f in range(FT):
                        for w, x in PARTS:
                            last = pe.matmul(m.bank[5 + slot % 2][0:ROWS, i * CH:(i + 1) * CH],
                                             hs[slot % 2][x][:, f, i * ROWS:(i + 1) * ROWS], w2[w][:, f, :],
                                             start=(f == 0 and (w, x) == PARTS[0]),
                                             stop=(f == FT - 1 and (w, x) == PARTS[-1]))
                last.then_inc(FE["down"], 1)

            run_pipeline(pe, [(up, 1), (turn_in, 0), (down, 2)], N, U)


def combine(nc, m, r, out):
    ctx = ExitStack()
    with ctx:
        def sb(name, shape, dt=FP32):
            return ctx.enter_context(nc.sbuf_tensor(name, shape, dt))

        def sem(name):
            return ctx.enter_context(nc.semaphore(name))

        S = 4
        got = [sb(f"e_got{s}", [P, TOPK, CH]) for s in range(S)]
        one = [sb(f"e_one{s}", [P, CH]) for s in range(2)]
        two = [sb(f"e_two{s}", [P, CH]) for s in range(2)]
        gated = [sb(f"e_gated{s}", [P, CH]) for s in range(2)]
        final = [sb(f"e_final{s}", [P, CH]) for s in range(S)]
        got_in = [sem(f"e_got_in{s}") for s in range(S)]
        stored = [sem(f"e_stored{s}") for s in range(S)]
        CD = Steps(sem("combine_dve"), "one two gated final")
        block = ctx.enter_context(nc.Block())

        @block.gpsimd
        def _(pool):
            for t in range(TILES):
                if t >= S:
                    pool.wait_ge(*CD("two", t - S))
                for k in range(TOPK):
                    pool.indirect_dma_start(
                        out=got[t % S][:, k, :], out_offset=None, in_=r.back[:, :],
                        in_offset=bass.IndirectOffsetOnAxis(ap=m.get[:, k, t:t + 1], axis=0)).then_inc(got_in[t % S], 16)

        @block.vector
        def _(dve):
            def add(t, slot, turn):
                yield 0
                x = m.x[:, bass.ds(t, 1), :].rearrange("p a c -> p (a c)")
                dve.wait_ge(got_in[slot], turn * 32 + 32)
                dve.tensor_scalar(one[slot % 2][:, :], got[slot][:, 0, :], m.gate[:, 0, bass.ds(t, 1)], None, ALU.mult)\
                   .then_inc(CD["one"], 1)
                dve.wait_ge(*CD("one", t))
                dve.scalar_tensor_tensor(two[slot % 2][:, :], got[slot][:, 1, :], m.gate[:, 1, bass.ds(t, 1)],
                                         one[slot % 2][:, :], ALU.mult, ALU.add).then_inc(CD["two"], 1)
                dve.wait_ge(*CD("two", t))
                dve.tensor_tensor(gated[slot % 2][:, :], two[slot % 2][:, :], m.mod[1][:, 5, :], ALU.mult)\
                   .then_inc(CD["gated"], 1)
                dve.wait_ge(*CD("gated", t))
                if begun(t, S):
                    dve.wait_ge(stored[slot], turn * 32)
                dve.tensor_tensor(final[slot][:, :], gated[slot % 2][:, :], x, ALU.add).then_inc(CD["final"], 1)

            run_pipeline(dve, [(add, 0)], TILES, S)

        @block.sync
        def _(sp):
            def store(t, slot, turn):
                yield 0
                sp.wait_ge(*CD("final", t))
                for b in range(BATCH):
                    sp.dma_start(out[b, bass.ds(t * STEPS, STEPS), :], final[slot][b * STEPS:(b + 1) * STEPS, :])\
                      .then_inc(stored[slot], 16)

            run_pipeline(sp, [(store, 0)], TILES, S)
            for s in range(S):
                sp.wait_ge(stored[s], 32 * (TILES // S))


def program(nc, a, out):
    ctx = ExitStack()
    with ctx:
        m = alloc(nc, ctx)
        r = Memory()
        r.sent = nc.dram_tensor("sent", (NSLOT + TOPK * TOKENS, CH), FP32, kind="Internal").ap()
        r.back = nc.dram_tensor("results", (NSLOT, CH), FP32, kind="Internal").ap()
        with ExitStack() as for_ffn:
            alloc_ffn(nc, for_ffn, m)
            with ExitStack() as for_mix:
                alloc_mix(nc, for_mix, m)
                prologue(nc, m, a)
                time_mix(nc, m, a)
            ffn_and_training(nc, m, r, a)
        routing(nc, m, r)
        experts(nc, m, r, a)
        combine(nc, m, r, out)


def kernel(**inputs):
    import concourse.bacc as _bacc
    from concourse.bass_utils import run_bass_kernel_spmd as _run

    nc = _bacc.Bacc("TRN2", target_bir_lowering=False, num_devices=1)
    used = [n for n in inputs if n not in ("L0_attn_key", "L0_attn_value")]
    arrays, aps = {}, {}
    for name in used:
        arr = np.ascontiguousarray(inputs[name])
        arrays[f"in_{name}"] = arr
        aps[name] = nc.dram_tensor(f"in_{name}", arr.shape, mybir.dt.from_np(arr.dtype), kind="ExternalInput").ap()
    out = nc.dram_tensor("out", (BATCH, TIME, CH), FP32, kind="ExternalOutput").ap()
    program(nc, aps, out)
    return _run(nc, [arrays], core_ids=[0]).results[0]["out"]
```
